# Optimizing a Trainium2 kernel written in Bass

```python
import numpy as np
import jax
import jax.numpy as jnp

def _softmax(x, axis=-1):
    return jax.nn.softmax(x, axis=axis)

def _gelu(x):
    return jax.nn.gelu(x, approximate=True)

def _silu(x):
    return jax.nn.silu(x)

def _sigmoid(x):
    return jax.nn.sigmoid(x)

def _layernorm(x, axis=-1, eps=1e-05):
    m = jnp.mean(x, axis=axis, keepdims=True)
    v = jnp.var(x, axis=axis, keepdims=True)
    return (x - m) / jnp.sqrt(v + eps)

def _scatter_add(tgt, idx, src, axis=0):
    return tgt.at[idx].add(src)

def _segment_sum(src, seg, n):
    return jax.ops.segment_sum(src, seg, n)
kernel_name = 'mk_vit_tower_d2_tok_img1024_r4_2dbc95'

def setup_inputs(seed: int=0):
    np.random.seed(seed)
    _w = jnp.asarray

    def _rec_inputs():
        import jax
        import jax.numpy as jnp
        _rk = jax.random.key(seed)
        x = jax.random.uniform(jax.random.fold_in(_rk, 1), (32, 3, 256, 256), jnp.float32, 0.0, 1)
        return x
    x = _rec_inputs()

    def _L0_tok_setup():
        import jax, jax.numpy as jnp
        import numpy as np
        _GRAY_W = (0.2989, 0.587, 0.114)
        key = jax.random.key(seed)
        x = jax.random.uniform(key, (32, 3, 256, 256), dtype=jnp.float32)
        sx = jnp.array([[-3.0, 0.0, 3.0], [-10.0, 0.0, 10.0], [-3.0, 0.0, 3.0]], dtype=jnp.float32)
        scharr = jnp.stack([sx, sx.T])[:, None, :, :]
        return {'x': x, 'scharr': scharr}
    _L0_tok_all = _L0_tok_setup()
    _L0_tok_in = {k: v for k, v in _L0_tok_all.items() if k in ('scharr',)}
    del _L0_tok_all

    def _L0_attn_setup():
        import jax, jax.numpy as jnp
        import numpy as np
        import math
        EMBED_DIM = 256
        N_HEADS = 16
        HEAD_DIM = EMBED_DIM // N_HEADS
        NUM_FEATURES = 32
        R_NODES = 2
        EPS = 1e-06
        C_CONST = 2.0 + EPS
        CHUNK = 128

        def _compute_features(z, omega, quad_nodes, quad_weights):
            R, M = (omega.shape[0], omega.shape[-1])
            nrm = jnp.linalg.norm(z, axis=-1, keepdims=True)
            zn = z / jnp.maximum(nrm, 1e-12)
            proj = jnp.einsum('bhtd,rhdm->rbhtm', zn, omega)
            inv_sqrt_m = 1.0 / math.sqrt(M)
            poly = proj ** 2 * inv_sqrt_m
            s = quad_nodes.reshape(R, 1, 1, 1, 1)
            sqrt_2s = jnp.sqrt(2.0 * jnp.maximum(quad_nodes, 0.0)).reshape(R, 1, 1, 1, 1)
            exp_arg = jnp.clip(proj * sqrt_2s - s, -20.0, 20.0)
            prf = jnp.exp(exp_arg) * inv_sqrt_m
            sqw = jnp.sqrt(jnp.maximum(quad_weights, 0.0)).reshape(R, 1, 1, 1, 1)
            fused = poly * prf * sqw
            B, H, T = (z.shape[0], z.shape[1], z.shape[2])
            return jnp.transpose(fused, (1, 2, 3, 0, 4)).reshape(B, H, T, R * M)

        def _forward(x, w_qkv, b_qkv, w_out, b_out, omega, quad_nodes, quad_weights):
            B, T, C = x.shape
            H, D = (N_HEADS, HEAD_DIM)
            qkv = x @ w_qkv.T + b_qkv
            q, k, v = jnp.split(qkv, 3, axis=-1)

            def to_bhtd(t):
                return jnp.transpose(t.reshape(B, T, H, D), (0, 2, 1, 3)).astype(jnp.float32)
            q, k, v = (to_bhtd(q), to_bhtd(k), to_bhtd(v))
            qf = _compute_features(q, omega, quad_nodes, quad_weights)
            kf = _compute_features(k, omega, quad_nodes, quad_weights)
            F_dim = qf.shape[-1]
            nc = T // CHUNK

            def to_chunks(t):
                new_shape = (t.shape[0], t.shape[1], nc, CHUNK) + t.shape[3:]
                return jnp.moveaxis(t.reshape(new_shape), 2, 0)
            qf_c, kf_c, v_c = (to_chunks(qf), to_chunks(kf), to_chunks(v))
            kv0 = jnp.zeros((B, H, F_dim, D), dtype=jnp.float32)
            k0 = jnp.zeros((B, H, F_dim), dtype=jnp.float32)

            def step(carry, inp):
                kv_s, k_s = carry
                qc, kc, vc = inp
                kv_prod = jnp.einsum('bhtf,bhtd->bhtfd', kc, vc)
                kv_cum = jnp.cumsum(kv_prod, axis=2) + kv_s[:, :, None]
                k_cum = jnp.cumsum(kc, axis=2) + k_s[:, :, None]
                ctx = jnp.einsum('bhtf,bhtfd->bhtd', qc, kv_cum)
                den = jnp.maximum(jnp.einsum('bhtf,bhtf->bht', qc, k_cum), 1e-06)
                out_c = ctx / den[..., None]
                return ((kv_cum[:, :, -1], k_cum[:, :, -1]), out_c)
            _, out_chunks = jax.lax.scan(step, (kv0, k0), (qf_c, kf_c, v_c))
            out = jnp.moveaxis(out_chunks, 0, 2).reshape(B, H, T, D)
            out = jnp.transpose(out, (0, 2, 1, 3)).reshape(B, T, C)
            return out @ w_out.T + b_out
        key = jax.random.key(seed)
        ks = jax.random.split(key, 8)
        B, T = (2, 1024)
        x = jax.random.normal(ks[0], (B, T, EMBED_DIM), dtype=jnp.float32)
        w_qkv = jax.random.normal(ks[1], (3 * EMBED_DIM, EMBED_DIM), dtype=jnp.float32) * 0.02
        b_qkv = jnp.zeros((3 * EMBED_DIM,), dtype=jnp.float32)
        w_out = jax.random.normal(ks[2], (EMBED_DIM, EMBED_DIM), dtype=jnp.float32) * 0.02
        b_out = jnp.zeros((EMBED_DIM,), dtype=jnp.float32)
        omega = jax.random.normal(ks[3], (R_NODES, N_HEADS, HEAD_DIM, NUM_FEATURES), dtype=jnp.float32)
        nodes, weights = np.polynomial.laguerre.laggauss(R_NODES)
        quad_nodes = jnp.asarray(nodes, dtype=jnp.float32) / C_CONST
        quad_weights = jnp.asarray(weights, dtype=jnp.float32) / C_CONST
        return {'x': x, 'w_qkv': w_qkv, 'b_qkv': b_qkv, 'w_out': w_out, 'b_out': b_out, 'omega': omega, 'quad_nodes': quad_nodes, 'quad_weights': quad_weights}
    _L0_attn_all = _L0_attn_setup()
    _L0_attn_in = {k: v for k, v in _L0_attn_all.items() if k in ('w_qkv', 'b_qkv', 'w_out', 'b_out', 'omega', 'quad_nodes', 'quad_weights')}
    del _L0_attn_all

    def _L0_ffn_setup():
        import jax, jax.numpy as jnp
        import numpy as np
        FP8_MAX = 448.0
        SCALE = 1.0
        _FP8_DTYPE = getattr(jnp, 'float8_e4m3fn', jnp.float16)

        def quantize_e4m3(t, scale):
            return jnp.clip(t / scale, -FP8_MAX, FP8_MAX).astype(_FP8_DTYPE)
        key = jax.random.key(seed)
        kx, kw = jax.random.split(key)
        B, N, C, F = (8, 1024, 256, 256)
        x = jax.random.normal(kx, (B, N, C), dtype=jnp.float32)
        weight = jax.random.normal(kw, (F, C), dtype=jnp.float32) * 0.02
        bias = jnp.zeros((F,), dtype=jnp.float32)
        return {'x': x, 'weight': weight, 'bias': bias}
    _L0_ffn_all = _L0_ffn_setup()
    _L0_ffn_in = {k: v for k, v in _L0_ffn_all.items() if k in ('weight', 'bias')}
    del _L0_ffn_all

    def _L1_attn_setup():
        import jax, jax.numpy as jnp
        import numpy as np
        HIDDEN = 256
        NHEADS = 16
        HEAD_DIM = HIDDEN // NHEADS
        CONV_K = 4
        EPS = 1e-06

        def _short_conv(x, w):
            K = w.shape[-1]
            L = x.shape[1]
            xp = jnp.pad(x, ((0, 0), (K - 1, 0), (0, 0)))
            y = jnp.zeros_like(x)
            for k in range(K):
                y = y + xp[:, k:k + L, :] * w[:, k]
            return y

        def _l2norm(x):
            n = jnp.sqrt(jnp.sum(x * x, axis=-1, keepdims=True))
            return x / jnp.maximum(n, EPS)

        def _delta_rule(q, k, v, beta):
            b, h, l, dk = q.shape
            dv = v.shape[-1]
            q = q * dk ** (-0.5)
            S0 = jnp.zeros((b, h, dk, dv), dtype=v.dtype)

            def step(S, inp):
                q_t, k_t, v_t, b_t = inp
                v_new = (v_t - jnp.einsum('bhd,bhdm->bhm', k_t, S)) * b_t[..., None]
                S = S + jnp.einsum('bhd,bhm->bhdm', k_t, v_new)
                o_t = jnp.einsum('bhd,bhdm->bhm', q_t, S)
                return (S, o_t)
            ql, kl, vl = (t.transpose(2, 0, 1, 3) for t in (q, k, v))
            bl = beta.transpose(2, 0, 1)
            S, o = jax.lax.scan(step, S0, (ql, kl, vl, bl))
            return (o.transpose(1, 2, 0, 3), S)

        def _reference_tuple_inner(x, Wq, Wk, Wv, Wb, Wo, conv_q, conv_k, conv_v, o_norm_w):
            b, l, _ = x.shape
            q = x @ Wq.T
            k = x @ Wk.T
            v = x @ Wv.T
            beta = jax.nn.sigmoid(x @ Wb.T)
            q = jax.nn.silu(_short_conv(q, conv_q))
            k = jax.nn.silu(_short_conv(k, conv_k))
            v = jax.nn.silu(_short_conv(v, conv_v))

            def to_heads(t):
                return t.reshape(b, l, NHEADS, HEAD_DIM).transpose(0, 2, 1, 3)
            q, k, v = (to_heads(q), to_heads(k), to_heads(v))
            beta = beta.transpose(0, 2, 1)
            q = _l2norm(q)
            k = _l2norm(k)
            o, S = _delta_rule(q, k, v, beta)
            o = o * jax.lax.rsqrt(jnp.mean(o * o, axis=-1, keepdims=True) + EPS) * o_norm_w
            out = o.transpose(0, 2, 1, 3).reshape(b, l, HIDDEN) @ Wo.T
            return (out, S)
        key = jax.random.key(seed)
        ks = jax.random.split(key, 10)
        b, l = (4, 256)
        init = 0.02
        return {'x': jax.random.normal(ks[0], (b, l, HIDDEN), dtype=jnp.float32), 'Wq': jax.random.normal(ks[1], (HIDDEN, HIDDEN), dtype=jnp.float32) * init, 'Wk': jax.random.normal(ks[2], (HIDDEN, HIDDEN), dtype=jnp.float32) * init, 'Wv': jax.random.normal(ks[3], (HIDDEN, HIDDEN), dtype=jnp.float32) * init, 'Wb': jax.random.normal(ks[4], (NHEADS, HIDDEN), dtype=jnp.float32) * init, 'Wo': jax.random.normal(ks[5], (HIDDEN, HIDDEN), dtype=jnp.float32) * init, 'conv_q': jax.random.normal(ks[6], (HIDDEN, CONV_K), dtype=jnp.float32) * 0.3, 'conv_k': jax.random.normal(ks[7], (HIDDEN, CONV_K), dtype=jnp.float32) * 0.3, 'conv_v': jax.random.normal(ks[8], (HIDDEN, CONV_K), dtype=jnp.float32) * 0.3, 'o_norm_w': jnp.ones((HEAD_DIM,), dtype=jnp.float32)}
    _L1_attn_all = _L1_attn_setup()
    _L1_attn_in = {k: v for k, v in _L1_attn_all.items() if k in ('Wq', 'Wk', 'Wv', 'Wb', 'Wo', 'conv_q', 'conv_k', 'conv_v', 'o_norm_w')}
    del _L1_attn_all

    def _L1_ffn_setup():
        import jax, jax.numpy as jnp
        import numpy as np
        D, H, E, K = (256, 256, 8, 2)

        def _moe(x, router_w, w_in, b_in, w_out, b_out):
            B, S, Dm = x.shape
            T = B * S
            x2 = x.reshape(T, Dm)
            logits = x2 @ router_w
            probs = jax.nn.softmax(logits, axis=-1)
            top_p, top_e = jax.lax.top_k(probs, K)
            flat_e = top_e.reshape(-1)
            flat_p = top_p.reshape(-1)
            tok = jnp.repeat(jnp.arange(T), K)
            order = jnp.argsort(flat_e)
            se, sp, st = (flat_e[order], flat_p[order], tok[order])
            xd = x2[st]
            N = xd.shape[0]
            h = jnp.zeros((N, H), x.dtype)
            for e in range(E):
                m = (se == e)[:, None]
                h = h + jnp.where(m, jax.nn.gelu(xd @ w_in[e] + b_in[e]), 0.0)
            y = jnp.zeros((N, Dm), x.dtype)
            for e in range(E):
                m = (se == e)[:, None]
                y = y + jnp.where(m, h @ w_out[e] + b_out[e], 0.0)
            y = y * sp[:, None]
            out = jnp.zeros((T, Dm), x.dtype).at[st].add(y)
            return out.reshape(B, S, Dm)
        key = jax.random.key(seed)
        ks = jax.random.split(key, 5)
        s = lambda k, shape, scale: jax.random.normal(k, shape, dtype=jnp.float32) * scale
        return {'input_batch': s(ks[0], (2, 128, D), 1.0), 'router_w': s(ks[1], (D, E), D ** (-0.5)), 'w_in': s(ks[2], (E, D, H), D ** (-0.5)), 'b_in': jnp.zeros((E, H), jnp.float32), 'w_out': s(ks[3], (E, H, D), H ** (-0.5)), 'b_out': jnp.zeros((E, D), jnp.float32)}
    _L1_ffn_all = _L1_ffn_setup()
    _L1_ffn_in = {k: v for k, v in _L1_ffn_all.items() if k in ('router_w', 'w_in', 'b_in', 'w_out', 'b_out')}
    del _L1_ffn_all
    return {'x': x, 'L0_tok_scharr': _L0_tok_in['scharr'], 'L0_attn_w_qkv': _L0_attn_in['w_qkv'], 'L0_attn_b_qkv': _L0_attn_in['b_qkv'], 'L0_attn_w_out': _L0_attn_in['w_out'], 'L0_attn_b_out': _L0_attn_in['b_out'], 'L0_attn_omega': _L0_attn_in['omega'], 'L0_attn_quad_nodes': _L0_attn_in['quad_nodes'], 'L0_attn_quad_weights': _L0_attn_in['quad_weights'], 'L0_ffn_weight': _L0_ffn_in['weight'], 'L0_ffn_bias': _L0_ffn_in['bias'], 'L1_attn_Wq': _L1_attn_in['Wq'], 'L1_attn_Wk': _L1_attn_in['Wk'], 'L1_attn_Wv': _L1_attn_in['Wv'], 'L1_attn_Wb': _L1_attn_in['Wb'], 'L1_attn_Wo': _L1_attn_in['Wo'], 'L1_attn_conv_q': _L1_attn_in['conv_q'], 'L1_attn_conv_k': _L1_attn_in['conv_k'], 'L1_attn_conv_v': _L1_attn_in['conv_v'], 'L1_attn_o_norm_w': _L1_attn_in['o_norm_w'], 'L1_ffn_router_w': _L1_ffn_in['router_w'], 'L1_ffn_w_in': _L1_ffn_in['w_in'], 'L1_ffn_b_in': _L1_ffn_in['b_in'], 'L1_ffn_w_out': _L1_ffn_in['w_out'], 'L1_ffn_b_out': _L1_ffn_in['b_out']}

def reference(x, L0_tok_scharr, L0_attn_w_qkv, L0_attn_b_qkv, L0_attn_w_out, L0_attn_b_out, L0_attn_omega, L0_attn_quad_nodes, L0_attn_quad_weights, L0_ffn_weight, L0_ffn_bias, L1_attn_Wq, L1_attn_Wk, L1_attn_Wv, L1_attn_Wb, L1_attn_Wo, L1_attn_conv_q, L1_attn_conv_k, L1_attn_conv_v, L1_attn_o_norm_w, L1_ffn_router_w, L1_ffn_w_in, L1_ffn_b_in, L1_ffn_w_out, L1_ffn_b_out):
    import jax
    import jax.numpy as jnp

    def _L0_tok_ref(x, scharr):
        import jax, jax.numpy as jnp
        import numpy as np
        _GRAY_W = (0.2989, 0.587, 0.114)
        w = jnp.asarray(_GRAY_W, dtype=x.dtype)
        gray = jnp.einsum('bchw,c->bhw', x, w)[:, None]
        edges = jax.lax.conv_general_dilated(gray, scharr, window_strides=(1, 1), padding='SAME', dimension_numbers=('NCHW', 'OIHW', 'NCHW'))
        abs_edges = jnp.sqrt(jnp.square(edges))
        edge = abs_edges.sum(axis=1) / 2
        return edge

    def _L0_attn_ref(x, w_qkv, b_qkv, w_out, b_out, omega, quad_nodes, quad_weights):
        import jax, jax.numpy as jnp
        import numpy as np
        import math
        EMBED_DIM = 256
        N_HEADS = 16
        HEAD_DIM = EMBED_DIM // N_HEADS
        NUM_FEATURES = 32
        R_NODES = 2
        EPS = 1e-06
        C_CONST = 2.0 + EPS
        CHUNK = 128

        def _compute_features(z, omega, quad_nodes, quad_weights):
            R, M = (omega.shape[0], omega.shape[-1])
            nrm = jnp.linalg.norm(z, axis=-1, keepdims=True)
            zn = z / jnp.maximum(nrm, 1e-12)
            proj = jnp.einsum('bhtd,rhdm->rbhtm', zn, omega)
            inv_sqrt_m = 1.0 / math.sqrt(M)
            poly = proj ** 2 * inv_sqrt_m
            s = quad_nodes.reshape(R, 1, 1, 1, 1)
            sqrt_2s = jnp.sqrt(2.0 * jnp.maximum(quad_nodes, 0.0)).reshape(R, 1, 1, 1, 1)
            exp_arg = jnp.clip(proj * sqrt_2s - s, -20.0, 20.0)
            prf = jnp.exp(exp_arg) * inv_sqrt_m
            sqw = jnp.sqrt(jnp.maximum(quad_weights, 0.0)).reshape(R, 1, 1, 1, 1)
            fused = poly * prf * sqw
            B, H, T = (z.shape[0], z.shape[1], z.shape[2])
            return jnp.transpose(fused, (1, 2, 3, 0, 4)).reshape(B, H, T, R * M)

        def _forward(x, w_qkv, b_qkv, w_out, b_out, omega, quad_nodes, quad_weights):
            B, T, C = x.shape
            H, D = (N_HEADS, HEAD_DIM)
            qkv = x @ w_qkv.T + b_qkv
            q, k, v = jnp.split(qkv, 3, axis=-1)

            def to_bhtd(t):
                return jnp.transpose(t.reshape(B, T, H, D), (0, 2, 1, 3)).astype(jnp.float32)
            q, k, v = (to_bhtd(q), to_bhtd(k), to_bhtd(v))
            qf = _compute_features(q, omega, quad_nodes, quad_weights)
            kf = _compute_features(k, omega, quad_nodes, quad_weights)
            F_dim = qf.shape[-1]
            nc = T // CHUNK

            def to_chunks(t):
                new_shape = (t.shape[0], t.shape[1], nc, CHUNK) + t.shape[3:]
                return jnp.moveaxis(t.reshape(new_shape), 2, 0)
            qf_c, kf_c, v_c = (to_chunks(qf), to_chunks(kf), to_chunks(v))
            kv0 = jnp.zeros((B, H, F_dim, D), dtype=jnp.float32)
            k0 = jnp.zeros((B, H, F_dim), dtype=jnp.float32)

            def step(carry, inp):
                kv_s, k_s = carry
                qc, kc, vc = inp
                kv_prod = jnp.einsum('bhtf,bhtd->bhtfd', kc, vc)
                kv_cum = jnp.cumsum(kv_prod, axis=2) + kv_s[:, :, None]
                k_cum = jnp.cumsum(kc, axis=2) + k_s[:, :, None]
                ctx = jnp.einsum('bhtf,bhtfd->bhtd', qc, kv_cum)
                den = jnp.maximum(jnp.einsum('bhtf,bhtf->bht', qc, k_cum), 1e-06)
                out_c = ctx / den[..., None]
                return ((kv_cum[:, :, -1], k_cum[:, :, -1]), out_c)
            _, out_chunks = jax.lax.scan(step, (kv0, k0), (qf_c, kf_c, v_c))
            out = jnp.moveaxis(out_chunks, 0, 2).reshape(B, H, T, D)
            out = jnp.transpose(out, (0, 2, 1, 3)).reshape(B, T, C)
            return out @ w_out.T + b_out
        return _forward(x, w_qkv, b_qkv, w_out, b_out, omega, quad_nodes, quad_weights)

    def _L0_ffn_ref(x, weight, bias):
        import jax, jax.numpy as jnp
        import numpy as np
        FP8_MAX = 448.0
        SCALE = 1.0
        _FP8_DTYPE = getattr(jnp, 'float8_e4m3fn', jnp.float16)

        def quantize_e4m3(t, scale):
            return jnp.clip(t / scale, -FP8_MAX, FP8_MAX).astype(_FP8_DTYPE)
        B, N, C = x.shape
        x2d = x.reshape(B * N, C)
        x_mat = quantize_e4m3(x2d, SCALE).astype(jnp.float16)
        w_mat = quantize_e4m3(weight, SCALE).astype(jnp.float16)
        out2d = (x_mat @ w_mat.T).astype(jnp.float32) * (SCALE * SCALE)
        out2d = out2d + bias
        return out2d.reshape(B, N, -1)

    def _L1_attn_ref(x, Wq, Wk, Wv, Wb, Wo, conv_q, conv_k, conv_v, o_norm_w):
        import jax, jax.numpy as jnp
        import numpy as np
        HIDDEN = 256
        NHEADS = 16
        HEAD_DIM = HIDDEN // NHEADS
        CONV_K = 4
        EPS = 1e-06

        def _short_conv(x, w):
            K = w.shape[-1]
            L = x.shape[1]
            xp = jnp.pad(x, ((0, 0), (K - 1, 0), (0, 0)))
            y = jnp.zeros_like(x)
            for k in range(K):
                y = y + xp[:, k:k + L, :] * w[:, k]
            return y

        def _l2norm(x):
            n = jnp.sqrt(jnp.sum(x * x, axis=-1, keepdims=True))
            return x / jnp.maximum(n, EPS)

        def _delta_rule(q, k, v, beta):
            b, h, l, dk = q.shape
            dv = v.shape[-1]
            q = q * dk ** (-0.5)
            S0 = jnp.zeros((b, h, dk, dv), dtype=v.dtype)

            def step(S, inp):
                q_t, k_t, v_t, b_t = inp
                v_new = (v_t - jnp.einsum('bhd,bhdm->bhm', k_t, S)) * b_t[..., None]
                S = S + jnp.einsum('bhd,bhm->bhdm', k_t, v_new)
                o_t = jnp.einsum('bhd,bhdm->bhm', q_t, S)
                return (S, o_t)
            ql, kl, vl = (t.transpose(2, 0, 1, 3) for t in (q, k, v))
            bl = beta.transpose(2, 0, 1)
            S, o = jax.lax.scan(step, S0, (ql, kl, vl, bl))
            return (o.transpose(1, 2, 0, 3), S)

        def _reference_tuple_inner(x, Wq, Wk, Wv, Wb, Wo, conv_q, conv_k, conv_v, o_norm_w):
            b, l, _ = x.shape
            q = x @ Wq.T
            k = x @ Wk.T
            v = x @ Wv.T
            beta = jax.nn.sigmoid(x @ Wb.T)
            q = jax.nn.silu(_short_conv(q, conv_q))
            k = jax.nn.silu(_short_conv(k, conv_k))
            v = jax.nn.silu(_short_conv(v, conv_v))

            def to_heads(t):
                return t.reshape(b, l, NHEADS, HEAD_DIM).transpose(0, 2, 1, 3)
            q, k, v = (to_heads(q), to_heads(k), to_heads(v))
            beta = beta.transpose(0, 2, 1)
            q = _l2norm(q)
            k = _l2norm(k)
            o, S = _delta_rule(q, k, v, beta)
            o = o * jax.lax.rsqrt(jnp.mean(o * o, axis=-1, keepdims=True) + EPS) * o_norm_w
            out = o.transpose(0, 2, 1, 3).reshape(b, l, HIDDEN) @ Wo.T
            return (out, S)
        return _reference_tuple_inner(x, Wq, Wk, Wv, Wb, Wo, conv_q, conv_k, conv_v, o_norm_w)[0]

    def _L1_ffn_ref(input_batch, router_w, w_in, b_in, w_out, b_out):
        import jax, jax.numpy as jnp
        import numpy as np
        D, H, E, K = (256, 256, 8, 2)

        def _moe(x, router_w, w_in, b_in, w_out, b_out):
            B, S, Dm = x.shape
            T = B * S
            x2 = x.reshape(T, Dm)
            logits = x2 @ router_w
            probs = jax.nn.softmax(logits, axis=-1)
            top_p, top_e = jax.lax.top_k(probs, K)
            flat_e = top_e.reshape(-1)
            flat_p = top_p.reshape(-1)
            tok = jnp.repeat(jnp.arange(T), K)
            order = jnp.argsort(flat_e)
            se, sp, st = (flat_e[order], flat_p[order], tok[order])
            xd = x2[st]
            N = xd.shape[0]
            h = jnp.zeros((N, H), x.dtype)
            for e in range(E):
                m = (se == e)[:, None]
                h = h + jnp.where(m, jax.nn.gelu(xd @ w_in[e] + b_in[e]), 0.0)
            y = jnp.zeros((N, Dm), x.dtype)
            for e in range(E):
                m = (se == e)[:, None]
                y = y + jnp.where(m, h @ w_out[e] + b_out[e], 0.0)
            y = y * sp[:, None]
            out = jnp.zeros((T, Dm), x.dtype).at[st].add(y)
            return out.reshape(B, S, Dm)
        return _moe(input_batch, router_w, w_in, b_in, w_out, b_out)
    h = _L0_tok_ref(x, L0_tok_scharr)
    h = h + _L0_attn_ref(_layernorm(h, axis=-1), L0_attn_w_qkv, L0_attn_b_qkv, L0_attn_w_out, L0_attn_b_out, L0_attn_omega, L0_attn_quad_nodes, L0_attn_quad_weights)
    h = h + _L0_ffn_ref(_layernorm(h, axis=-1), L0_ffn_weight, L0_ffn_bias)
    h = h + _L1_attn_ref(_layernorm(h, axis=-1), L1_attn_Wq, L1_attn_Wk, L1_attn_Wv, L1_attn_Wb, L1_attn_Wo, L1_attn_conv_q, L1_attn_conv_k, L1_attn_conv_v, L1_attn_o_norm_w)
    h = h + _L1_ffn_ref(_layernorm(h, axis=-1), L1_ffn_router_w, L1_ffn_w_in, L1_ffn_b_in, L1_ffn_w_out, L1_ffn_b_out)
    return h

_drawn_inputs = setup_inputs


def setup_inputs(seed=0):
    import zlib

    import numpy as np

    out = dict(_drawn_inputs(seed))
    spreads = {'L0_attn_b_qkv': (0.0, 0.384),
     'L0_attn_b_out': (0.0, 0.1),
     'L0_ffn_bias': (0.0, 0.1),
     'L1_attn_o_norm_w': (1.0, 0.2),
     'L1_ffn_b_in': (0.0, 0.761),
     'L1_ffn_b_out': (0.0, 0.508)}
    factors = {'L0_attn_w_qkv': 2.881,
     'L0_attn_omega': 4.323,
     'L0_attn_quad_nodes': 4.537,
     'L0_attn_quad_weights': 6.49}
    for name, (base, spread) in spreads.items():
        noise = np.random.default_rng([zlib.crc32(name.encode()), seed]).standard_normal(out[name].shape)
        drawn = base * np.exp(spread * noise) if base else spread * noise
        out[name] = jnp.asarray(drawn.astype(out[name].dtype))
    for name, factor in factors.items():
        out[name] = (out[name] * factor).astype(out[name].dtype)
    return out
```

```python
import concourse.bass as bass
from concourse import mybir
from contextlib import ExitStack
import numpy as np

P = 128
T = 256
C = 256
NT = T // P
CT = C // P
H = 16
D = C // H
NODES, M = 2, 32
F = NODES * M
E = 8
TR = 37
XT = -(-T // TR)
XR = TR + 2
KX = 3 * XR
GRAY = (0.2989, 0.587, 0.114)
LANES = P // H
TB = 64
IDLE = 33
LN_EPS = 1e-5
RMS_EPS = 1e-6


def at(b, k, per=1, unit=1, credit=0):
    return b * (per * unit) + (k * unit + credit)


CREDIT = dict(credit=1)


def apart(eng, idle, sem, value, turn=[0]):
    eng.wait_ge(sem, value)
    turn[0] = turn[0] % (IDLE - 1) + 1
    if eng.engine == mybir.EngineType.Pool:
        eng.tensor_tensor(idle[:, turn[0]:turn[0] + 1], idle[:, 0:1], idle[:, 0:1], mybir.AluOpType.add)
    else:
        eng.memset(idle[:, turn[0]:turn[0] + 1], 0.0)


def image(ap, b):
    return ap[bass.ds(b, 1), :, :].rearrange("o (c p) t -> p (o c) t", p=P)


def tower(nc, x, scharr, taps, ident, causal, first, parity, w_qkv, b_qkv, w_out, b_out, omega, nodes, weights,
          ffn_w, ffn_b, w1_qkv, w1_b, w1_o, conv_w, norm_w, router, w_in, b_in, w_dn, b_dn, out):
    f32, bf16, f16, f8 = mybir.dt.float32, mybir.dt.bfloat16, mybir.dt.float16, mybir.dt.float8e4
    NB = x.shape[0]
    scratch = {n: nc.dram_tensor(f"scr_{n}", s, f32, kind="Internal").ap() for n, s in
               {"h": (NB, T, C), "q": (NB, C, T), "k": (NB, C, T), "v": (NB, C, T), "o": (NB, C, T),
                "beta": (NB, H, T)}.items()}
    front(nc, NB, x, scharr, taps, ident, causal, parity, w_qkv, b_qkv, w_out, b_out, omega, nodes, weights,
          ffn_w, ffn_b, w1_qkv, w1_b, conv_w, scratch)
    delta_rule(nc, NB, scratch)
    back(nc, NB, ident, first, w1_o, norm_w, router, w_in, b_in, w_dn, b_dn, scratch, out)


def front(nc, NB, x, scharr, taps, ident_d, causal_d, parity_d, w_qkv, b_qkv, w_out, b_out, omega, nodes, weights,
          ffn_w, ffn_b, w1_qkv, w1_b, conv_w, scratch):
    f32, bf16, f16, f8 = mybir.dt.float32, mybir.dt.bfloat16, mybir.dt.float16, mybir.dt.float8e4
    ALU, ACT, AX = mybir.AluOpType, mybir.ActivationFunctionType, mybir.AxisListType
    LO, HI = float(np.exp(-20.0)), float(np.exp(20.0))
    NF = 8
    with ExitStack() as ctx:
        sb = lambda n, s, t=f32: ctx.enter_context(nc.sbuf_tensor(n, s, t))
        ps = lambda n, s, t=f32: ctx.enter_context(nc.psum_tensor(n, s, t))
        sem = lambda n: ctx.enter_context(nc.semaphore(n))

        idle_pool, idle_dve = sb("idle_pool", [1, IDLE]), sb("idle_dve", [1, IDLE])
        ident = sb("ident", [P, P])
        identb = sb("identb", [P, P], bf16)
        causal = sb("causal", [P, T + P])
        parity = sb("parity", [P, 2])
        sch = sb("sch", [P, 2, 3, 3])
        tap = sb("tap", [KX, 3, TR])
        band = sb("band", [KX, 3, 2, TR])
        wqkv = sb("wqkv", [P, CT, 3 * C])
        bqkv = sb("bqkv", [P, 3 * C])
        wout = sb("wout", [P, CT, C])
        bout = sb("bout", [P, C])
        om = sb("om", [P, CT, F])
        omblk = sb("omblk", [P, CT, 2, F])
        fw = sb("fw", [P, CT, C])
        fw8 = sb("fw8", [P, CT, C], f8)
        fwa = sb("fwa", [P, CT, C])
        fwb = sb("fwb", [P, CT, C])
        fwm = sb("fwm", [P, CT, C])
        fwq = sb("fwq", [P, CT, C], bf16)
        fb = sb("fb", [P, C])
        w1 = sb("w1", [P, CT, 3 * C])
        w1b = sb("w1b", [P, CT, H])
        cw = sb("cw", [P, 6, 4])
        cwh = sb("cwh", [P, 6, 4])
        node = sb("node", [P, 1])
        nneg = sb("nneg", [P, 1])
        n2p = sb("n2p", [P, 1])
        root2s = sb("root2s", [P, 1])
        wgt = sb("wgt", [P, 1])
        wpos = sb("wpos", [P, 1])
        wroot = sb("wroot", [P, 1])
        sqscale = sb("sqscale", [P, 1])
        half = sb("half", [P, 1])
        quarter = sb("quarter", [P, 1])
        minus_half = sb("minus_half", [P, NT * 2 * H])

        xin = sb("xin", [P, XT, C + 2])
        edges = sb("edges", [P, CT, 2, T])
        edge = sb("edge", [P, CT, T])
        h0 = sb("h0", [P, NT, C])
        h0b = sb("h0b", [P, NT, C])
        stats = sb("stats", [P, NT, 6])
        mv = sb("mv", [P, NT, 2])
        vare = sb("vare", [P, NT])
        rstd = sb("rstd", [P, NT])
        xn = sb("xn", [P, NT, C])
        xT = sb("xT", [P, CT, T])
        qk = sb("qk", [P, NT, 2 * C])
        qksq = sb("qksq", [P, NT, 2 * C])
        vv = sb("vv", [P, NT, H, D + 1])
        qkss = sb("qkss", [P, NT * 2 * H])
        qkss2 = sb("qkss2", [P, NT * 2 * H])
        qkr = sb("qkr", [P, NT * 2 * H])
        qkn = sb("qkn", [P, NT, 2 * C])
        qkT = sb("qkT", [P, 4, T])
        fsq = sb("fsq", [P, 2, 2, T])
        fexp = sb("fexp", [P, 2, 2, T])
        feats = sb("feats", [P, 2, 8, T])
        att = sb("att", [P, 2, T + P])
        den = sb("den", [P, 2, NT, 8])
        rden = sb("rden", [P, 2, NT, 8])
        on = sb("on", [P, NT, H, D])
        onT = sb("onT", [P, CT, T])
        h1 = sb("h1", [P, NT, C])
        h1b = sb("h1b", [P, NT, C])
        x8 = sb("x8", [P, NT, C], f8)
        x8b = sb("x8b", [P, NT, C], bf16)
        x8T = sb("x8T", [P, CT, T], bf16)
        y16 = sb("y16", [P, NT, C], f16)
        h2 = sb("h2", [P, NT, C])
        raw = sb("raw", [P, 6, T + 3])
        yc = sb("yc", [P, 6, T])
        th = sb("th", [P, 6, T])
        act = sb("act", [P, 6, T])
        thb = sb("thb", [H, T])
        beta = sb("beta", [H, T])

        pf = ps("pf", [P, 2, 512])
        pe_ = [ps(f"pfeat{i}", [P, 2, T]) for i in range(2)]
        psc = [ps(f"pscore{i}", [P, 512]) for i in range(2)]
        ppv = ps("ppv", [P, NT, 8, D + 1])
        ptr = ps("ptr", [P, 512])
        ppv2 = ptr[:, 0:NT * 8 * (D + 1)].rearrange("p (a h d) -> p a h d", a=NT, h=8)
        pv_of = [ppv[:, :, :, :], ppv2]

        s_w = sem("weights_loaded")
        s_set = sem("setup_step")
        s_band = sem("band_ready")
        s_setp = sem("pool_setup_step")
        s_x = sem("x_loaded")
        s_conv = sem("conv_done")
        s_edges = sem("edges_abs")
        s_edge = sem("edge_summed")
        s_hT = sem("h0_in_psum")
        s_h0 = sem("h0_ready")
        s_stat = sem("ln_stats")
        s_pool = sem("pool_step")
        s_rstd = sem("ln_rstd")
        s_ln = sem("ln_out")
        s_dve = sem("vector_step")
        s_xTp = sem("xT_in_psum")
        s_xT = sem("xT_ready")
        s_qkp = sem("qk_in_psum")
        s_vp = sem("v_in_psum")
        s_qk = sem("qk_ready")
        s_v = sem("v_ready")
        s_qksq = sem("qk_squared")
        s_qkss = sem("qk_sums")
        s_qkr = sem("qk_rnorm")
        s_qkn = sem("qk_normed")
        s_qkTp = sem("qkT_in_psum")
        s_qkT = sem("qkT_ready")
        s_fp = sem("proj_in_psum")
        s_fe = sem("feature_parts")
        s_f = sem("features_ready")
        s_sc = sem("scores_in_psum")
        s_att = sem("att_masked")
        s_pv = sem("pv_done")
        s_on = sem("out_normed")
        s_onTp = sem("onT_in_psum")
        s_onT = sem("onT_ready")
        s_op = sem("proj_out_in_psum")
        s_h0b = sem("h0_plus_bias")
        s_h1 = sem("h1_ready")
        s_h1b = sem("h1_plus_bias")
        s_x8b = sem("x8_as_bf16")
        s_x8Tp = sem("x8T_in_psum")
        s_x8T = sem("x8T_ready")
        s_yp = sem("ffn_in_psum")
        s_y16 = sem("ffn_as_f16")
        s_h2 = sem("h2_ready")
        s_h2st = sem("h2_stored")
        s_l1p = sem("l1_in_psum")
        s_raw = sem("l1_raw")
        s_yc = sem("short_conv")
        s_th = sem("tanh_done")
        s_act = sem("l1_silu")
        s_bp = sem("beta_in_psum")
        s_thb = sem("beta_tanh")
        s_beta = sem("beta_ready")
        s_st = sem("l1_stored")
        s_bst = sem("beta_stored")
        block = ctx.enter_context(nc.Block())

        loads = [(ident, ident_d), (causal, causal_d), (parity, parity_d), (sch, scharr), (tap, taps),
                 (wqkv, w_qkv.rearrange("(c p) n -> p c n", p=P)), (bqkv, b_qkv),
                 (wout, w_out.rearrange("(c p) n -> p c n", p=P)), (bout, b_out),
                 (om, omega.rearrange("(c p) n -> p c n", p=P)),
                 (fw, ffn_w.rearrange("(c p) n -> p c n", p=P)), (fb, ffn_b),
                 (w1, w1_qkv.rearrange("(c p) n -> p c n", p=P)), (w1b, w1_b.rearrange("(c p) n -> p c n", p=P)),
                 (cw, conv_w.rearrange("(c p) k -> p c k", p=P)), (node, nodes), (wgt, weights)]
        NW = 16 * len(loads)
        NX = 16 * 9

        @block.sync
        def _(sp):
            for sem_ in (s_conv, s_h2st, s_thb, s_raw, s_bst, s_st):
                sp.sem_inc(sem_, 1)
            for tile, src in loads:
                sp.dma_start(tile[tuple(slice(None) for _ in tile.shape)], src).then_inc(s_w, 16)
            sp.wait_ge(s_set, 1)
            with sp.Fori(0, NB) as b:
                sp.wait_ge(s_conv, at(b, 0, **CREDIT))
                for c in range(3):
                    img = x[bass.ds(b, 1), c, :, :].rearrange("o r w -> (o r) w")
                    sp.dma_start(xin[c * XR + 1:(c + 1) * XR, 0, 1:C + 1], img[0:XR - 1, :]).then_inc(s_x, 16)
                    for j in range(1, XT - 1):
                        pass
                    mid = bass.AP(tensor=img.tensor, offset=img.offset + (TR - 1) * C,
                                  ap=[[C, XR], [TR * C, XT - 2], [1, C]])
                    sp.dma_start(xin[c * XR:(c + 1) * XR, 1:XT - 1, 1:C + 1], mid).then_inc(s_x, 16)
                    r0 = (XT - 1) * TR - 1
                    sp.dma_start(xin[c * XR:c * XR + T - r0, XT - 1, 1:C + 1], img[r0:T, :]).then_inc(s_x, 16)
                sp.wait_ge(s_h2, at(b, 1))
                sp.dma_start(image(scratch["h"], b), h2[:, :, :]).then_inc(s_h2st, 16)
                sp.wait_ge(s_beta, at(b, 1))
                sp.dma_start(scratch["beta"][bass.ds(b, 1), :, :].rearrange("o h t -> (o h) t"),
                             beta[:, :]).then_inc(s_bst, 16)
                sp.wait_ge(s_act, at(b, 1))
                for i, n in enumerate("qkv"):
                    sp.dma_start(image(scratch[n], b), act[:, 2 * i:2 * i + 2, :]).then_inc(s_st, 16)
            sp.wait_ge(s_h2st, 16 * NB + 1)
            sp.wait_ge(s_bst, 16 * NB + 1)
            sp.wait_ge(s_st, 48 * NB + 1)

        @block.gpsimd
        def _(pool):
            n = [0]

            def step(ins):
                n[0] += 1
                ins.then_inc(s_setp, 1)
                pool.wait_ge(s_setp, n[0])

            step(nc.gpsimd.memset(idle_pool[:, :], 0.0))
            step(nc.gpsimd.memset(half[:, :], 0.5))
            step(nc.gpsimd.memset(quarter[:, :], 0.25))
            step(nc.gpsimd.memset(minus_half[:, :], -0.5))
            pool.wait_ge(s_w, NW)
            step(nc.gpsimd.tensor_scalar(n2p[:, :], node[:, :], 0.0, 2.0, ALU.max, ALU.mult))
            step(nc.gpsimd.tensor_tensor(root2s[:, :], n2p[:, :], half[:, :], ALU.pow))
            step(nc.gpsimd.tensor_scalar(nneg[:, :], node[:, :], -1.0, None, ALU.mult))
            step(nc.gpsimd.tensor_scalar(wpos[:, :], wgt[:, :], 0.0, None, ALU.max))
            step(nc.gpsimd.tensor_tensor(wroot[:, :], wpos[:, :], quarter[:, :], ALU.pow))
            step(nc.gpsimd.tensor_scalar(sqscale[:, :], wroot[:, :], float(M ** -0.5), None, ALU.mult))
            with pool.Fori(0, NB) as b:
                def rsqrt_ln(k):
                    apart(pool, idle_pool, s_stat, at(b, k, 3))
                    nc.gpsimd.tensor_scalar(vare[:, :], mv[:, :, 1], LN_EPS, None, ALU.add).then_inc(s_pool, 1)
                    pool.wait_ge(s_pool, at(b, k if k == 1 else k + 1, 4))
                    nc.gpsimd.tensor_tensor(rstd[:, :], vare[:, :], minus_half[:, 0:NT], ALU.pow).then_inc(s_rstd, 1)

                pool.wait_ge(s_edges, at(b, 1))
                nc.gpsimd.tensor_tensor(edge[:, :, :], edges[:, :, 0, :], edges[:, :, 1, :], ALU.add).then_inc(s_edge, 1)
                rsqrt_ln(1)
                nc.gpsimd.tensor_tensor(h0b[:, :, :], h0[:, :, :], bout[:, :].unsqueeze(1).to_broadcast([P, NT, C]),
                                        ALU.add).then_inc(s_h0b, 1)
                apart(pool, idle_pool, s_qkss, at(b, 1))
                nc.gpsimd.tensor_scalar(qkss2[:, :], qkss[:, :], 1e-24, None, ALU.max).then_inc(s_pool, 1)
                pool.wait_ge(s_pool, at(b, 2, 4))
                nc.gpsimd.tensor_tensor(qkr[:, :], qkss2[:, :], minus_half[:, :], ALU.pow).then_inc(s_qkr, 1)
                rsqrt_ln(2)
                nc.gpsimd.tensor_tensor(h1b[:, :, :], h1[:, :, :], fb[:, :].unsqueeze(1).to_broadcast([P, NT, C]),
                                        ALU.add).then_inc(s_h1b, 1)
                apart(pool, idle_pool, s_ln, at(b, 2, 3))
                nc.gpsimd.tensor_copy(x8b[:, :, :], x8[:, :, :]).then_inc(s_x8b, 1)
                rsqrt_ln(3)

        @block.vector
        def _(dve):
            n = [0]

            def step(ins):
                n[0] += 1
                ins.then_inc(s_set, 1)
                dve.wait_ge(s_set, n[0])

            step(nc.vector.memset(xin[:, :, :], 0.0))
            step(nc.vector.memset(raw[:, :, 0:3], 0.0))
            step(nc.vector.memset(vv[:, :, :, D:D + 1], 1.0))
            dve.wait_ge(s_w, NW)
            step(nc.vector.tensor_copy(identb[:, :], ident[:, :]))
            step(nc.vector.tensor_scalar(cwh[:, :, :], cw[:, :, :], 0.5, None, ALU.mult))
            for a in range(2):
                step(nc.vector.tensor_scalar(omblk[:, :, a, :], om[:, :, :], parity[:, a:a + 1], None, ALU.mult))
            for dx in range(3):
                for f in range(2):
                    step(nc.vector.tensor_scalar(band[:, dx, f, :], tap[:, 0, :], sch[0:KX, f, 0, dx:dx + 1], None,
                                                 ALU.mult))
                    for dy in (1, 2):
                        step(nc.vector.scalar_tensor_tensor(band[:, dx, f, :], tap[:, dy, :],
                                                            sch[0:KX, f, dy, dx:dx + 1], band[:, dx, f, :],
                                                            ALU.mult, ALU.add))
            step(nc.vector.tensor_scalar(fw8[:, :, :], fw[:, :, :], 240.0, -240.0, ALU.min, ALU.max, saturate=False))
            step(nc.vector.tensor_copy(fwa[:, :, :], fw8[:, :, :]))
            step(nc.vector.tensor_scalar(fwb[:, :, :], fw[:, :, :], 448.0, -448.0, ALU.min, ALU.max))
            step(nc.vector.tensor_scalar(fw8[:, :, :], fwb[:, :, :], 0.5, None, ALU.mult, saturate=False))
            step(nc.vector.tensor_copy(fwb[:, :, :], fw8[:, :, :]))
            step(nc.vector.scalar_tensor_tensor(fwb[:, :, :], fwb[:, :, :], 2.0, fwa[:, :, :], ALU.mult, ALU.subtract))
            step(nc.vector.tensor_tensor(fwm[:, :, :], fw[:, :, :], fw[:, :, :], ALU.mult))
            step(nc.vector.tensor_scalar(fwm[:, :, :], fwm[:, :, :], 128.0 * 128.0, None, ALU.is_ge))
            step(nc.vector.tensor_tensor(fwb[:, :, :], fwb[:, :, :], fwm[:, :, :], ALU.mult))
            nc.vector.tensor_tensor(fwq[:, :, :], fwa[:, :, :], fwb[:, :, :], ALU.add).then_inc(s_band, 1)
            with dve.Fori(0, NB) as b:
                m = [0]
                PER = 3 + 8 + 2 * 2 + 4 - 1

                def link(ins, alone=False):
                    m[0] += 1
                    ins.then_inc(s_dve, 1)
                    if alone:
                        apart(dve, idle_dve, s_dve, at(b, m[0], PER))
                    else:
                        dve.wait_ge(s_dve, at(b, m[0], PER))

                def layernorm(k, h, out, **kinds):
                    for t in range(NT):
                        last = nc.vector.bn_stats(stats[:, t, :], h[:, t, :])
                    link(last, alone=True)
                    for t in range(NT):
                        last = nc.vector.bn_aggr(mv[:, t, :], stats[:, t, :])
                    last.then_inc(s_stat, 1)
                    apart(dve, idle_dve, s_rstd, at(b, k, 3))
                    for t in range(NT):
                        last = nc.vector.tensor_scalar(out[:, t, :], h[:, t, :], mv[:, t, 0:1], rstd[:, t:t + 1],
                                                       ALU.subtract, ALU.mult, **kinds)
                    last.then_inc(s_ln, 1)

                dve.wait_ge(s_hT, at(b, 1))
                nc.vector.tensor_copy(h0[:, :, :].rearrange("p a c -> p (a c)"), ptr[:, :]).then_inc(s_h0, 1)
                dve.wait_ge(s_h0, at(b, 1))
                layernorm(1, h0, xn)
                dve.wait_ge(s_qkp, at(b, 1))
                nc.vector.tensor_tensor(qk[:, :, :], pf[:, :, :], bqkv[:, 0:2 * C].unsqueeze(1).to_broadcast([P, NT, 2 * C]),
                                        ALU.add).then_inc(s_qk, 1)
                dve.wait_ge(s_vp, at(b, 1))
                for t in range(NT):
                    last = nc.vector.tensor_tensor(vv[:, t, :, 0:D], ptr[:, t * C:(t + 1) * C].rearrange("p (h d) -> p h d", h=H),
                                                   bqkv[:, 2 * C:3 * C].rearrange("p (h d) -> p h d", h=H), ALU.add)
                last.then_inc(s_v, 1)
                dve.wait_ge(s_qksq, at(b, 1))
                nc.vector.tensor_reduce(qkss[:, :], qksq[:, :, :].rearrange("p a (h d) -> p (a h) d", d=D), AX.X,
                                        ALU.add).then_inc(s_qkss, 1)
                dve.wait_ge(s_qkr, at(b, 1))
                nc.vector.tensor_tensor(qkn[:, :, :].rearrange("p a (h d) -> p (a h) d", d=D),
                                        qk[:, :, :].rearrange("p a (h d) -> p (a h) d", d=D),
                                        qkr[:, :].unsqueeze(2).to_broadcast([P, NT * 2 * H, D]),
                                        ALU.mult).then_inc(s_qkn, 1)
                for i in range(NF):
                    dve.wait_ge(s_fe, at(b, i + 1, NF))
                    link(nc.vector.tensor_scalar(fexp[:, i % 2, :, :], fexp[:, i % 2, :, :], LO, HI, ALU.max, ALU.min))
                    nc.vector.tensor_tensor(feats[:, i // 4, i % 4:i % 4 + 5:4, :], fsq[:, i % 2, :, :],
                                            fexp[:, i % 2, :, :], ALU.mult).then_inc(s_f, 1)
                for h in range(H):
                    dve.wait_ge(s_sc, at(b, h + 1, H))
                    if h >= 2:
                        dve.wait_ge(s_pv, at(b, h - 1, H))
                    nc.vector.tensor_tensor(att[:, h % 2, :], psc[h % 2][:, 0:T + P], causal[:, :],
                                            ALU.mult).then_inc(s_att, 1)
                for g in range(2):
                    dve.wait_ge(s_pv, at(b, 8 * (g + 1), H))
                    link(nc.vector.tensor_scalar(den[:, g, :, :], pv_of[g][:, :, :, D], 1e-6, None, ALU.max))
                    link(nc.vector.reciprocal(rden[:, g, :, :], den[:, g, :, :]))
                    for t in range(NT):
                        last = nc.vector.tensor_tensor(on[:, t, 8 * g:8 * g + 8, :], pv_of[g][:, t, :, 0:D],
                                                       rden[:, g, t, :].unsqueeze(2).to_broadcast([P, 8, D]), ALU.mult)
                    last.then_inc(s_on, 1)
                dve.wait_ge(s_op, at(b, 1))
                dve.wait_ge(s_h0b, at(b, 1))
                nc.vector.tensor_tensor(h1[:, :, :].rearrange("p a c -> p (a c)"), ptr[:, :],
                                        h0b[:, :, :].rearrange("p a c -> p (a c)"), ALU.add).then_inc(s_h1, 1)
                dve.wait_ge(s_h1, at(b, 1))
                layernorm(2, h1, x8, saturate=False)
                dve.wait_ge(s_y16, at(b, 1))
                dve.wait_ge(s_h1b, at(b, 1))
                dve.wait_ge(s_h2st, at(b, 0, unit=16, **CREDIT))
                nc.vector.tensor_tensor(h2[:, :, :], y16[:, :, :], h1b[:, :, :], ALU.add).then_inc(s_h2, 1)
                dve.wait_ge(s_h2, at(b, 1))
                layernorm(3, h2, xn)
                dve.wait_ge(s_raw, at(b, 3, 3, **CREDIT))
                for o in range(6):
                    last = nc.vector.tensor_scalar(yc[:, o, :], raw[:, o, 3:T + 3], cwh[:, o, 3:4], None, ALU.mult)
                link(last)
                for k in range(3):
                    for o in range(6):
                        last = nc.vector.scalar_tensor_tensor(yc[:, o, :], raw[:, o, k:k + T], cwh[:, o, k:k + 1],
                                                              yc[:, o, :], ALU.mult, ALU.add)
                    if k < 2:
                        link(last)
                last.then_inc(s_yc, 1)
                dve.wait_ge(s_thb, at(b, 1, **CREDIT))
                dve.wait_ge(s_bst, at(b, 0, unit=16, **CREDIT))
                nc.vector.tensor_scalar(beta[:, :], thb[:, :], 0.5, 0.5, ALU.mult, ALU.add).then_inc(s_beta, 1)
                dve.wait_ge(s_th, at(b, 1))
                dve.wait_ge(s_yc, at(b, 1))
                dve.wait_ge(s_st, at(b, 0, unit=48, **CREDIT))
                nc.vector.scalar_tensor_tensor(act[:, :, :], th[:, :, :], 1.0, yc[:, :, :], ALU.add,
                                               ALU.mult).then_inc(s_act, 1)
                assert m[0] == PER, m[0]

        @block.scalar
        def _(sc):
            A = nc.scalar.activation
            sc.wait_ge(s_setp, 10)
            with sc.Fori(0, NB) as b:
                sc.wait_ge(s_conv, at(b, 1, **CREDIT))
                A(edges[:, :, :, :].rearrange("p c f t -> p c (f t)"), pf[:, :, :], ACT.Abs, scale=0.5).then_inc(s_edges, 1)

                def evict_xT(k):
                    sc.wait_ge(s_xTp, at(b, k, 2))
                    A(xT[:, :, :].rearrange("p c t -> p (c t)"), ptr[:, :], ACT.Copy).then_inc(s_xT, 1)

                evict_xT(1)
                sc.wait_ge(s_qk, at(b, 1))
                A(qksq[:, :, :], qk[:, :, :], ACT.Square).then_inc(s_qksq, 1)
                sc.wait_ge(s_qkTp, at(b, 1))
                for i in range(2):
                    last = A(qkT[:, 2 * i:2 * i + 2, :], pe_[i][:, :, :], ACT.Copy)
                last.then_inc(s_qkT, 1)
                for i in range(NF):
                    sc.wait_ge(s_fp, at(b, i + 1, NF))
                    if i >= 2:
                        sc.wait_ge(s_f, at(b, i - 1, NF))
                    A(fsq[:, i % 2, :, :], pe_[i % 2][:, :, :], ACT.Square, scale=sqscale[:, 0:1])
                    A(fexp[:, i % 2, :, :], pe_[i % 2][:, :, :], ACT.Exp, bias=nneg[:, 0:1],
                      scale=root2s[:, 0:1]).then_inc(s_fe, 1)
                sc.wait_ge(s_onTp, at(b, 1))
                A(onT[:, :, :].rearrange("p c t -> p (c t)"), ptr[:, :], ACT.Copy).then_inc(s_onT, 1)
                sc.wait_ge(s_x8Tp, at(b, 1))
                A(x8T[:, :, :].rearrange("p c t -> p (c t)"), ptr[:, 0:T].bitcast(bf16), ACT.Copy).then_inc(s_x8T, 1)
                sc.wait_ge(s_yp, at(b, 1))
                A(y16[:, :, :].rearrange("p c t -> p (c t)"), ptr[:, :], ACT.Copy).then_inc(s_y16, 1)
                evict_xT(2)
                for r in range(3):
                    sc.wait_ge(s_l1p, at(b, r + 1, 3))
                    A(raw[:, 2 * r:2 * r + 2, 3:T + 3], pf[:, r % 2, :].rearrange("p (o t) -> p o t", o=2),
                      ACT.Copy).then_inc(s_raw, 1)
                sc.wait_ge(s_bp, at(b, 1))
                A(thb[:, :], ptr[0:H, 0:T], ACT.Tanh, scale=0.5).then_inc(s_thb, 1)
                sc.wait_ge(s_yc, at(b, 1))
                A(th[:, :, :], yc[:, :, :], ACT.Tanh).then_inc(s_th, 1)

        @block.tensor
        def _(pe):
            mm, tr = nc.tensor.matmul, nc.tensor.transpose
            pe.wait_ge(s_band, 1)
            with pe.Fori(0, NB) as b:
                pe.wait_ge(s_x, at(b, 1) * NX)
                pe.wait_ge(s_raw, at(b, 0, 3, **CREDIT))
                for c in range(CT):
                    for j in range(XT):
                        rows = min(TR, T - j * TR)
                        dst = pf[:, c, :].rearrange("p (f t) -> p f t", f=2)[:, :, j * TR:j * TR + rows]
                        for dx in range(3):
                            last = mm(dst, xin[0:KX, j, c * P + dx:c * P + dx + P], band[:, dx, :, 0:rows],
                                      start=(dx == 0), stop=(dx == 2))
                last.then_inc(s_conv, 1)

                def turn(src, dst, ident_=None):
                    for i in range(2):
                        for j in range(2):
                            last = tr(dst[:, i * T + j * P:i * T + (j + 1) * P], src[:, j, i * P:(i + 1) * P],
                                      ident_ if ident_ is not None else ident[:, :])
                    return last

                pe.wait_ge(s_edge, at(b, 1))
                pe.wait_ge(s_thb, at(b, 0, **CREDIT))
                turn(edge, ptr[:, :]).then_inc(s_hT, 1)
                pe.wait_ge(s_ln, at(b, 1, 3))
                turn(xn, ptr[:, :]).then_inc(s_xTp, 1)
                pe.wait_ge(s_xT, at(b, 1, 2))
                for t in range(NT):
                    for c in range(CT):
                        last = mm(pf[:, t, :], xT[:, c, t * P:(t + 1) * P], wqkv[:, c, 0:2 * C], start=(c == 0),
                                  stop=(c == CT - 1))
                last.then_inc(s_qkp, 1)
                for t in range(NT):
                    for c in range(CT):
                        last = mm(ptr[:, t * C:(t + 1) * C], xT[:, c, t * P:(t + 1) * P], wqkv[:, c, 2 * C:3 * C],
                                  start=(c == 0), stop=(c == CT - 1))
                last.then_inc(s_vp, 1)
                pe.wait_ge(s_qkn, at(b, 1))
                for j in range(4):
                    for t in range(NT):
                        last = tr(pe_[j // 2][:, j % 2, t * P:(t + 1) * P], qkn[:, t, j * P:(j + 1) * P], ident[:, :])
                last.then_inc(s_qkTp, 1)
                pe.wait_ge(s_qkT, at(b, 1))
                for i in range(NF):
                    if i >= 2:
                        pe.wait_ge(s_fe, at(b, i - 1, NF))
                    rows = slice(32 * (i % 4), 32 * (i % 4) + 32)
                    for c in range(CT):
                        last = mm(pe_[i % 2][:, c, :], omblk[rows, c, :, :], qkT[rows, 2 * (i // 4) + c, :],
                                  start=True, stop=True)
                    last.then_inc(s_fp, 1)
                pe.wait_ge(s_v, at(b, 1))
                pe.wait_ge(s_f, at(b, NF, NF))
                for h in range(H + 1):
                    if h < H:
                        if h >= 2:
                            pe.wait_ge(s_att, at(b, h - 1, H))
                        rows = slice(F * (h % 2), F * (h % 2) + F)
                        q, k = feats[rows, 0, h // 2, :], feats[rows, 1, h // 2, :]
                        mm(psc[h % 2][:, 0:T], k[:, 0:P], q, start=True, stop=True)
                        mm(psc[h % 2][:, T:T + P], k[:, P:T], q[:, P:T], start=True, stop=True).then_inc(s_sc, 1)
                    if h >= 1:
                        g = h - 1
                        pe.wait_ge(s_att, at(b, g + 1, H))
                        acc, a = pv_of[g // 8], att[:, g % 2, :]
                        mm(acc[:, 0, g % 8, :], a[:, 0:P], vv[:, 0, g, :], start=True, stop=True)
                        mm(acc[:, 1, g % 8, :], a[:, P:T], vv[:, 0, g, :], start=True, stop=False)
                        mm(acc[:, 1, g % 8, :], a[:, T:T + P], vv[:, 1, g, :], start=False, stop=True).then_inc(s_pv, 1)
                pe.wait_ge(s_on, at(b, 2, 2))
                for i in range(CT):
                    for j in range(NT):
                        last = tr(ptr[:, i * T + j * P:i * T + (j + 1) * P],
                                  on[:, j, :, :].rearrange("p h d -> p (h d)")[:, i * P:(i + 1) * P], ident[:, :])
                last.then_inc(s_onTp, 1)
                pe.wait_ge(s_onT, at(b, 1))
                for t in range(NT):
                    for c in range(CT):
                        last = mm(ptr[:, t * C:(t + 1) * C], onT[:, c, t * P:(t + 1) * P], wout[:, c, :],
                                  start=(c == 0), stop=(c == CT - 1))
                last.then_inc(s_op, 1)
                pe.wait_ge(s_x8b, at(b, 1))
                turn(x8b, ptr[:, 0:T].bitcast(bf16), identb[:, :]).then_inc(s_x8Tp, 1)
                pe.wait_ge(s_x8T, at(b, 1))
                for t in range(NT):
                    for c in range(CT):
                        last = mm(ptr[:, t * C:(t + 1) * C], x8T[:, c, t * P:(t + 1) * P], fwq[:, c, :],
                                  start=(c == 0), stop=(c == CT - 1))
                last.then_inc(s_yp, 1)
                pe.wait_ge(s_ln, at(b, 3, 3))
                turn(xn, ptr[:, :]).then_inc(s_xTp, 1)
                pe.wait_ge(s_xT, at(b, 2, 2))
                for r in range(3):
                    if r == 2:
                        pe.wait_ge(s_raw, at(b, 1, 3, **CREDIT))
                    for o in range(2):
                        for c in range(CT):
                            last = mm(pf[:, r % 2, o * T:(o + 1) * T], w1[:, c, (2 * r + o) * P:(2 * r + o + 1) * P],
                                      xT[:, c, :], start=(c == 0), stop=(c == CT - 1))
                    last.then_inc(s_l1p, 1)
                for c in range(CT):
                    last = mm(ptr[0:H, 0:T], w1b[:, c, :], xT[:, c, :], start=(c == 0), stop=(c == CT - 1))
                last.then_inc(s_bp, 1)


def delta_rule(nc, NB, scratch):
    f32 = mybir.dt.float32
    ALU, ACT, AX = mybir.AluOpType, mybir.ActivationFunctionType, mybir.AxisListType
    G, BLOCKS = NB // LANES, T // TB
    lanes = lambda n: scratch[n].rearrange("(g b) (h d) t -> g (b h) d t", b=LANES, h=H)
    with ExitStack() as ctx:
        sb = lambda n, s, t=f32: ctx.enter_context(nc.sbuf_tensor(n, s, t))
        sem = lambda n: ctx.enter_context(nc.semaphore(n))
        idle_pool = sb("d_idle", [1, IDLE])
        kr, qr, vr = (sb(f"d_{n}raw", [P, G, D, TB]) for n in "kqv")
        br = sb("d_beta", [P, G, TB])
        kn, kb, qn, vb = (sb(f"d_{n}", [P, G, D, TB]) for n in ("kn", "kb", "qn", "vb"))
        tmp = sb("d_tmp", [P, G, D, TB])
        ss = sb("d_ss", [P, G, TB])
        ss2 = sb("d_ss2", [P, G, TB])
        rn = sb("d_rn", [P, G, TB])
        dot = sb("d_dot", [P, G, TB])
        ub = sb("d_u", [P, G, D, TB])
        ob = sb("d_o", [P, G, D, TB])
        mh = sb("d_mh", [P, G, TB])
        S = sb("d_S", [P, G, D, D])
        pk = sb("d_pk", [P, G, D, D])
        pq = sb("d_pq", [P, G, D, D])
        outer = sb("d_outer", [P, G, D, D])
        kS = sb("d_kS", [P, G, D])

        s_ld = sem("d_loaded")
        s_free = sem("d_raw_used")
        s_prep = sem("d_prep_step")
        s_pprep = sem("d_pool_prep_step")
        s_aprep = sem("d_act_prep_step")
        s_S = sem("d_state_ready")
        s_pq = sem("d_qS_products")
        s_step = sem("d_vector_step")
        s_o = sem("d_block_ready")
        s_st = sem("d_block_stored")
        s_init = sem("d_init")
        block = ctx.enter_context(nc.Block())
        NLD = 4 * G * 16
        full = [P, G, D, TB]
        over_d = lambda a: a[:, :, :].unsqueeze(2).to_broadcast(full)
        inner = lambda a: a[:, :, :, :].rearrange("p g d t -> p g t d")
        NP, NPP, NA = 10, 10, 3

        @block.sync
        def _(sp):
            for sem_ in (s_free, s_st):
                sp.sem_inc(sem_, 1)
            with sp.Fori(0, BLOCKS) as n:
                sp.wait_ge(s_free, at(n, 0, **CREDIT))
                for g in range(G):
                    for tile, name in ((kr, "k"), (qr, "q"), (vr, "v")):
                        sp.dma_start(tile[:, g, :, :], lanes(name)[g, :, :, bass.ds(n * TB, TB)]).then_inc(s_ld, 16)
                    sp.dma_start(br[:, g, :], scratch["beta"].rearrange("(g b) h t -> g (b h) t", b=LANES)
                                 [g, :, bass.ds(n * TB, TB)]).then_inc(s_ld, 16)
                sp.wait_ge(s_o, at(n, 1))
                for g in range(G):
                    sp.dma_start(lanes("o")[g, :, :, bass.ds(n * TB, TB)], ob[:, g, :, :]).then_inc(s_st, 16)
            sp.wait_ge(s_st, 16 * G * BLOCKS + 1)

        @block.scalar
        def _(sc):
            with sc.Fori(0, BLOCKS) as n:
                sc.wait_ge(s_ld, at(n, 1) * NLD)
                nc.scalar.activation(tmp[:, :, :, :], kr[:, :, :, :], ACT.Square).then_inc(s_aprep, 1)
                sc.wait_ge(s_prep, at(n, 1, NP))
                nc.scalar.activation(tmp[:, :, :, :], qr[:, :, :, :], ACT.Square).then_inc(s_aprep, 1)
                sc.wait_ge(s_prep, at(n, 9, NP))
                nc.scalar.activation(tmp[:, :, :, :], ob[:, :, :, :], ACT.Square).then_inc(s_aprep, 1)

        @block.gpsimd
        def _(pool):
            nc.gpsimd.memset(mh[:, :, :], -0.5).then_inc(s_init, 1)
            nc.gpsimd.memset(idle_pool[:, :], 0.0).then_inc(s_init, 1)
            pool.wait_ge(s_init, 2)
            with pool.Fori(0, BLOCKS) as n:
                m = [0]

                def link(ins):
                    m[0] += 1
                    ins.then_inc(s_pprep, 1)
                    apart(pool, idle_pool, s_pprep, at(n, m[0], NPP))

                TS, TT = nc.gpsimd.tensor_scalar, nc.gpsimd.tensor_tensor
                apart(pool, idle_pool, s_prep, at(n, 1, NP))
                link(TS(ss2[:, :, :], ss[:, :, :], RMS_EPS * RMS_EPS, None, ALU.max))
                link(TT(rn[:, :, :], ss2[:, :, :], mh[:, :, :], ALU.pow))
                apart(pool, idle_pool, s_prep, at(n, 4, NP))
                link(TS(ss2[:, :, :], ss[:, :, :], RMS_EPS * RMS_EPS, None, ALU.max))
                link(TT(rn[:, :, :], ss2[:, :, :], mh[:, :, :], ALU.pow))
                link(TS(rn[:, :, :], rn[:, :, :], float(D) ** -0.5, None, ALU.mult))
                link(TT(vb[:, :, :, :], vr[:, :, :, :], over_d(br), ALU.mult))
                apart(pool, idle_pool, s_prep, at(n, 5, NP))
                link(TT(tmp[:, :, :, :], kn[:, :, :, :], qn[:, :, :, :], ALU.mult))
                apart(pool, idle_pool, s_prep, at(n, 7, NP))
                with pool.Fori(0, TB) as t:
                    pool.wait_ge(s_S, n * TB + t + 1)
                    TT(pq[:, :, :, :], S[:, :, :, :],
                       qn[:, :, :, bass.ds(t, 1)].rearrange("p g d o -> p g (o d)").unsqueeze(2).to_broadcast([P, G, D, D]),
                       ALU.mult).then_inc(s_pq, 1)
                pool.wait_ge(s_prep, at(n, 8, NP))
                link(TT(tmp[:, :, :, :], ub[:, :, :, :], over_d(dot), ALU.mult))
                apart(pool, idle_pool, s_prep, at(n, 10, NP))
                link(TS(ss2[:, :, :], ss[:, :, :], 1.0 / D, RMS_EPS, ALU.mult, ALU.add))
                link(TT(rn[:, :, :], ss2[:, :, :], mh[:, :, :], ALU.pow))
                assert m[0] == NPP

        @block.vector
        def _(dve):
            nc.vector.memset(S[:, :, :, :], 0.0).then_inc(s_S, 1)
            TT, RED = nc.vector.tensor_tensor, nc.vector.tensor_reduce
            with dve.Fori(0, BLOCKS) as n:
                m = [0]

                def link(ins):
                    m[0] += 1
                    ins.then_inc(s_prep, 1)
                    dve.wait_ge(s_prep, at(n, m[0], NP))

                dve.wait_ge(s_aprep, at(n, 1, NA))
                link(RED(ss[:, :, :], inner(tmp), AX.X, ALU.add))
                dve.wait_ge(s_pprep, at(n, 2, NPP))
                link(TT(kn[:, :, :, :], kr[:, :, :, :], over_d(rn), ALU.mult))
                link(TT(kb[:, :, :, :], kn[:, :, :, :], over_d(br), ALU.mult))
                dve.wait_ge(s_aprep, at(n, 2, NA))
                link(RED(ss[:, :, :], inner(tmp), AX.X, ALU.add))
                dve.wait_ge(s_pprep, at(n, 5, NPP))
                link(TT(qn[:, :, :, :], qr[:, :, :, :], over_d(rn), ALU.mult))
                dve.wait_ge(s_pprep, at(n, 7, NPP))
                link(RED(dot[:, :, :], inner(tmp), AX.X, ALU.add))
                dve.wait_ge(s_st, at(n, 0, unit=16 * G, **CREDIT))
                link(nc.vector.memset(kS[:, :, :], 0.0))
                nc.vector.memset(kS[:, :, :], 0.0).then_inc(s_free, 1)
                with dve.Fori(0, TB) as t:
                    def col(a):
                        return a[:, :, :, bass.ds(t, 1)].rearrange("p g d o -> p g (o d)")

                    def wait_step(k):
                        dve.wait_ge(s_step, (n * TB + t) * 4 + k)

                    TT(pk[:, :, :, :], S[:, :, :, :], col(kb).unsqueeze(2).to_broadcast([P, G, D, D]),
                       ALU.mult).then_inc(s_step, 1)
                    wait_step(1)
                    RED(kS[:, :, :], pk[:, :, :, :], AX.X, ALU.add).then_inc(s_step, 1)
                    wait_step(2)
                    TT(col(ub), col(vb), kS[:, :, :], ALU.subtract).then_inc(s_step, 1)
                    wait_step(3)
                    TT(outer[:, :, :, :], col(ub).unsqueeze(3).to_broadcast([P, G, D, D]),
                       col(kn).unsqueeze(2).to_broadcast([P, G, D, D]), ALU.mult).then_inc(s_step, 1)
                    dve.wait_ge(s_pq, n * TB + t + 1)
                    RED(col(ob), pq[:, :, :, :], AX.X, ALU.add)
                    wait_step(4)
                    TT(S[:, :, :, :], S[:, :, :, :], outer[:, :, :, :], ALU.add).then_inc(s_S, 1)
                    dve.wait_ge(s_S, n * TB + t + 2)
                link(nc.vector.memset(kS[:, :, :], 0.0))
                dve.wait_ge(s_pprep, at(n, 8, NPP))
                link(TT(ob[:, :, :, :], ob[:, :, :, :], tmp[:, :, :, :], ALU.add))
                dve.wait_ge(s_aprep, at(n, 3, NA))
                link(RED(ss[:, :, :], inner(tmp), AX.X, ALU.add))
                dve.wait_ge(s_pprep, at(n, 10, NPP))
                TT(ob[:, :, :, :], ob[:, :, :, :], over_d(rn), ALU.mult).then_inc(s_o, 1)
                dve.wait_ge(s_o, at(n, 1))
                assert m[0] == NP


def back(nc, NB, ident_d, first_d, w1_o, norm_w, router, w_in, b_in, w_dn, b_dn, scratch, out):
    f32 = mybir.dt.float32
    ALU, ACT, AX = mybir.AluOpType, mybir.ActivationFunctionType, mybir.AxisListType
    with ExitStack() as ctx:
        sb = lambda n, s, t=f32: ctx.enter_context(nc.sbuf_tensor(n, s, t))
        ps = lambda n, s, t=f32: ctx.enter_context(nc.psum_tensor(n, s, t))
        sem = lambda n: ctx.enter_context(nc.semaphore(n))
        idle_pool, idle_dve = sb("m_idle_pool", [1, IDLE]), sb("m_idle_dve", [1, IDLE])
        ident = sb("m_ident", [P, P])
        first = sb("m_first", [P, E, E])
        wo = sb("m_wo", [P, CT, C])
        nw = sb("m_nw", [P, 1])
        wr = sb("m_wr", [P, CT, E])
        wi = sb("m_wi", [P, E, CT, C])
        bi = sb("m_bi", [P, E, CT])
        wd = sb("m_wd", [P, E, CT, C])
        bd = sb("m_bd", [E, C])
        mh = sb("m_mh", [P, NT])
        euler = sb("m_euler", [P, NT, E])

        oT = sb("m_oT", [P, CT, T])
        oTw = sb("m_oTw", [P, CT, T])
        h2 = sb("m_h2", [P, NT, C])
        h3 = sb("m_h3", [P, NT, C])
        stats = sb("m_stats", [P, NT, 6])
        mv = sb("m_mv", [P, NT, 2])
        vare = sb("m_vare", [P, NT])
        rstd = sb("m_rstd", [P, NT])
        xn = sb("m_xn", [P, NT, C])
        xT = sb("m_xT", [P, CT, T])
        lmax = sb("m_lmax", [P, NT])
        lsub = sb("m_lsub", [P, NT, E])
        pexp = sb("m_pexp", [P, NT, E])
        psum_ = sb("m_psum", [P, NT])
        prec = sb("m_prec", [P, NT])
        prob = sb("m_prob", [P, NT, E])
        gt = sb("m_gt", [P, NT, E, E])
        eq = sb("m_eq", [P, NT, E, E])
        rank = sb("m_rank", [P, NT, E])
        gate = sb("m_gate", [P, NT, E])
        gateT = sb("m_gateT", [E, T])
        hid = sb("m_hid", [P, 2, CT, T])
        acc = sb("m_acc", [P, NT, C])

        pA = ps("m_pA", [P, 512])
        pG = ps("m_pG", [P, 512])
        pH = [ps(f"m_pH{i}", [P, CT, T]) for i in range(2)]
        pY = [ps(f"m_pY{i}", [P, NT, C]) for i in range(2)]

        s_w = sem("m_weights")
        s_in = sem("m_loaded")
        s_init = sem("m_init")
        s_ow = sem("m_o_weighted")
        s_wo = sem("m_wo_in_psum")
        s_h3 = sem("m_h3_ready")
        s_stat = sem("m_ln_stats")
        s_rstd = sem("m_ln_rstd")
        s_ln = sem("m_ln_out")
        s_pool = sem("m_pool_step")
        s_xTp = sem("m_xT_in_psum")
        s_xT = sem("m_xT_ready")
        s_lg = sem("m_logits_in_psum")
        s_lsub = sem("m_logits_less_max")
        s_pexp = sem("m_exponentials")
        s_dve = sem("m_vector_step")
        s_gate = sem("m_gates")
        s_gTp = sem("m_gateT_in_psum")
        s_gT = sem("m_gateT_ready")
        s_bp = sem("m_bias_in_psum")
        s_hp = sem("m_hidden_in_psum")
        s_hid = sem("m_hidden_ready")
        s_yp = sem("m_y_in_psum")
        s_acc = sem("m_y_added")
        s_out = sem("m_out_ready")
        s_st = sem("m_out_stored")
        block = ctx.enter_context(nc.Block())
        loads = [(ident, ident_d), (first, first_d), (wo, w1_o.rearrange("(c p) n -> p c n", p=P)), (nw, norm_w),
                 (wr, router.rearrange("(c p) n -> p c n", p=P)),
                 (wi, w_in.rearrange("e (c p) n -> p (e c) n", p=P).rearrange("p (e c) n -> p e c n", c=CT)),
                 (bi, b_in.rearrange("e (c p) -> p e c", p=P)),
                 (wd, w_dn.rearrange("e (c p) n -> p (e c) n", p=P).rearrange("p (e c) n -> p e c n", c=CT)), (bd, b_dn)]
        NW = 16 * len(loads)

        @block.sync
        def _(sp):
            for sem_ in (s_h3, s_out, s_st):
                sp.sem_inc(sem_, 1)
            for tile, src in loads:
                with nc.allow_non_contiguous_dma(reason="biases, once"):
                    sp.dma_start(tile[tuple(slice(None) for _ in tile.shape)], src).then_inc(s_w, 16)
            with sp.Fori(0, NB) as b:
                sp.wait_ge(s_h3, at(b, 0, **CREDIT))
                sp.dma_start(oT[:, :, :], image(scratch["o"], b)).then_inc(s_in, 16)
                sp.dma_start(h2[:, :, :], image(scratch["h"], b)).then_inc(s_in, 16)
                sp.wait_ge(s_out, at(b, 1, **CREDIT))
                sp.dma_start(image(out, b), acc[:, :, :]).then_inc(s_st, 16)
            sp.wait_ge(s_st, 16 * NB + 1)

        @block.gpsimd
        def _(pool):
            nc.gpsimd.memset(mh[:, :], -0.5).then_inc(s_init, 1)
            nc.gpsimd.memset(euler[:, :, :], float(np.e)).then_inc(s_init, 1)
            nc.gpsimd.memset(idle_pool[:, :], 0.0).then_inc(s_init, 1)
            pool.wait_ge(s_init, 3)
            with pool.Fori(0, NB) as b:
                apart(pool, idle_pool, s_stat, at(b, 1))
                nc.gpsimd.tensor_scalar(vare[:, :], mv[:, :, 1], LN_EPS, None, ALU.add).then_inc(s_pool, 1)
                pool.wait_ge(s_pool, at(b, 1))
                nc.gpsimd.tensor_tensor(rstd[:, :], vare[:, :], mh[:, :], ALU.pow).then_inc(s_rstd, 1)
                pool.wait_ge(s_lsub, at(b, 1))
                nc.gpsimd.tensor_tensor(pexp[:, :, :], euler[:, :, :], lsub[:, :, :], ALU.pow).then_inc(s_pexp, 1)

        @block.vector
        def _(dve):
            TT, RED = nc.vector.tensor_tensor, nc.vector.tensor_reduce
            dve.wait_ge(s_w, NW)
            with dve.Fori(0, NB) as b:
                m = [0]
                PER = 7

                def link(ins, alone=False):
                    m[0] += 1
                    ins.then_inc(s_dve, 1)
                    if alone:
                        apart(dve, idle_dve, s_dve, at(b, m[0], PER))
                    else:
                        dve.wait_ge(s_dve, at(b, m[0], PER))

                dve.wait_ge(s_wo, at(b, 1))
                TT(h3[:, :, :].rearrange("p a c -> p (a c)"), pA[:, :], h2[:, :, :].rearrange("p a c -> p (a c)"),
                   ALU.add).then_inc(s_h3, 1)
                dve.wait_ge(s_h3, at(b, 1, **CREDIT))
                for t in range(NT):
                    last = nc.vector.bn_stats(stats[:, t, :], h3[:, t, :])
                link(last, alone=True)
                for t in range(NT):
                    last = nc.vector.bn_aggr(mv[:, t, :], stats[:, t, :])
                last.then_inc(s_stat, 1)
                dve.wait_ge(s_rstd, at(b, 1))
                for t in range(NT):
                    last = nc.vector.tensor_scalar(xn[:, t, :], h3[:, t, :], mv[:, t, 0:1], rstd[:, t:t + 1],
                                                   ALU.subtract, ALU.mult)
                last.then_inc(s_ln, 1)
                dve.wait_ge(s_lg, at(b, 1))
                lg = pG[:, 0:NT * E].rearrange("p (a e) -> p a e", a=NT)
                wide = [P, NT, E]
                link(RED(lmax[:, :], lg, AX.X, ALU.max))
                TT(lsub[:, :, :], lg, lmax[:, :].unsqueeze(2).to_broadcast(wide), ALU.subtract).then_inc(s_lsub, 1)
                dve.wait_ge(s_pexp, at(b, 1))
                link(RED(psum_[:, :], pexp[:, :, :], AX.X, ALU.add))
                link(nc.vector.reciprocal(prec[:, :], psum_[:, :]))
                link(TT(prob[:, :, :], pexp[:, :, :], prec[:, :].unsqueeze(2).to_broadcast(wide), ALU.mult))
                for t in range(NT):
                    mine = prob[:, t, :].unsqueeze(2).to_broadcast([P, E, E])
                    theirs = prob[:, t, :].unsqueeze(1).to_broadcast([P, E, E])
                    TT(gt[:, t, :, :], theirs, mine, ALU.is_gt)
                    last = TT(eq[:, t, :, :], theirs, mine, ALU.is_equal)
                link(last)
                for t in range(NT):
                    last = TT(eq[:, t, :, :], eq[:, t, :, :], first[:, :, :], ALU.mult)
                link(last)
                flat = lambda a: a[:, :, :, :].rearrange("p a e f -> p (a e f)")
                TT(flat(gt), flat(gt), flat(eq), ALU.add).then_inc(s_gate, 1)
                dve.wait_ge(s_gate, at(b, 1, 3))
                RED(rank[:, :, :].rearrange("p a e -> p (a e)"), gt[:, :, :, :].rearrange("p a e f -> p (a e) f"),
                    AX.X, ALU.add).then_inc(s_gate, 1)
                dve.wait_ge(s_gate, at(b, 2, 3))
                nc.vector.scalar_tensor_tensor(gate[:, :, :], rank[:, :, :], 2.0, prob[:, :, :], ALU.is_lt,
                                               ALU.mult).then_inc(s_gate, 1)
                dve.wait_ge(s_gate, at(b, 3, 3))
                dve.wait_ge(s_st, at(b, 0, unit=16, **CREDIT))
                for e in range(E):
                    dve.wait_ge(s_yp, at(b, e + 1, E))
                    if e:
                        dve.wait_ge(s_acc, at(b, e, E))
                    for t in range(NT):
                        last = nc.vector.scalar_tensor_tensor(acc[:, t, :], pY[e % 2][:, t, :], gate[:, t, e:e + 1],
                                                              (acc if e else h3)[:, t, :], ALU.mult, ALU.add)
                    last.then_inc(s_acc, 1)
                dve.wait_ge(s_acc, at(b, E, E))
                dve.wait_ge(s_bp, at(b, 1))
                TT(acc[:, :, :].rearrange("p a c -> p (a c)"), acc[:, :, :].rearrange("p a c -> p (a c)"), pA[:, :],
                   ALU.add).then_inc(s_out, 1)
                assert m[0] == PER, m[0]

        @block.scalar
        def _(sc):
            A = nc.scalar.activation
            sc.wait_ge(s_w, NW)
            with sc.Fori(0, NB) as b:
                sc.wait_ge(s_in, at(b, 1) * 32)
                A(oTw[:, :, :], oT[:, :, :], ACT.Copy, scale=nw[:, 0:1]).then_inc(s_ow, 1)
                sc.wait_ge(s_xTp, at(b, 1))
                A(xT[:, :, :].rearrange("p c t -> p (c t)"), pA[:, :], ACT.Copy).then_inc(s_xT, 1)
                for e in range(E):
                    sc.wait_ge(s_hp, at(b, e + 1, E))
                    if e >= 2:
                        sc.wait_ge(s_yp, at(b, e - 1, E))
                    for c in range(CT):
                        last = A(hid[:, e % 2, c, :], pH[e % 2][:, c, :], ACT.Gelu_apprx_tanh, bias=bi[:, e, c:c + 1])
                    last.then_inc(s_hid, 1)
                    if e == 1:
                        sc.wait_ge(s_gTp, at(b, 1))
                        A(gateT[:, :], pG[0:E, 0:T], ACT.Copy).then_inc(s_gT, 1)

        @block.tensor
        def _(pe):
            mm, tr = nc.tensor.matmul, nc.tensor.transpose
            pe.wait_ge(s_w, NW)
            with pe.Fori(0, NB) as b:
                pe.wait_ge(s_ow, at(b, 1))
                pe.wait_ge(s_out, at(b, 0, **CREDIT))
                for t in range(NT):
                    for c in range(CT):
                        last = mm(pA[:, t * C:(t + 1) * C], oTw[:, c, t * P:(t + 1) * P], wo[:, c, :],
                                  start=(c == 0), stop=(c == CT - 1))
                last.then_inc(s_wo, 1)
                pe.wait_ge(s_ln, at(b, 1))
                for i in range(CT):
                    for j in range(NT):
                        last = tr(pA[:, i * T + j * P:i * T + (j + 1) * P], xn[:, j, i * P:(i + 1) * P], ident[:, :])
                last.then_inc(s_xTp, 1)
                pe.wait_ge(s_xT, at(b, 1))
                for t in range(NT):
                    for c in range(CT):
                        last = mm(pG[:, t * E:(t + 1) * E], xT[:, c, t * P:(t + 1) * P], wr[:, c, :], start=(c == 0),
                                  stop=(c == CT - 1))
                last.then_inc(s_lg, 1)

                def up(e):
                    if e >= 2:
                        pe.wait_ge(s_hid, at(b, e - 1, E))
                    for f in range(CT):
                        for c in range(CT):
                            last = mm(pH[e % 2][:, f, :], wi[:, e, c, f * P:(f + 1) * P], xT[:, c, :],
                                      start=(c == 0), stop=(c == CT - 1))
                    last.then_inc(s_hp, 1)

                def down(e):
                    pe.wait_ge(s_hid, at(b, e + 1, E))
                    if e >= 2:
                        pe.wait_ge(s_acc, at(b, e - 1, E))
                    for t in range(NT):
                        for c in range(CT):
                            last = mm(pY[e % 2][:, t, :], hid[:, e % 2, c, t * P:(t + 1) * P], wd[:, e, c, :],
                                      start=(c == 0), stop=(c == CT - 1))
                    last.then_inc(s_yp, 1)

                up(0)
                for e in range(1, E + 1):
                    if e < E:
                        up(e)
                    if e == 2:
                        pe.wait_ge(s_gate, at(b, 3, 3))
                        for t in range(NT):
                            last = tr(pG[0:E, t * P:(t + 1) * P], gate[:, t, :], ident[:, :])
                        last.then_inc(s_gTp, 1)
                    down(e - 1)
                pe.wait_ge(s_gT, at(b, 1))
                for t in range(NT):
                    last = mm(pA[:, t * C:(t + 1) * C], gateT[:, t * P:(t + 1) * P], bd[:, :], start=True, stop=True)
                last.then_inc(s_bp, 1)


def kernel(**inputs):
    import numpy as _np
    import concourse.bacc as _bacc
    from concourse import mybir as _mybir
    from concourse.bass_utils import run_bass_kernel_spmd as _run

    a = {k: _np.asarray(v) for k, v in inputs.items()}
    rows = lambda v: _np.broadcast_to(v.reshape(1, -1), (P, v.size))
    tap = _np.zeros((3, XR, 3, TR), _np.float32)
    for c in range(3):
        for dy in range(3):
            for r in range(TR):
                tap[c, r + dy, dy, r] = GRAY[c]
    s, t = _np.arange(P)[:, None], _np.arange(P)[None, :]
    tri = (t >= s).astype(_np.float32)
    causal = _np.concatenate([tri, _np.ones((P, P), _np.float32), tri], 1)
    parity = _np.stack([(_np.arange(P) // D) % 2 == i for i in range(2)], 1).astype(_np.float32)
    first = _np.broadcast_to((_np.arange(E)[None, :] < _np.arange(E)[:, None]).astype(_np.float32), (P, E, E))
    laid = {
        "x": a["x"],
        "scharr": rows(a["L0_tok_scharr"]).reshape(P, 2, 3, 3),
        "taps": tap.reshape(KX, 3, TR),
        "ident": _np.eye(P, dtype=_np.float32),
        "causal": causal,
        "first": first,
        "parity": parity,
        "w_qkv": a["L0_attn_w_qkv"].T,
        "b_qkv": rows(a["L0_attn_b_qkv"]),
        "w_out": a["L0_attn_w_out"].T,
        "b_out": rows(a["L0_attn_b_out"]),
        "omega": a["L0_attn_omega"].transpose(1, 2, 0, 3).reshape(C, F),
        "nodes": _np.tile(_np.repeat(a["L0_attn_quad_nodes"], M), 2).reshape(P, 1),
        "weights": _np.tile(_np.repeat(a["L0_attn_quad_weights"], M), 2).reshape(P, 1),
        "ffn_w": a["L0_ffn_weight"].T,
        "ffn_b": rows(a["L0_ffn_bias"]),
        "w1_qkv": _np.concatenate([a["L1_attn_Wq"], a["L1_attn_Wk"], a["L1_attn_Wv"]], 0).T,
        "w1_b": a["L1_attn_Wb"].T,
        "w1_o": a["L1_attn_Wo"].T,
        "conv_w": _np.concatenate([a["L1_attn_conv_q"], a["L1_attn_conv_k"], a["L1_attn_conv_v"]], 0),
        "norm_w": _np.tile(a["L1_attn_o_norm_w"], P // D).reshape(P, 1),
        "router": a["L1_ffn_router_w"],
        "w_in": a["L1_ffn_w_in"],
        "b_in": a["L1_ffn_b_in"],
        "w_dn": a["L1_ffn_w_out"],
        "b_dn": a["L1_ffn_b_out"],
    }
    nc = _bacc.Bacc("TRN2", target_bir_lowering=False, num_devices=1)
    arrays, args = {}, {}
    for name, v in laid.items():
        v = _np.ascontiguousarray(v)
        arrays[f"in_{name}"] = v
        args[name] = nc.dram_tensor(f"in_{name}", v.shape, _mybir.dt.from_np(v.dtype), kind="ExternalInput").ap()
    shape = (a["x"].shape[0], T, C)
    args["out"] = nc.dram_tensor("out_0", shape, _mybir.dt.float32, kind="ExternalOutput").ap()
    tower(nc, **args)
    return _run(nc, [arrays], core_ids=[0]).results[0]["out_0"]
```

```python
import concourse.bass as bass
from concourse import mybir
from contextlib import ExitStack
import numpy as np

P = 128
T = 256
C = 256
NT = T // P
CT = C // P
H = 16
D = C // H
NODES, M = 2, 32
F = NODES * M
E = 8
TR = 37
XT = -(-T // TR)
XR = TR + 2
KX = 3 * XR
GRAY = (0.2989, 0.587, 0.114)
LANES = P // H
TB = 64
IDLE = 33
LN_EPS = 1e-5
RMS_EPS = 1e-6


def at(b, k, per=1, unit=1, credit=0):
    return b * (per * unit) + (k * unit + credit)


CREDIT = dict(credit=1)


class Cols:

    def __init__(self, start, size):
        self.start, self.size = start, size


def b_is(b, value):
    return isinstance(b, int) and b == value


def apart(eng, idle, sem, value, turn=[0]):
    eng.wait_ge(sem, value)
    turn[0] = turn[0] % (IDLE - 1) + 1
    if eng.engine == mybir.EngineType.Pool:
        eng.tensor_tensor(idle[:, turn[0]:turn[0] + 1], idle[:, 0:1], idle[:, 0:1], mybir.AluOpType.add)
    else:
        eng.memset(idle[:, turn[0]:turn[0] + 1], 0.0)


def image(ap, b):
    return ap[bass.ds(b, 1), :, :].rearrange("o (c p) t -> p (o c) t", p=P)


def tower(nc, x, scharr, taps, ident, causal, first, parity, w_qkv, b_qkv, w_out, b_out, omega, nodes, weights,
          ffn_w, ffn_b, w1_qkv, w1_b, w1_o, conv_w, norm_w, router, w_in, b_in, w_dn, b_dn, out):
    f32, bf16, f16, f8 = mybir.dt.float32, mybir.dt.bfloat16, mybir.dt.float16, mybir.dt.float8e4
    NB = x.shape[0]
    scratch = {n: nc.dram_tensor(f"scr_{n}", s, f32, kind="Internal").ap() for n, s in
               {"h": (NB, T, C), "q": (NB, C, T), "k": (NB, C, T), "v": (NB, C, T), "o": (NB, C, T),
                "beta": (NB, H, T)}.items()}
    front(nc, NB, x, scharr, taps, ident, causal, parity, w_qkv, b_qkv, w_out, b_out, omega, nodes, weights,
          ffn_w, ffn_b, w1_qkv, w1_b, conv_w, scratch)
    delta_rule(nc, NB, scratch)
    back(nc, NB, ident, first, w1_o, norm_w, router, w_in, b_in, w_dn, b_dn, scratch, out)


def front(nc, NB, x, scharr, taps, ident_d, causal_d, parity_d, w_qkv, b_qkv, w_out, b_out, omega, nodes, weights,
          ffn_w, ffn_b, w1_qkv, w1_b, conv_w, scratch):
    f32, bf16, f16, f8 = mybir.dt.float32, mybir.dt.bfloat16, mybir.dt.float16, mybir.dt.float8e4
    ALU, ACT, AX = mybir.AluOpType, mybir.ActivationFunctionType, mybir.AxisListType
    LO, HI = float(np.exp(-20.0)), float(np.exp(20.0))
    NF = 8
    with ExitStack() as ctx:
        sb = lambda n, s, t=f32: ctx.enter_context(nc.sbuf_tensor(n, s, t))
        ps = lambda n, s, t=f32: ctx.enter_context(nc.psum_tensor(n, s, t))
        sem = lambda n: ctx.enter_context(nc.semaphore(n))

        idle_pool, idle_dve = sb("idle_pool", [1, IDLE]), sb("idle_dve", [1, IDLE])
        ident = sb("ident", [P, P])
        identb = sb("identb", [P, P], bf16)
        causal = sb("causal", [P, T + P])
        parity = sb("parity", [P, 2])
        sch = sb("sch", [P, 2, 3, 3])
        tap = sb("tap", [KX, 3, TR])
        band = sb("band", [KX, 3, 2, TR])
        wqkv = sb("wqkv", [P, CT, 3 * C])
        bqkv = sb("bqkv", [P, 3 * C])
        wout = sb("wout", [P, CT, C])
        bout = sb("bout", [P, C])
        om = sb("om", [P, CT, F])
        omblk = sb("omblk", [P, CT, 2, F])
        fw = sb("fw", [P, CT, C])
        fw8 = sb("fw8", [P, CT, C], f8)
        fwa = sb("fwa", [P, CT, C])
        fwb = sb("fwb", [P, CT, C])
        fwm = sb("fwm", [P, CT, C])
        fwq = sb("fwq", [P, CT, C], bf16)
        fb = sb("fb", [P, C])
        w1 = sb("w1", [P, CT, 3 * C])
        w1b = sb("w1b", [P, CT, H])
        cw = sb("cw", [P, 6, 4])
        cwh = sb("cwh", [P, 6, 4])
        node = sb("node", [P, 1])
        nneg = sb("nneg", [P, 1])
        n2p = sb("n2p", [P, 1])
        root2s = sb("root2s", [P, 1])
        wgt = sb("wgt", [P, 1])
        wpos = sb("wpos", [P, 1])
        wroot = sb("wroot", [P, 1])
        sqscale = sb("sqscale", [P, 1])
        half = sb("half", [P, 1])
        quarter = sb("quarter", [P, 1])
        minus_half = sb("minus_half", [P, NT * 2 * H])

        xin = sb("xin", [P, XT, C + 2])
        edges = sb("edges", [P, CT, 2, T])
        edge = sb("edge", [P, CT, T])
        h0 = sb("h0", [P, NT, C])
        h0b = sb("h0b", [P, NB * NT, C])
        stats = sb("stats", [P, NT, 6])
        mv = sb("mv", [P, NT, 2])
        vare = sb("vare", [P, NT])
        rstd = sb("rstd", [P, NT])
        xn1 = sb("xn1", [P, NT, C])
        xT1 = sb("xT1", [P, CT, T])
        xn3 = sb("xn3", [P, NT, C])
        xT3 = sb("xT3", [P, CT, T])
        qk = sb("qk", [P, NT, 2 * C])
        qksq = sb("qksq", [P, NT, 2 * C])
        vv = sb("vv", [P, NT, H, D + 1])
        qkss = sb("qkss", [P, NT * 2 * H])
        qkss2 = sb("qkss2", [P, NT * 2 * H])
        qkr = sb("qkr", [P, NT * 2 * H])
        qkn = sb("qkn", [P, NT, 2 * C])
        qkT = sb("qkT", [P, 4, T])
        fsq = sb("fsq", [P, 2, 2, T])
        fexp = sb("fexp", [P, 2, 2, T])
        feats = sb("feats", [P, 2, 8, T])
        att = sb("att", [P, 2, T + P])
        den = sb("den", [P, NT, 8])
        rden = sb("rden", [P, NT, 8])
        on = sb("on", [P, NT, H, D])
        onT = sb("onT", [P, CT, T])
        h1 = sb("h1", [P, NT, C])
        h1b = sb("h1b", [P, NT, C])
        x8 = sb("x8", [P, NT, C], f8)
        x8b = sb("x8b", [P, NT, C], bf16)
        x8T = sb("x8T", [P, CT, T], bf16)
        y16 = sb("y16", [P, NT, C], f16)
        h2 = sb("h2", [P, NT, C])
        raw = sb("raw", [P, 6, T + 3])
        yc = sb("yc", [P, 6, T])
        th = sb("th", [P, 6, T])
        act = sb("act", [P, 6, T])
        thb = sb("thb", [H, T])
        beta = sb("beta", [H, T])

        pf = ps("pf", [P, 2, 512])
        pe_ = [ps(f"pfeat{i}", [P, 2, T]) for i in range(2)]
        psc = [ps(f"pscore{i}", [P, 512]) for i in range(2)]
        ppv = ps("ppv", [P, NT, 8, D + 1])
        ptr = ps("ptr", [P, 512])

        s_w = sem("weights_loaded")
        s_set = sem("setup_step")
        s_band = sem("band_ready")
        s_setp = sem("pool_setup_step")
        s_x = sem("x_loaded")
        s_conv = sem("conv_done")
        s_edges = sem("edges_abs")
        s_edge = sem("edge_summed")
        s_hT = sem("h0_in_psum")
        s_h0 = sem("h0_ready")
        s_stat1 = sem("ln1_stats")
        s_stat2 = sem("ln2_stats")
        s_stat3 = sem("ln3_stats")
        s_var1 = sem("ln1_variance")
        s_var2 = sem("ln2_variance")
        s_var3 = sem("ln3_variance")
        s_qkmax = sem("qk_sums_guarded")
        s_rstd1 = sem("ln1_rstd")
        s_rstd2 = sem("ln2_rstd")
        s_rstd3 = sem("ln3_rstd")
        s_xn1 = sem("xn1_ready")
        s_x8 = sem("x8_ready")
        s_xn3 = sem("xn3_ready")
        s_bn1 = sem("ln1_partial_stats")
        s_bn2 = sem("ln2_partial_stats")
        s_bn3 = sem("ln3_partial_stats")
        s_clip = sem("exponentials_clipped")
        s_den = sem("denominators")
        s_tap = sem("short_conv_taps")
        s_xT1p = sem("xT1_in_psum")
        s_xT1 = sem("xT1_ready")
        s_xT3p = sem("xT3_in_psum")
        s_xT3 = sem("xT3_ready")
        s_qkp = sem("qk_in_psum")
        s_vp = sem("v_in_psum")
        s_qk = sem("qk_ready")
        s_v = sem("v_ready")
        s_qksq = sem("qk_squared")
        s_qkss = sem("qk_sums")
        s_qkr = sem("qk_rnorm")
        s_qkn = sem("qk_normed")
        s_qkTp = sem("qkT_in_psum")
        s_qkT = sem("qkT_ready")
        s_fp = sem("proj_in_psum")
        s_fe = sem("feature_parts")
        s_f = sem("features_ready")
        s_sc = sem("scores_in_psum")
        s_att = sem("att_masked")
        s_pv = sem("pv_done")
        s_on = sem("out_normed")
        s_onTp = sem("onT_in_psum")
        s_onT = sem("onT_ready")
        s_op = sem("proj_out_in_psum")
        s_h0b = sem("h0_plus_bias")
        s_h1 = sem("h1_ready")
        s_h1b = sem("h1_plus_bias")
        s_x8b = sem("x8_as_bf16")
        s_x8Tp = sem("x8T_in_psum")
        s_x8T = sem("x8T_ready")
        s_yp = sem("ffn_in_psum")
        s_y16 = sem("ffn_as_f16")
        s_h2 = sem("h2_ready")
        s_h2st = sem("h2_stored")
        s_l1p = sem("l1_in_psum")
        s_raw = sem("l1_raw")
        s_yc = sem("short_conv")
        s_th = sem("tanh_done")
        s_act = sem("l1_silu")
        s_bp = sem("beta_in_psum")
        s_thb = sem("beta_tanh")
        s_beta = sem("beta_ready")
        s_st = sem("l1_stored")
        s_bst = sem("beta_stored")
        block = ctx.enter_context(nc.Block())

        loads = [(ident, ident_d), (causal, causal_d), (parity, parity_d), (sch, scharr), (tap, taps),
                 (wqkv, w_qkv.rearrange("(c p) n -> p c n", p=P)), (bqkv, b_qkv),
                 (wout, w_out.rearrange("(c p) n -> p c n", p=P)), (bout, b_out),
                 (om, omega.rearrange("(c p) n -> p c n", p=P)),
                 (fw, ffn_w.rearrange("(c p) n -> p c n", p=P)), (fb, ffn_b),
                 (w1, w1_qkv.rearrange("(c p) n -> p c n", p=P)), (w1b, w1_b.rearrange("(c p) n -> p c n", p=P)),
                 (cw, conv_w.rearrange("(c p) k -> p c k", p=P)), (node, nodes), (wgt, weights)]
        NW = 16 * len(loads)
        NX = 16 * 9

        def rounds(engine, body, stages_of=lambda b: (b + 1 < NB, 0 <= b < NB, 0 < b)):
            for b in (-1, 0):
                body(b, *stages_of(b))
            with engine.Fori(1, NB - 2) as b:
                body(b, True, True, True)
            for b in (NB - 2, NB - 1, NB):
                body(b, *stages_of(b))

        @block.sync
        def _(sp):
            for sem_ in (s_conv, s_h2st, s_thb, s_raw, s_bst, s_st):
                sp.sem_inc(sem_, 1)
            for tile, src in loads:
                sp.dma_start(tile[tuple(slice(None) for _ in tile.shape)], src).then_inc(s_w, 16)
            sp.wait_ge(s_set, 1)

            def load(n):
                for c in range(3):
                    img = x[bass.ds(n, 1), c, :, :].rearrange("o r w -> (o r) w")
                    sp.dma_start(xin[c * XR + 1:(c + 1) * XR, 0, 1:C + 1], img[0:XR - 1, :]).then_inc(s_x, 16)
                    mid = bass.AP(tensor=img.tensor, offset=img.offset + (TR - 1) * C,
                                  ap=[[C, XR], [TR * C, XT - 2], [1, C]])
                    sp.dma_start(xin[c * XR:(c + 1) * XR, 1:XT - 1, 1:C + 1], mid).then_inc(s_x, 16)
                    r0 = (XT - 1) * TR - 1
                    sp.dma_start(xin[c * XR:c * XR + T - r0, XT - 1, 1:C + 1], img[r0:T, :]).then_inc(s_x, 16)

            load(0)

            def body(b, a, v, c):
                n, p = b + 1, b - 1
                if v or a:
                    if a and not (isinstance(b, int) and n + 1 >= NB):
                        sp.wait_ge(s_conv, at(n, 1, **CREDIT))
                        load(n + 1)
                if c:
                    sp.wait_ge(s_h2, at(p, 1))
                    sp.dma_start(image(scratch["h"], p), h2[:, :, :]).then_inc(s_h2st, 16)
                    sp.wait_ge(s_beta, at(p, 1))
                    sp.dma_start(scratch["beta"][bass.ds(p, 1), :, :].rearrange("o h t -> (o h) t"),
                                 beta[:, :]).then_inc(s_bst, 16)
                    sp.wait_ge(s_act, at(p, 1))
                    for i, name in enumerate("qkv"):
                        sp.dma_start(image(scratch[name], p), act[:, 2 * i:2 * i + 2, :]).then_inc(s_st, 16)

            rounds(sp, body)
            sp.wait_ge(s_h2st, 16 * NB + 1)
            sp.wait_ge(s_bst, 16 * NB + 1)
            sp.wait_ge(s_st, 48 * NB + 1)

        @block.gpsimd
        def _(pool):
            n = [0]

            def step(ins):
                n[0] += 1
                ins.then_inc(s_setp, 1)
                pool.wait_ge(s_setp, n[0])

            step(nc.gpsimd.memset(idle_pool[:, :], 0.0))
            step(nc.gpsimd.memset(half[:, :], 0.5))
            step(nc.gpsimd.memset(quarter[:, :], 0.25))
            step(nc.gpsimd.memset(minus_half[:, :], -0.5))
            pool.wait_ge(s_w, NW)
            step(nc.gpsimd.tensor_scalar(n2p[:, :], node[:, :], 0.0, 2.0, ALU.max, ALU.mult))
            step(nc.gpsimd.tensor_tensor(root2s[:, :], n2p[:, :], half[:, :], ALU.pow))
            step(nc.gpsimd.tensor_scalar(nneg[:, :], node[:, :], -1.0, None, ALU.mult))
            step(nc.gpsimd.tensor_scalar(wpos[:, :], wgt[:, :], 0.0, None, ALU.max))
            step(nc.gpsimd.tensor_tensor(wroot[:, :], wpos[:, :], quarter[:, :], ALU.pow))
            step(nc.gpsimd.tensor_scalar(sqscale[:, :], wroot[:, :], float(M ** -0.5), None, ALU.mult))

            def body(b, a, v, c):
                n, p = b + 1, b - 1

                def rsqrt_ln(i, s_stat, s_var, s_rstd):
                    apart(pool, idle_pool, s_stat, at(i, 1))
                    nc.gpsimd.tensor_scalar(vare[:, :], mv[:, :, 1], LN_EPS, None, ALU.add).then_inc(s_var, 1)
                    pool.wait_ge(s_var, at(i, 1))
                    nc.gpsimd.tensor_tensor(rstd[:, :], vare[:, :], minus_half[:, 0:NT], ALU.pow).then_inc(s_rstd, 1)

                if a:
                    pool.wait_ge(s_edges, at(n, 1))
                    nc.gpsimd.tensor_tensor(edge[:, :, :], edges[:, :, 0, :], edges[:, :, 1, :],
                                            ALU.add).then_inc(s_edge, 1)
                    rsqrt_ln(n, s_stat1, s_var1, s_rstd1)
                    nc.gpsimd.tensor_tensor(h0b[:, bass.ds(n * NT, NT), :], h0[:, :, :],
                                            bout[:, :].unsqueeze(1).to_broadcast([P, NT, C]),
                                            ALU.add).then_inc(s_h0b, 1)
                if c:
                    rsqrt_ln(p, s_stat2, s_var2, s_rstd2)
                    nc.gpsimd.tensor_tensor(h1b[:, :, :], h1[:, :, :], fb[:, :].unsqueeze(1).to_broadcast([P, NT, C]),
                                            ALU.add).then_inc(s_h1b, 1)
                    apart(pool, idle_pool, s_x8, at(p, 1))
                    nc.gpsimd.tensor_copy(x8b[:, :, :], x8[:, :, :]).then_inc(s_x8b, 1)
                if a:
                    apart(pool, idle_pool, s_qkss, at(n, 1))
                    nc.gpsimd.tensor_scalar(qkss2[:, :], qkss[:, :], 1e-24, None, ALU.max).then_inc(s_qkmax, 1)
                    pool.wait_ge(s_qkmax, at(n, 1))
                    nc.gpsimd.tensor_tensor(qkr[:, :], qkss2[:, :], minus_half[:, :], ALU.pow).then_inc(s_qkr, 1)
                if c:
                    rsqrt_ln(p, s_stat3, s_var3, s_rstd3)

            rounds(pool, body)

        @block.vector
        def _(dve):
            n = [0]

            def step(ins):
                n[0] += 1
                ins.then_inc(s_set, 1)
                dve.wait_ge(s_set, n[0])

            step(nc.vector.memset(xin[:, :, :], 0.0))
            step(nc.vector.memset(raw[:, :, 0:3], 0.0))
            step(nc.vector.memset(vv[:, :, :, D:D + 1], 1.0))
            dve.wait_ge(s_w, NW)
            step(nc.vector.tensor_copy(identb[:, :], ident[:, :]))
            step(nc.vector.tensor_scalar(cwh[:, :, :], cw[:, :, :], 0.5, None, ALU.mult))
            for a in range(2):
                step(nc.vector.tensor_scalar(omblk[:, :, a, :], om[:, :, :], parity[:, a:a + 1], None, ALU.mult))
            for dx in range(3):
                for f in range(2):
                    step(nc.vector.tensor_scalar(band[:, dx, f, :], tap[:, 0, :], sch[0:KX, f, 0, dx:dx + 1], None,
                                                 ALU.mult))
                    for dy in (1, 2):
                        step(nc.vector.scalar_tensor_tensor(band[:, dx, f, :], tap[:, dy, :],
                                                            sch[0:KX, f, dy, dx:dx + 1], band[:, dx, f, :],
                                                            ALU.mult, ALU.add))
            step(nc.vector.tensor_scalar(fw8[:, :, :], fw[:, :, :], 240.0, -240.0, ALU.min, ALU.max, saturate=False))
            step(nc.vector.tensor_copy(fwa[:, :, :], fw8[:, :, :]))
            step(nc.vector.tensor_scalar(fwb[:, :, :], fw[:, :, :], 448.0, -448.0, ALU.min, ALU.max))
            step(nc.vector.tensor_scalar(fw8[:, :, :], fwb[:, :, :], 0.5, None, ALU.mult, saturate=False))
            step(nc.vector.tensor_copy(fwb[:, :, :], fw8[:, :, :]))
            step(nc.vector.scalar_tensor_tensor(fwb[:, :, :], fwb[:, :, :], 2.0, fwa[:, :, :], ALU.mult, ALU.subtract))
            step(nc.vector.tensor_tensor(fwm[:, :, :], fw[:, :, :], fw[:, :, :], ALU.mult))
            step(nc.vector.tensor_scalar(fwm[:, :, :], fwm[:, :, :], 128.0 * 128.0, None, ALU.is_ge))
            step(nc.vector.tensor_tensor(fwb[:, :, :], fwb[:, :, :], fwm[:, :, :], ALU.mult))
            nc.vector.tensor_tensor(fwq[:, :, :], fwa[:, :, :], fwb[:, :, :], ALU.add).then_inc(s_band, 1)

            def body(b, a, v, c):
                n, p = b + 1, b - 1

                def ln_stats(h, i, s_h, s_bn, s_stat):
                    dve.wait_ge(s_h, at(i, 1))
                    for t in range(NT):
                        last = nc.vector.bn_stats(stats[:, t, :], h[:, t, :])
                    last.then_inc(s_bn, 1)
                    apart(dve, idle_dve, s_bn, at(i, 1))
                    for t in range(NT):
                        last = nc.vector.bn_aggr(mv[:, t, :], stats[:, t, :])
                    last.then_inc(s_stat, 1)

                def ln_apply(h, out, i, s_rstd, s_out, **kinds):
                    apart(dve, idle_dve, s_rstd, at(i, 1))
                    for t in range(NT):
                        last = nc.vector.tensor_scalar(out[:, t, :], h[:, t, :], mv[:, t, 0:1], rstd[:, t:t + 1],
                                                       ALU.subtract, ALU.mult, **kinds)
                    last.then_inc(s_out, 1)

                def values():
                    dve.wait_ge(s_vp, at(b, 1))
                    for t in range(NT):
                        last = nc.vector.tensor_tensor(vv[:, t, :, 0:D],
                                                       ptr[:, t * C:(t + 1) * C].rearrange("p (h d) -> p h d", h=H),
                                                       bqkv[:, 2 * C:3 * C].rearrange("p (h d) -> p h d", h=H), ALU.add)
                    last.then_inc(s_v, 1)

                def feature(i):
                    dve.wait_ge(s_fe, at(b, i + 1, NF))
                    nc.vector.tensor_scalar(fexp[:, i % 2, :, :], fexp[:, i % 2, :, :], LO, HI, ALU.max,
                                            ALU.min).then_inc(s_clip, 1)
                    dve.wait_ge(s_clip, at(b, i + 1, NF))
                    nc.vector.tensor_tensor(feats[:, i // 4, i % 4:i % 4 + 5:4, :], fsq[:, i % 2, :, :],
                                            fexp[:, i % 2, :, :], ALU.mult).then_inc(s_f, 1)

                def mask(h):
                    dve.wait_ge(s_sc, at(b, h + 1, H))
                    if h >= 2:
                        dve.wait_ge(s_pv, at(b, h - 1, H))
                    nc.vector.tensor_tensor(att[:, h % 2, :], psc[h % 2][:, 0:T + P], causal[:, :],
                                            ALU.mult).then_inc(s_att, 1)

                def divide(g):
                    dve.wait_ge(s_pv, at(b, 8 * (g + 1), H))
                    nc.vector.tensor_scalar(den[:, :, :], ppv[:, :, :, D], 1e-6, None, ALU.max).then_inc(s_den, 1)
                    dve.wait_ge(s_den, at(b, 2 * g + 1, 4))
                    nc.vector.reciprocal(rden[:, :, :], den[:, :, :]).then_inc(s_den, 1)
                    dve.wait_ge(s_den, at(b, 2 * g + 2, 4))
                    for t in range(NT):
                        last = nc.vector.tensor_tensor(on[:, t, 8 * g:8 * g + 8, :], ppv[:, t, :, 0:D],
                                                       rden[:, t, :].unsqueeze(2).to_broadcast([P, 8, D]), ALU.mult)
                    last.then_inc(s_on, 1)

                def h0_stats():
                    dve.wait_ge(s_hT, at(n, 1))
                    nc.vector.tensor_copy(h0[:, :, :].rearrange("p a c -> p (a c)"), ptr[:, :]).then_inc(s_h0, 1)
                    ln_stats(h0, n, s_h0, s_bn1, s_stat1)

                def qk_bias():
                    dve.wait_ge(s_qkp, at(n, 1))
                    nc.vector.tensor_tensor(qk[:, :, :], pf[:, :, :],
                                            bqkv[:, 0:2 * C].unsqueeze(1).to_broadcast([P, NT, 2 * C]),
                                            ALU.add).then_inc(s_qk, 1)

                def qk_sums():
                    dve.wait_ge(s_qksq, at(n, 1))
                    nc.vector.tensor_reduce(qkss[:, :], qksq[:, :, :].rearrange("p a (h d) -> p (a h) d", d=D), AX.X,
                                            ALU.add).then_inc(s_qkss, 1)

                def qk_norm():
                    dve.wait_ge(s_qkr, at(n, 1))
                    nc.vector.tensor_tensor(qkn[:, :, :].rearrange("p a (h d) -> p (a h) d", d=D),
                                            qk[:, :, :].rearrange("p a (h d) -> p (a h) d", d=D),
                                            qkr[:, :].unsqueeze(2).to_broadcast([P, NT * 2 * H, D]),
                                            ALU.mult).then_inc(s_qkn, 1)

                def h1_stats():
                    dve.wait_ge(s_op, at(p, 1))
                    dve.wait_ge(s_h0b, at(p, 1))
                    nc.vector.tensor_tensor(h1[:, :, :], ptr[:, :].rearrange("p (a c) -> p a c", a=NT),
                                            h0b[:, bass.ds(p * NT, NT), :], ALU.add).then_inc(s_h1, 1)
                    ln_stats(h1, p, s_h1, s_bn2, s_stat2)

                def h2_stats():
                    dve.wait_ge(s_y16, at(p, 1))
                    dve.wait_ge(s_h1b, at(p, 1))
                    dve.wait_ge(s_h2st, at(p, 0, unit=16, **CREDIT))
                    nc.vector.tensor_tensor(h2[:, :, :], y16[:, :, :], h1b[:, :, :], ALU.add).then_inc(s_h2, 1)
                    ln_stats(h2, p, s_h2, s_bn3, s_stat3)

                def short_conv(k):
                    if k == 3:
                        dve.wait_ge(s_raw, at(p, 3, 3, **CREDIT))
                        for o in range(6):
                            last = nc.vector.tensor_scalar(yc[:, o, :], raw[:, o, 3:T + 3], cwh[:, o, 3:4], None,
                                                           ALU.mult)
                        last.then_inc(s_tap, 1)
                        return
                    dve.wait_ge(s_tap, at(p, k + 1, 3))
                    for o in range(6):
                        last = nc.vector.scalar_tensor_tensor(yc[:, o, :], raw[:, o, k:k + T], cwh[:, o, k:k + 1],
                                                              yc[:, o, :], ALU.mult, ALU.add)
                    last.then_inc(s_yc if k == 2 else s_tap, 1)

                def beta_out():
                    dve.wait_ge(s_thb, at(p, 1, **CREDIT))
                    dve.wait_ge(s_bst, at(p, 0, unit=16, **CREDIT))
                    nc.vector.tensor_scalar(beta[:, :], thb[:, :], 0.5, 0.5, ALU.mult, ALU.add).then_inc(s_beta, 1)

                def silu():
                    dve.wait_ge(s_th, at(p, 1))
                    dve.wait_ge(s_st, at(p, 0, unit=48, **CREDIT))
                    nc.vector.scalar_tensor_tensor(act[:, :, :], th[:, :, :], 1.0, yc[:, :, :], ALU.add,
                                                   ALU.mult).then_inc(s_act, 1)

                if v:
                    values()
                    for i in range(4):
                        feature(i)
                if a:
                    h0_stats()
                if v:
                    feature(4)
                if a:
                    ln_apply(h0, xn1, n, s_rstd1, s_xn1)
                if c:
                    h1_stats()
                if v:
                    feature(5)
                if c:
                    ln_apply(h1, x8, p, s_rstd2, s_x8, saturate=False)
                if a:
                    qk_bias()
                if v:
                    feature(6)
                if a:
                    qk_sums()
                if v:
                    feature(7)
                if a:
                    qk_norm()
                if c:
                    h2_stats()
                if v:
                    mask(0)
                    mask(1)
                if c:
                    ln_apply(h2, xn3, p, s_rstd3, s_xn3)
                if v:
                    for h in range(2, 8):
                        mask(h)
                if c:
                    short_conv(3)
                if v:
                    mask(8)
                    divide(0)
                    mask(9)
                if c:
                    short_conv(0)
                if v:
                    mask(10)
                if c:
                    short_conv(1)
                if v:
                    mask(11)
                if c:
                    short_conv(2)
                if v:
                    mask(12)
                if c:
                    beta_out()
                if v:
                    mask(13)
                    mask(14)
                if c:
                    silu()
                if v:
                    mask(15)
                    divide(1)

            rounds(dve, body)

        @block.scalar
        def _(sc):
            A = nc.scalar.activation
            sc.wait_ge(s_setp, 10)

            def body(b, a, v, c):
                n, p = b + 1, b - 1

                def feature(i):
                    sc.wait_ge(s_fp, at(b, i + 1, NF))
                    if i >= 2:
                        sc.wait_ge(s_f, at(b, i - 1, NF))
                    A(fsq[:, i % 2, :, :], pe_[i % 2][:, :, :], ACT.Square, scale=sqscale[:, 0:1])
                    A(fexp[:, i % 2, :, :], pe_[i % 2][:, :, :], ACT.Exp, bias=nneg[:, 0:1],
                      scale=root2s[:, 0:1]).then_inc(s_fe, 1)

                if v:
                    feature(0)
                    feature(1)
                if a:
                    sc.wait_ge(s_conv, at(n, 1, **CREDIT))
                    A(edges[:, :, :, :].rearrange("p c f t -> p c (f t)"), pf[:, :, :], ACT.Abs,
                      scale=0.5).then_inc(s_edges, 1)
                if v:
                    feature(2)
                if c:
                    sc.wait_ge(s_onTp, at(p, 1))
                    A(onT[:, :, :].rearrange("p c t -> p (c t)"), ptr[:, :], ACT.Copy).then_inc(s_onT, 1)
                if v:
                    for i in (3, 4, 5):
                        feature(i)
                if a:
                    sc.wait_ge(s_xT1p, at(n, 1))
                    A(xT1[:, :, :].rearrange("p c t -> p (c t)"), ptr[:, :], ACT.Copy).then_inc(s_xT1, 1)
                if v:
                    feature(6)
                if a:
                    sc.wait_ge(s_qk, at(n, 1))
                    A(qksq[:, :, :], qk[:, :, :], ACT.Square).then_inc(s_qksq, 1)
                if c:
                    sc.wait_ge(s_x8Tp, at(p, 1))
                    A(x8T[:, :, :].rearrange("p c t -> p (c t)"), ptr[:, 0:T].bitcast(bf16), ACT.Copy).then_inc(s_x8T, 1)
                if v:
                    feature(7)
                if c:
                    sc.wait_ge(s_yp, at(p, 1))
                    A(y16[:, :, :].rearrange("p c t -> p (c t)"), ptr[:, :], ACT.Copy).then_inc(s_y16, 1)
                    sc.wait_ge(s_xT3p, at(p, 1))
                    A(xT3[:, :, :].rearrange("p c t -> p (c t)"), ptr[:, :], ACT.Copy).then_inc(s_xT3, 1)
                    for r in range(3):
                        sc.wait_ge(s_l1p, at(p, r + 1, 3))
                        A(raw[:, 2 * r:2 * r + 2, 3:T + 3], pf[:, r % 2, :].rearrange("p (o t) -> p o t", o=2),
                          ACT.Copy).then_inc(s_raw, 1)
                    sc.wait_ge(s_bp, at(p, 1))
                    A(thb[:, :], ptr[0:H, 0:T], ACT.Tanh, scale=0.5).then_inc(s_thb, 1)
                if a:
                    sc.wait_ge(s_qkTp, at(n, 1))
                    for i in range(2):
                        last = A(qkT[:, 2 * i:2 * i + 2, :], pe_[i][:, :, :], ACT.Copy)
                    last.then_inc(s_qkT, 1)
                if c:
                    sc.wait_ge(s_yc, at(p, 1))
                    A(th[:, :, :], yc[:, :, :], ACT.Tanh).then_inc(s_th, 1)

            rounds(sc, body)

        @block.tensor
        def _(pe):
            mm, tr = nc.tensor.matmul, nc.tensor.transpose
            pe.wait_ge(s_band, 1)

            def body(b, a, v, c):
                n, p = b + 1, b - 1

                def turn(src, dst, ident_):
                    for i in range(2):
                        for j in range(2):
                            last = tr(dst[:, i * T + j * P:i * T + (j + 1) * P], src[:, j, i * P:(i + 1) * P], ident_)
                    return last

                def project(dst, lhs, w, cols):
                    for t in range(NT):
                        for k in range(CT):
                            last = mm(dst[:, t * cols.size:(t + 1) * cols.size], lhs[:, k, t * P:(t + 1) * P],
                                      w[:, k, cols.start:cols.start + cols.size], start=(k == 0), stop=(k == CT - 1))
                    return last

                def conv():
                    pe.wait_ge(s_x, at(n, 1, unit=NX))
                    if not isinstance(b, int) or n >= 1:
                        pe.wait_ge(s_qk, at(n - 1, 1))
                    if not isinstance(b, int) or n >= 2:
                        pe.wait_ge(s_raw, at(n - 2, 0, 3, **CREDIT))
                    for k in range(CT):
                        for j in range(XT):
                            rows = min(TR, T - j * TR)
                            dst = pf[:, k, :].rearrange("p (f t) -> p f t", f=2)[:, :, j * TR:j * TR + rows]
                            for dx in range(3):
                                last = mm(dst, xin[0:KX, j, k * P + dx:k * P + dx + P], band[:, dx, :, 0:rows],
                                          start=(dx == 0), stop=(dx == 2))
                    last.then_inc(s_conv, 1)

                def feature(i):
                    if i == 0:
                        pe.wait_ge(s_qkT, at(b, 1))
                    if i >= 2:
                        pe.wait_ge(s_fe, at(b, i - 1, NF))
                    rows = slice(32 * (i % 4), 32 * (i % 4) + 32)
                    for k in range(CT):
                        last = mm(pe_[i % 2][:, k, :], omblk[rows, k, :, :], qkT[rows, 2 * (i // 4) + k, :],
                                  start=True, stop=True)
                    last.then_inc(s_fp, 1)

                def score(h):
                    if h == 0:
                        pe.wait_ge(s_f, at(b, NF, NF))
                    if h >= 2:
                        pe.wait_ge(s_att, at(b, h - 1, H))
                    rows = slice(F * (h % 2), F * (h % 2) + F)
                    q, k = feats[rows, 0, h // 2, :], feats[rows, 1, h // 2, :]
                    mm(psc[h % 2][:, 0:T], k[:, 0:P], q, start=True, stop=True)
                    mm(psc[h % 2][:, T:T + P], k[:, P:T], q[:, P:T], start=True, stop=True).then_inc(s_sc, 1)

                def value(h):
                    pe.wait_ge(s_att, at(b, h + 1, H))
                    if h == 8:
                        pe.wait_ge(s_on, at(b, 1, 2))
                    w = att[:, h % 2, :]
                    mm(ppv[:, 0, h % 8, :], w[:, 0:P], vv[:, 0, h, :], start=True, stop=True)
                    mm(ppv[:, 1, h % 8, :], w[:, P:T], vv[:, 0, h, :], start=True, stop=False)
                    mm(ppv[:, 1, h % 8, :], w[:, T:T + P], vv[:, 1, h, :], start=False, stop=True).then_inc(s_pv, 1)

                if not isinstance(b, int) or b >= 1:
                    ptr_left = (s_thb, at(p, 0, **CREDIT))
                else:
                    ptr_left = None
                if v:
                    if b_is(b, 0):
                        ptr_left = (s_xT1, at(b, 1))
                    pe.wait_ge(*ptr_left)
                    project(ptr, xT1, wqkv, Cols(2 * C, C)).then_inc(s_vp, 1)
                    ptr_left = (s_v, at(b, 1))
                    feature(0)
                    feature(1)
                if a:
                    conv()
                if v:
                    feature(2)
                if c:
                    if b_is(b, NB):
                        pe.wait_ge(s_on, at(p, 2, 2))
                        pe.wait_ge(*ptr_left)
                    else:
                        pe.wait_ge(*ptr_left)
                        pe.wait_ge(s_on, at(p, 2, 2))
                    for i in range(CT):
                        for j in range(NT):
                            last = tr(ptr[:, i * T + j * P:i * T + (j + 1) * P],
                                      on[:, j, :, :].rearrange("p h d -> p (h d)")[:, i * P:(i + 1) * P], ident[:, :])
                    last.then_inc(s_onTp, 1)
                    ptr_left = (s_onT, at(p, 1))
                if v:
                    feature(3)
                if a:
                    pe.wait_ge(s_edge, at(n, 1))
                    if ptr_left:
                        pe.wait_ge(*ptr_left)
                    turn(edge, ptr[:, :], ident[:, :]).then_inc(s_hT, 1)
                    ptr_left = (s_h0, at(n, 1))
                if v:
                    feature(4)
                if c:
                    pe.wait_ge(s_onT, at(p, 1))
                    pe.wait_ge(*ptr_left)
                    project(ptr, onT, wout, Cols(0, C)).then_inc(s_op, 1)
                    ptr_left = (s_h1, at(p, 1))
                if v:
                    feature(5)
                if a:
                    pe.wait_ge(s_xn1, at(n, 1))
                    pe.wait_ge(*ptr_left)
                    turn(xn1, ptr[:, :], ident[:, :]).then_inc(s_xT1p, 1)
                    ptr_left = (s_xT1, at(n, 1))
                if v:
                    feature(6)
                if a:
                    pe.wait_ge(s_xT1, at(n, 1))
                    project(pf[:, :, :].rearrange("p a k -> p (a k)"), xT1, wqkv, Cols(0, 2 * C)).then_inc(s_qkp, 1)
                if c:
                    pe.wait_ge(s_x8b, at(p, 1))
                    pe.wait_ge(*ptr_left)
                    turn(x8b, ptr[:, 0:T].bitcast(bf16), identb[:, :]).then_inc(s_x8Tp, 1)
                if v:
                    feature(7)
                if c:
                    pe.wait_ge(s_x8T, at(p, 1))
                    project(ptr, x8T, fwq, Cols(0, C)).then_inc(s_yp, 1)
                if v:
                    score(0)
                    score(1)
                    value(0)
                    score(2)
                    value(1)
                if c:
                    pe.wait_ge(s_y16, at(p, 1))
                    pe.wait_ge(s_xn3, at(p, 1))
                    turn(xn3, ptr[:, :], ident[:, :]).then_inc(s_xT3p, 1)
                for r in range(3):
                    if v:
                        score(3 + r)
                        value(2 + r)
                    if c:
                        if r == 0:
                            pe.wait_ge(s_xT3, at(p, 1))
                            if a:
                                pe.wait_ge(s_qk, at(n, 1))
                        if r == 2:
                            pe.wait_ge(s_raw, at(p, 1, 3, **CREDIT))
                        for o in range(2):
                            for k in range(CT):
                                last = mm(pf[:, r % 2, o * T:(o + 1) * T],
                                          w1[:, k, (2 * r + o) * P:(2 * r + o + 1) * P], xT3[:, k, :],
                                          start=(k == 0), stop=(k == CT - 1))
                        last.then_inc(s_l1p, 1)
                if c:
                    for k in range(CT):
                        last = mm(ptr[0:H, 0:T], w1b[:, k, :], xT3[:, k, :], start=(k == 0), stop=(k == CT - 1))
                    last.then_inc(s_bp, 1)
                if v:
                    for h in range(6, 11):
                        score(h)
                        value(h - 1)
                if a:
                    pe.wait_ge(s_qkn, at(n, 1))
                    if v:
                        pe.wait_ge(s_fe, at(b, NF, NF))
                    for j in range(4):
                        for t in range(NT):
                            last = tr(pe_[j // 2][:, j % 2, t * P:(t + 1) * P], qkn[:, t, j * P:(j + 1) * P],
                                      ident[:, :])
                    last.then_inc(s_qkTp, 1)
                if v:
                    for h in range(11, H):
                        score(h)
                        value(h - 1)
                    value(H - 1)

            rounds(pe, body)


def delta_rule(nc, NB, scratch):
    f32 = mybir.dt.float32
    ALU, ACT, AX = mybir.AluOpType, mybir.ActivationFunctionType, mybir.AxisListType
    G, BLOCKS = NB // LANES, T // TB
    lanes = lambda n: scratch[n].rearrange("(g b) (h d) t -> g (b h) d t", b=LANES, h=H)
    with ExitStack() as ctx:
        sb = lambda n, s, t=f32: ctx.enter_context(nc.sbuf_tensor(n, s, t))
        sem = lambda n: ctx.enter_context(nc.semaphore(n))
        idle_pool = sb("d_idle", [1, IDLE])
        kr, qr, vr = (sb(f"d_{n}raw", [P, G, D, TB]) for n in "kqv")
        br = sb("d_beta", [P, G, TB])
        kn, kb, qn, vb = (sb(f"d_{n}", [P, G, D, TB]) for n in ("kn", "kb", "qn", "vb"))
        tmp = sb("d_tmp", [P, G, D, TB])
        ss = sb("d_ss", [P, G, TB])
        ss2 = sb("d_ss2", [P, G, TB])
        rn = sb("d_rn", [P, G, TB])
        dot = sb("d_dot", [P, G, TB])
        ub = sb("d_u", [P, G, D, TB])
        ob = sb("d_o", [P, G, D, TB])
        mh = sb("d_mh", [P, G, TB])
        S = sb("d_S", [P, G, D, D])
        pk = sb("d_pk", [P, G, D, D])
        pq = sb("d_pq", [P, G, D, D])
        outer = sb("d_outer", [P, G, D, D])
        kS = sb("d_kS", [P, G, D])

        s_ld = sem("d_loaded")
        s_free = sem("d_raw_used")
        s_prep = sem("d_prep_step")
        s_pprep = sem("d_pool_prep_step")
        s_aprep = sem("d_act_prep_step")
        s_S = sem("d_state_ready")
        s_pq = sem("d_qS_products")
        s_step = sem("d_vector_step")
        s_o = sem("d_block_ready")
        s_st = sem("d_block_stored")
        s_init = sem("d_init")
        block = ctx.enter_context(nc.Block())
        NLD = 4 * G * 16
        full = [P, G, D, TB]
        over_d = lambda a: a[:, :, :].unsqueeze(2).to_broadcast(full)
        inner = lambda a: a[:, :, :, :].rearrange("p g d t -> p g t d")
        NP, NPP, NA = 10, 10, 3

        @block.sync
        def _(sp):
            for sem_ in (s_free, s_st):
                sp.sem_inc(sem_, 1)
            with sp.Fori(0, BLOCKS) as n:
                sp.wait_ge(s_free, at(n, 0, **CREDIT))
                for g in range(G):
                    for tile, name in ((kr, "k"), (qr, "q"), (vr, "v")):
                        sp.dma_start(tile[:, g, :, :], lanes(name)[g, :, :, bass.ds(n * TB, TB)]).then_inc(s_ld, 16)
                    sp.dma_start(br[:, g, :], scratch["beta"].rearrange("(g b) h t -> g (b h) t", b=LANES)
                                 [g, :, bass.ds(n * TB, TB)]).then_inc(s_ld, 16)
                sp.wait_ge(s_o, at(n, 1))
                for g in range(G):
                    sp.dma_start(lanes("o")[g, :, :, bass.ds(n * TB, TB)], ob[:, g, :, :]).then_inc(s_st, 16)
            sp.wait_ge(s_st, 16 * G * BLOCKS + 1)

        @block.scalar
        def _(sc):
            with sc.Fori(0, BLOCKS) as n:
                sc.wait_ge(s_ld, at(n, 1) * NLD)
                nc.scalar.activation(tmp[:, :, :, :], kr[:, :, :, :], ACT.Square).then_inc(s_aprep, 1)
                sc.wait_ge(s_prep, at(n, 1, NP))
                nc.scalar.activation(tmp[:, :, :, :], qr[:, :, :, :], ACT.Square).then_inc(s_aprep, 1)
                sc.wait_ge(s_prep, at(n, 9, NP))
                nc.scalar.activation(tmp[:, :, :, :], ob[:, :, :, :], ACT.Square).then_inc(s_aprep, 1)

        @block.gpsimd
        def _(pool):
            nc.gpsimd.memset(mh[:, :, :], -0.5).then_inc(s_init, 1)
            nc.gpsimd.memset(idle_pool[:, :], 0.0).then_inc(s_init, 1)
            pool.wait_ge(s_init, 2)
            with pool.Fori(0, BLOCKS) as n:
                m = [0]

                def link(ins):
                    m[0] += 1
                    ins.then_inc(s_pprep, 1)
                    apart(pool, idle_pool, s_pprep, at(n, m[0], NPP))

                TS, TT = nc.gpsimd.tensor_scalar, nc.gpsimd.tensor_tensor
                apart(pool, idle_pool, s_prep, at(n, 1, NP))
                link(TS(ss2[:, :, :], ss[:, :, :], RMS_EPS * RMS_EPS, None, ALU.max))
                link(TT(rn[:, :, :], ss2[:, :, :], mh[:, :, :], ALU.pow))
                apart(pool, idle_pool, s_prep, at(n, 4, NP))
                link(TS(ss2[:, :, :], ss[:, :, :], RMS_EPS * RMS_EPS, None, ALU.max))
                link(TT(rn[:, :, :], ss2[:, :, :], mh[:, :, :], ALU.pow))
                link(TS(rn[:, :, :], rn[:, :, :], float(D) ** -0.5, None, ALU.mult))
                link(TT(vb[:, :, :, :], vr[:, :, :, :], over_d(br), ALU.mult))
                apart(pool, idle_pool, s_prep, at(n, 5, NP))
                link(TT(tmp[:, :, :, :], kn[:, :, :, :], qn[:, :, :, :], ALU.mult))
                apart(pool, idle_pool, s_prep, at(n, 7, NP))
                with pool.Fori(0, TB) as t:
                    pool.wait_ge(s_S, n * TB + t + 1)
                    TT(pq[:, :, :, :], S[:, :, :, :],
                       qn[:, :, :, bass.ds(t, 1)].rearrange("p g d o -> p g (o d)").unsqueeze(2).to_broadcast([P, G, D, D]),
                       ALU.mult).then_inc(s_pq, 1)
                pool.wait_ge(s_prep, at(n, 8, NP))
                link(TT(tmp[:, :, :, :], ub[:, :, :, :], over_d(dot), ALU.mult))
                apart(pool, idle_pool, s_prep, at(n, 10, NP))
                link(TS(ss2[:, :, :], ss[:, :, :], 1.0 / D, RMS_EPS, ALU.mult, ALU.add))
                link(TT(rn[:, :, :], ss2[:, :, :], mh[:, :, :], ALU.pow))
                assert m[0] == NPP

        @block.vector
        def _(dve):
            nc.vector.memset(S[:, :, :, :], 0.0).then_inc(s_S, 1)
            TT, RED = nc.vector.tensor_tensor, nc.vector.tensor_reduce
            with dve.Fori(0, BLOCKS) as n:
                m = [0]

                def link(ins):
                    m[0] += 1
                    ins.then_inc(s_prep, 1)
                    dve.wait_ge(s_prep, at(n, m[0], NP))

                dve.wait_ge(s_aprep, at(n, 1, NA))
                link(RED(ss[:, :, :], inner(tmp), AX.X, ALU.add))
                dve.wait_ge(s_pprep, at(n, 2, NPP))
                link(TT(kn[:, :, :, :], kr[:, :, :, :], over_d(rn), ALU.mult))
                link(TT(kb[:, :, :, :], kn[:, :, :, :], over_d(br), ALU.mult))
                dve.wait_ge(s_aprep, at(n, 2, NA))
                link(RED(ss[:, :, :], inner(tmp), AX.X, ALU.add))
                dve.wait_ge(s_pprep, at(n, 5, NPP))
                link(TT(qn[:, :, :, :], qr[:, :, :, :], over_d(rn), ALU.mult))
                dve.wait_ge(s_pprep, at(n, 7, NPP))
                link(RED(dot[:, :, :], inner(tmp), AX.X, ALU.add))
                dve.wait_ge(s_st, at(n, 0, unit=16 * G, **CREDIT))
                link(nc.vector.memset(kS[:, :, :], 0.0))
                nc.vector.memset(kS[:, :, :], 0.0).then_inc(s_free, 1)
                with dve.Fori(0, TB) as t:
                    def col(a):
                        return a[:, :, :, bass.ds(t, 1)].rearrange("p g d o -> p g (o d)")

                    def wait_step(k):
                        dve.wait_ge(s_step, (n * TB + t) * 4 + k)

                    TT(pk[:, :, :, :], S[:, :, :, :], col(kb).unsqueeze(2).to_broadcast([P, G, D, D]),
                       ALU.mult).then_inc(s_step, 1)
                    wait_step(1)
                    RED(kS[:, :, :], pk[:, :, :, :], AX.X, ALU.add).then_inc(s_step, 1)
                    wait_step(2)
                    TT(col(ub), col(vb), kS[:, :, :], ALU.subtract).then_inc(s_step, 1)
                    wait_step(3)
                    TT(outer[:, :, :, :], col(ub).unsqueeze(3).to_broadcast([P, G, D, D]),
                       col(kn).unsqueeze(2).to_broadcast([P, G, D, D]), ALU.mult).then_inc(s_step, 1)
                    dve.wait_ge(s_pq, n * TB + t + 1)
                    RED(col(ob), pq[:, :, :, :], AX.X, ALU.add)
                    wait_step(4)
                    TT(S[:, :, :, :], S[:, :, :, :], outer[:, :, :, :], ALU.add).then_inc(s_S, 1)
                    dve.wait_ge(s_S, n * TB + t + 2)
                link(nc.vector.memset(kS[:, :, :], 0.0))
                dve.wait_ge(s_pprep, at(n, 8, NPP))
                link(TT(ob[:, :, :, :], ob[:, :, :, :], tmp[:, :, :, :], ALU.add))
                dve.wait_ge(s_aprep, at(n, 3, NA))
                link(RED(ss[:, :, :], inner(tmp), AX.X, ALU.add))
                dve.wait_ge(s_pprep, at(n, 10, NPP))
                TT(ob[:, :, :, :], ob[:, :, :, :], over_d(rn), ALU.mult).then_inc(s_o, 1)
                dve.wait_ge(s_o, at(n, 1))
                assert m[0] == NP


def back(nc, NB, ident_d, first_d, w1_o, norm_w, router, w_in, b_in, w_dn, b_dn, scratch, out):
    f32 = mybir.dt.float32
    ALU, ACT, AX = mybir.AluOpType, mybir.ActivationFunctionType, mybir.AxisListType
    with ExitStack() as ctx:
        sb = lambda n, s, t=f32: ctx.enter_context(nc.sbuf_tensor(n, s, t))
        ps = lambda n, s, t=f32: ctx.enter_context(nc.psum_tensor(n, s, t))
        sem = lambda n: ctx.enter_context(nc.semaphore(n))
        idle_pool, idle_dve = sb("m_idle_pool", [1, IDLE]), sb("m_idle_dve", [1, IDLE])
        ident = sb("m_ident", [P, P])
        first = sb("m_first", [P, E, E])
        wo = sb("m_wo", [P, CT, C])
        nw = sb("m_nw", [P, 1])
        wr = sb("m_wr", [P, CT, E])
        wi = sb("m_wi", [P, E, CT, C])
        bi = sb("m_bi", [P, E, CT])
        wd = sb("m_wd", [P, E, CT, C])
        bd = sb("m_bd", [E, C])
        mh = sb("m_mh", [P, NT])
        euler = sb("m_euler", [P, NT, E])

        oT = sb("m_oT", [P, CT, T])
        oTw = sb("m_oTw", [P, CT, T])
        h2 = sb("m_h2", [P, NT, C])
        h3 = sb("m_h3", [P, NT, C])
        stats = sb("m_stats", [P, NT, 6])
        mv = sb("m_mv", [P, NT, 2])
        vare = sb("m_vare", [P, NT])
        rstd = sb("m_rstd", [P, NT])
        xn = sb("m_xn", [P, NT, C])
        xT = sb("m_xT", [P, CT, T])
        lmax = sb("m_lmax", [P, NT])
        lsub = sb("m_lsub", [P, NT, E])
        pexp = sb("m_pexp", [P, NT, E])
        psum_ = sb("m_psum", [P, NT])
        prec = sb("m_prec", [P, NT])
        prob = sb("m_prob", [P, NT, E])
        gt = sb("m_gt", [P, NT, E, E])
        eq = sb("m_eq", [P, NT, E, E])
        rank = sb("m_rank", [P, NT, E])
        gate = sb("m_gate", [P, NT, E])
        gateT = sb("m_gateT", [E, T])
        hid = sb("m_hid", [P, 2, CT, T])
        acc = sb("m_acc", [P, NT, C])

        pA = ps("m_pA", [P, 512])
        pG = ps("m_pG", [P, 512])
        pH = [ps(f"m_pH{i}", [P, CT, T]) for i in range(2)]
        pY = [ps(f"m_pY{i}", [P, NT, C]) for i in range(2)]

        s_w = sem("m_weights")
        s_in = sem("m_loaded")
        s_init = sem("m_init")
        s_ow = sem("m_o_weighted")
        s_wo = sem("m_wo_in_psum")
        s_h3 = sem("m_h3_ready")
        s_stat = sem("m_ln_stats")
        s_rstd = sem("m_ln_rstd")
        s_ln = sem("m_ln_out")
        s_pool = sem("m_pool_step")
        s_xTp = sem("m_xT_in_psum")
        s_xT = sem("m_xT_ready")
        s_lg = sem("m_logits_in_psum")
        s_lsub = sem("m_logits_less_max")
        s_pexp = sem("m_exponentials")
        s_dve = sem("m_vector_step")
        s_gate = sem("m_gates")
        s_gTp = sem("m_gateT_in_psum")
        s_gT = sem("m_gateT_ready")
        s_bp = sem("m_bias_in_psum")
        s_hp = sem("m_hidden_in_psum")
        s_hid = sem("m_hidden_ready")
        s_yp = sem("m_y_in_psum")
        s_acc = sem("m_y_added")
        s_out = sem("m_out_ready")
        s_st = sem("m_out_stored")
        block = ctx.enter_context(nc.Block())
        loads = [(ident, ident_d), (first, first_d), (wo, w1_o.rearrange("(c p) n -> p c n", p=P)), (nw, norm_w),
                 (wr, router.rearrange("(c p) n -> p c n", p=P)),
                 (wi, w_in.rearrange("e (c p) n -> p (e c) n", p=P).rearrange("p (e c) n -> p e c n", c=CT)),
                 (bi, b_in.rearrange("e (c p) -> p e c", p=P)),
                 (wd, w_dn.rearrange("e (c p) n -> p (e c) n", p=P).rearrange("p (e c) n -> p e c n", c=CT)), (bd, b_dn)]
        NW = 16 * len(loads)

        @block.sync
        def _(sp):
            for sem_ in (s_h3, s_out, s_st):
                sp.sem_inc(sem_, 1)
            for tile, src in loads:
                with nc.allow_non_contiguous_dma(reason="biases, once"):
                    sp.dma_start(tile[tuple(slice(None) for _ in tile.shape)], src).then_inc(s_w, 16)
            with sp.Fori(0, NB) as b:
                sp.wait_ge(s_h3, at(b, 0, **CREDIT))
                sp.dma_start(oT[:, :, :], image(scratch["o"], b)).then_inc(s_in, 16)
                sp.dma_start(h2[:, :, :], image(scratch["h"], b)).then_inc(s_in, 16)
                sp.wait_ge(s_out, at(b, 1, **CREDIT))
                sp.dma_start(image(out, b), acc[:, :, :]).then_inc(s_st, 16)
            sp.wait_ge(s_st, 16 * NB + 1)

        @block.gpsimd
        def _(pool):
            nc.gpsimd.memset(mh[:, :], -0.5).then_inc(s_init, 1)
            nc.gpsimd.memset(euler[:, :, :], float(np.e)).then_inc(s_init, 1)
            nc.gpsimd.memset(idle_pool[:, :], 0.0).then_inc(s_init, 1)
            pool.wait_ge(s_init, 3)
            with pool.Fori(0, NB) as b:
                apart(pool, idle_pool, s_stat, at(b, 1))
                nc.gpsimd.tensor_scalar(vare[:, :], mv[:, :, 1], LN_EPS, None, ALU.add).then_inc(s_pool, 1)
                pool.wait_ge(s_pool, at(b, 1))
                nc.gpsimd.tensor_tensor(rstd[:, :], vare[:, :], mh[:, :], ALU.pow).then_inc(s_rstd, 1)
                pool.wait_ge(s_lsub, at(b, 1))
                nc.gpsimd.tensor_tensor(pexp[:, :, :], euler[:, :, :], lsub[:, :, :], ALU.pow).then_inc(s_pexp, 1)

        @block.vector
        def _(dve):
            TT, RED = nc.vector.tensor_tensor, nc.vector.tensor_reduce
            dve.wait_ge(s_w, NW)
            with dve.Fori(0, NB) as b:
                m = [0]
                PER = 7

                def link(ins, alone=False):
                    m[0] += 1
                    ins.then_inc(s_dve, 1)
                    if alone:
                        apart(dve, idle_dve, s_dve, at(b, m[0], PER))
                    else:
                        dve.wait_ge(s_dve, at(b, m[0], PER))

                dve.wait_ge(s_wo, at(b, 1))
                TT(h3[:, :, :].rearrange("p a c -> p (a c)"), pA[:, :], h2[:, :, :].rearrange("p a c -> p (a c)"),
                   ALU.add).then_inc(s_h3, 1)
                dve.wait_ge(s_h3, at(b, 1, **CREDIT))
                for t in range(NT):
                    last = nc.vector.bn_stats(stats[:, t, :], h3[:, t, :])
                link(last, alone=True)
                for t in range(NT):
                    last = nc.vector.bn_aggr(mv[:, t, :], stats[:, t, :])
                last.then_inc(s_stat, 1)
                dve.wait_ge(s_rstd, at(b, 1))
                for t in range(NT):
                    last = nc.vector.tensor_scalar(xn[:, t, :], h3[:, t, :], mv[:, t, 0:1], rstd[:, t:t + 1],
                                                   ALU.subtract, ALU.mult)
                last.then_inc(s_ln, 1)
                dve.wait_ge(s_lg, at(b, 1))
                lg = pG[:, 0:NT * E].rearrange("p (a e) -> p a e", a=NT)
                wide = [P, NT, E]
                link(RED(lmax[:, :], lg, AX.X, ALU.max))
                TT(lsub[:, :, :], lg, lmax[:, :].unsqueeze(2).to_broadcast(wide), ALU.subtract).then_inc(s_lsub, 1)
                dve.wait_ge(s_pexp, at(b, 1))
                link(RED(psum_[:, :], pexp[:, :, :], AX.X, ALU.add))
                link(nc.vector.reciprocal(prec[:, :], psum_[:, :]))
                link(TT(prob[:, :, :], pexp[:, :, :], prec[:, :].unsqueeze(2).to_broadcast(wide), ALU.mult))
                for t in range(NT):
                    mine = prob[:, t, :].unsqueeze(2).to_broadcast([P, E, E])
                    theirs = prob[:, t, :].unsqueeze(1).to_broadcast([P, E, E])
                    TT(gt[:, t, :, :], theirs, mine, ALU.is_gt)
                    last = TT(eq[:, t, :, :], theirs, mine, ALU.is_equal)
                link(last)
                for t in range(NT):
                    last = TT(eq[:, t, :, :], eq[:, t, :, :], first[:, :, :], ALU.mult)
                link(last)
                flat = lambda a: a[:, :, :, :].rearrange("p a e f -> p (a e f)")
                TT(flat(gt), flat(gt), flat(eq), ALU.add).then_inc(s_gate, 1)
                dve.wait_ge(s_gate, at(b, 1, 3))
                RED(rank[:, :, :].rearrange("p a e -> p (a e)"), gt[:, :, :, :].rearrange("p a e f -> p (a e) f"),
                    AX.X, ALU.add).then_inc(s_gate, 1)
                dve.wait_ge(s_gate, at(b, 2, 3))
                nc.vector.scalar_tensor_tensor(gate[:, :, :], rank[:, :, :], 2.0, prob[:, :, :], ALU.is_lt,
                                               ALU.mult).then_inc(s_gate, 1)
                dve.wait_ge(s_gate, at(b, 3, 3))
                dve.wait_ge(s_st, at(b, 0, unit=16, **CREDIT))
                for e in range(E):
                    dve.wait_ge(s_yp, at(b, e + 1, E))
                    if e:
                        dve.wait_ge(s_acc, at(b, e, E))
                    for t in range(NT):
                        last = nc.vector.scalar_tensor_tensor(acc[:, t, :], pY[e % 2][:, t, :], gate[:, t, e:e + 1],
                                                              (acc if e else h3)[:, t, :], ALU.mult, ALU.add)
                    last.then_inc(s_acc, 1)
                dve.wait_ge(s_acc, at(b, E, E))
                dve.wait_ge(s_bp, at(b, 1))
                TT(acc[:, :, :].rearrange("p a c -> p (a c)"), acc[:, :, :].rearrange("p a c -> p (a c)"), pA[:, :],
                   ALU.add).then_inc(s_out, 1)
                assert m[0] == PER, m[0]

        @block.scalar
        def _(sc):
            A = nc.scalar.activation
            sc.wait_ge(s_w, NW)
            with sc.Fori(0, NB) as b:
                sc.wait_ge(s_in, at(b, 1) * 32)
                A(oTw[:, :, :], oT[:, :, :], ACT.Copy, scale=nw[:, 0:1]).then_inc(s_ow, 1)
                sc.wait_ge(s_xTp, at(b, 1))
                A(xT[:, :, :].rearrange("p c t -> p (c t)"), pA[:, :], ACT.Copy).then_inc(s_xT, 1)
                for e in range(E):
                    sc.wait_ge(s_hp, at(b, e + 1, E))
                    if e >= 2:
                        sc.wait_ge(s_yp, at(b, e - 1, E))
                    for c in range(CT):
                        last = A(hid[:, e % 2, c, :], pH[e % 2][:, c, :], ACT.Gelu_apprx_tanh, bias=bi[:, e, c:c + 1])
                    last.then_inc(s_hid, 1)
                    if e == 1:
                        sc.wait_ge(s_gTp, at(b, 1))
                        A(gateT[:, :], pG[0:E, 0:T], ACT.Copy).then_inc(s_gT, 1)

        @block.tensor
        def _(pe):
            mm, tr = nc.tensor.matmul, nc.tensor.transpose
            pe.wait_ge(s_w, NW)
            with pe.Fori(0, NB) as b:
                pe.wait_ge(s_ow, at(b, 1))
                pe.wait_ge(s_out, at(b, 0, **CREDIT))
                for t in range(NT):
                    for c in range(CT):
                        last = mm(pA[:, t * C:(t + 1) * C], oTw[:, c, t * P:(t + 1) * P], wo[:, c, :],
                                  start=(c == 0), stop=(c == CT - 1))
                last.then_inc(s_wo, 1)
                pe.wait_ge(s_ln, at(b, 1))
                for i in range(CT):
                    for j in range(NT):
                        last = tr(pA[:, i * T + j * P:i * T + (j + 1) * P], xn[:, j, i * P:(i + 1) * P], ident[:, :])
                last.then_inc(s_xTp, 1)
                pe.wait_ge(s_xT, at(b, 1))
                for t in range(NT):
                    for c in range(CT):
                        last = mm(pG[:, t * E:(t + 1) * E], xT[:, c, t * P:(t + 1) * P], wr[:, c, :], start=(c == 0),
                                  stop=(c == CT - 1))
                last.then_inc(s_lg, 1)

                def up(e):
                    if e >= 2:
                        pe.wait_ge(s_hid, at(b, e - 1, E))
                    for f in range(CT):
                        for c in range(CT):
                            last = mm(pH[e % 2][:, f, :], wi[:, e, c, f * P:(f + 1) * P], xT[:, c, :],
                                      start=(c == 0), stop=(c == CT - 1))
                    last.then_inc(s_hp, 1)

                def down(e):
                    pe.wait_ge(s_hid, at(b, e + 1, E))
                    if e >= 2:
                        pe.wait_ge(s_acc, at(b, e - 1, E))
                    for t in range(NT):
                        for c in range(CT):
                            last = mm(pY[e % 2][:, t, :], hid[:, e % 2, c, t * P:(t + 1) * P], wd[:, e, c, :],
                                      start=(c == 0), stop=(c == CT - 1))
                    last.then_inc(s_yp, 1)

                up(0)
                for e in range(1, E + 1):
                    if e < E:
                        up(e)
                    if e == 2:
                        pe.wait_ge(s_gate, at(b, 3, 3))
                        for t in range(NT):
                            last = tr(pG[0:E, t * P:(t + 1) * P], gate[:, t, :], ident[:, :])
                        last.then_inc(s_gTp, 1)
                    down(e - 1)
                pe.wait_ge(s_gT, at(b, 1))
                for t in range(NT):
                    last = mm(pA[:, t * C:(t + 1) * C], gateT[:, t * P:(t + 1) * P], bd[:, :], start=True, stop=True)
                last.then_inc(s_bp, 1)


def kernel(**inputs):
    import numpy as _np
    import concourse.bacc as _bacc
    from concourse import mybir as _mybir
    from concourse.bass_utils import run_bass_kernel_spmd as _run

    a = {k: _np.asarray(v) for k, v in inputs.items()}
    rows = lambda v: _np.broadcast_to(v.reshape(1, -1), (P, v.size))
    tap = _np.zeros((3, XR, 3, TR), _np.float32)
    for c in range(3):
        for dy in range(3):
            for r in range(TR):
                tap[c, r + dy, dy, r] = GRAY[c]
    s, t = _np.arange(P)[:, None], _np.arange(P)[None, :]
    tri = (t >= s).astype(_np.float32)
    causal = _np.concatenate([tri, _np.ones((P, P), _np.float32), tri], 1)
    parity = _np.stack([(_np.arange(P) // D) % 2 == i for i in range(2)], 1).astype(_np.float32)
    first = _np.broadcast_to((_np.arange(E)[None, :] < _np.arange(E)[:, None]).astype(_np.float32), (P, E, E))
    laid = {
        "x": a["x"],
        "scharr": rows(a["L0_tok_scharr"]).reshape(P, 2, 3, 3),
        "taps": tap.reshape(KX, 3, TR),
        "ident": _np.eye(P, dtype=_np.float32),
        "causal": causal,
        "first": first,
        "parity": parity,
        "w_qkv": a["L0_attn_w_qkv"].T,
        "b_qkv": rows(a["L0_attn_b_qkv"]),
        "w_out": a["L0_attn_w_out"].T,
        "b_out": rows(a["L0_attn_b_out"]),
        "omega": a["L0_attn_omega"].transpose(1, 2, 0, 3).reshape(C, F),
        "nodes": _np.tile(_np.repeat(a["L0_attn_quad_nodes"], M), 2).reshape(P, 1),
        "weights": _np.tile(_np.repeat(a["L0_attn_quad_weights"], M), 2).reshape(P, 1),
        "ffn_w": a["L0_ffn_weight"].T,
        "ffn_b": rows(a["L0_ffn_bias"]),
        "w1_qkv": _np.concatenate([a["L1_attn_Wq"], a["L1_attn_Wk"], a["L1_attn_Wv"]], 0).T,
        "w1_b": a["L1_attn_Wb"].T,
        "w1_o": a["L1_attn_Wo"].T,
        "conv_w": _np.concatenate([a["L1_attn_conv_q"], a["L1_attn_conv_k"], a["L1_attn_conv_v"]], 0),
        "norm_w": _np.tile(a["L1_attn_o_norm_w"], P // D).reshape(P, 1),
        "router": a["L1_ffn_router_w"],
        "w_in": a["L1_ffn_w_in"],
        "b_in": a["L1_ffn_b_in"],
        "w_dn": a["L1_ffn_w_out"],
        "b_dn": a["L1_ffn_b_out"],
    }
    nc = _bacc.Bacc("TRN2", target_bir_lowering=False, num_devices=1)
    arrays, args = {}, {}
    for name, v in laid.items():
        v = _np.ascontiguousarray(v)
        arrays[f"in_{name}"] = v
        args[name] = nc.dram_tensor(f"in_{name}", v.shape, _mybir.dt.from_np(v.dtype), kind="ExternalInput").ap()
    shape = (a["x"].shape[0], T, C)
    args["out"] = nc.dram_tensor("out_0", shape, _mybir.dt.float32, kind="ExternalOutput").ap()
    tower(nc, **args)
    return _run(nc, [arrays], core_ids=[0]).results[0]["out_0"]
```

```python
import concourse.bass as bass
from concourse import mybir
from contextlib import ExitStack
import numpy as np

P = 128
T = 256
C = 256
NT = T // P
CT = C // P
H = 16
D = C // H
NODES, M = 2, 32
F = NODES * M
E = 8
TR = 37
XT = -(-T // TR)
XR = TR + 2
KX = 3 * XR
GRAY = (0.2989, 0.587, 0.114)
LANES = P // H
TB = 64
IDLE = 33
LN_EPS = 1e-5
RMS_EPS = 1e-6


def at(b, k, per=1, unit=1, credit=0):
    return b * (per * unit) + (k * unit + credit)


CREDIT = dict(credit=1)


class Cols:

    def __init__(self, start, size):
        self.start, self.size = start, size


def b_is(b, value):
    return isinstance(b, int) and b == value


def apart(eng, idle, sem, value, turn=[0]):
    eng.wait_ge(sem, value)
    turn[0] = turn[0] % (IDLE - 1) + 1
    if eng.engine == mybir.EngineType.Pool:
        eng.tensor_tensor(idle[:, turn[0]:turn[0] + 1], idle[:, 0:1], idle[:, 0:1], mybir.AluOpType.add)
    else:
        eng.memset(idle[:, turn[0]:turn[0] + 1], 0.0)


def image(ap, b):
    return ap[bass.ds(b, 1), :, :].rearrange("o (c p) t -> p (o c) t", p=P)


def tower(nc, x, scharr, taps, ident, causal, first, parity, place, w_qkv, b_qkv, w_out, b_out, omega, nodes, weights,
          ffn_w, ffn_b, w1_qkv, w1_b, w1_o, conv_w, norm_w, router, w_in, b_in, w_dn, b_dn, out):
    f32, bf16, f16, f8 = mybir.dt.float32, mybir.dt.bfloat16, mybir.dt.float16, mybir.dt.float8e4
    NB = x.shape[0]
    scratch = {n: nc.dram_tensor(f"scr_{n}", s, f32, kind="Internal").ap() for n, s in
               {"h": (NB, T, C), "q": (NB, C, T), "k": (NB, C, T), "v": (NB, C, T), "o": (NB, C, T),
                "beta": (NB, H, T)}.items()}
    front(nc, NB, x, scharr, taps, ident, causal, parity, place, w_qkv, b_qkv, w_out, b_out, omega, nodes, weights,
          ffn_w, ffn_b, w1_qkv, w1_b, conv_w, scratch)
    delta_rule(nc, NB, ident, scratch)
    back(nc, NB, ident, first, w1_o, norm_w, router, w_in, b_in, w_dn, b_dn, scratch, out)


def front(nc, NB, x, scharr, taps, ident_d, causal_d, parity_d, place_d, w_qkv, b_qkv, w_out, b_out, omega, nodes,
          weights, ffn_w, ffn_b, w1_qkv, w1_b, conv_w, scratch):
    f32, bf16, f16, f8 = mybir.dt.float32, mybir.dt.bfloat16, mybir.dt.float16, mybir.dt.float8e4
    ALU, ACT, AX = mybir.AluOpType, mybir.ActivationFunctionType, mybir.AxisListType
    LO, HI = float(np.exp(-20.0)), float(np.exp(20.0))
    PAIRS = -(-XT // 2)
    VW = 32
    NF = 8
    with ExitStack() as ctx:
        sb = lambda n, s, t=f32: ctx.enter_context(nc.sbuf_tensor(n, s, t))
        ps = lambda n, s, t=f32: ctx.enter_context(nc.psum_tensor(n, s, t))
        sem = lambda n: ctx.enter_context(nc.semaphore(n))

        idle_pool, idle_dve = sb("idle_pool", [1, IDLE]), sb("idle_dve", [1, IDLE])
        ident = sb("ident", [P, P])
        identb = sb("identb", [P, P], bf16)
        causal = sb("causal", [P, T + P])
        parity = sb("parity", [P, 2])
        place = sb("place", [2 * TR, 2 * P + TR])
        sch = sb("sch", [P, 2, 3, 3])
        tap = sb("tap", [KX, 3, TR])
        band = sb("band", [KX, 3, 2, TR])
        wqkv = sb("wqkv", [P, CT, 3 * C])
        bqkv = sb("bqkv", [P, 3 * C])
        wout = sb("wout", [P, CT, C])
        bout = sb("bout", [P, C])
        om = sb("om", [P, CT, F])
        omblk = sb("omblk", [P, CT, 2, F])
        fw = sb("fw", [P, CT, C])
        fw8 = sb("fw8", [P, CT, C], f8)
        fwq = sb("fwq", [P, CT, C], bf16)
        fb = sb("fb", [P, C])
        w1 = sb("w1", [P, CT, 3 * C])
        w1b = sb("w1b", [P, CT, H])
        cw = sb("cw", [P, 6, 4])
        cwh = sb("cwh", [P, 6, 4])
        node = sb("node", [P, 1])
        nneg = sb("nneg", [P, 1])
        n2p = sb("n2p", [P, 1])
        root2s = sb("root2s", [P, 1])
        wgt = sb("wgt", [P, 1])
        wpos = sb("wpos", [P, 1])
        wroot = sb("wroot", [P, 1])
        sqscale = sb("sqscale", [P, 1])
        half = sb("half", [P, 1])
        quarter = sb("quarter", [P, 1])
        minus_half = sb("minus_half", [P, NT * 2 * H])

        xin = sb("xin", [P, XT, C + 2])
        edges = sb("edges", [2 * TR, XT, C])
        h0 = sb("h0", [P, NT, C])
        h0b = sb("h0b", [P, NB * NT, C])
        stats = sb("stats", [P, NT, 6])
        mv = sb("mv", [P, NT, 2])
        vare = sb("vare", [P, NT])
        rstd = sb("rstd", [P, NT])
        xn1 = sb("xn1", [P, NT, C])
        xT1 = sb("xT1", [P, CT, T])
        xn3 = sb("xn3", [P, NT, C])
        xT3 = sb("xT3", [P, CT, T])
        qk = sb("qk", [P, NT, 2 * C])
        qksq = sb("qksq", [P, NT, 2 * C])
        vv = sb("vv", [P, NT, H, VW])
        ctxT = sb("ctxT", [P, 2, T])
        qkss = sb("qkss", [P, NT * 2 * H])
        qkss2 = sb("qkss2", [P, NT * 2 * H])
        qkr = sb("qkr", [P, NT * 2 * H])
        qkn = sb("qkn", [P, NT, 2 * C])
        qkT = sb("qkT", [P, 4, T])
        fsq = sb("fsq", [P, 2, 2, T])
        fexp = sb("fexp", [P, 2, 2, T])
        feats = sb("feats", [P, 2, 8, T])
        att = sb("att", [P, 2, T + P])
        den = sb("den", [P, NT, 8])
        rden = sb("rden", [P, NT, 8])
        on = sb("on", [P, NT, H, D])
        onT = sb("onT", [P, CT, T])
        h1 = sb("h1", [P, NT, C])
        h1b = sb("h1b", [P, NT, C])
        x8 = sb("x8", [P, NT, C], f8)
        x8b = sb("x8b", [P, NT, C], bf16)
        x8T = sb("x8T", [P, CT, T], bf16)
        y16 = sb("y16", [P, NT, C], f16)
        h2 = sb("h2", [P, NT, C])
        raw = sb("raw", [P, 6, T + 3])
        yc = sb("yc", [P, 6, T])
        th = sb("th", [P, 6, T])
        act = sb("act", [P, 6, T])
        thb = sb("thb", [H, T])
        beta = sb("beta", [H, T])

        fwa, fwb, fwm = xn1, xn3, h0
        pf = ps("pf", [P, 2, 512])
        pe_ = [ps(f"pfeat{i}", [P, 2, T]) for i in range(2)]
        psc = [ps(f"pscore{i}", [P, 512]) for i in range(2)]
        ppv = ps("ppv", [P, 2, T])
        ptr = ps("ptr", [P, 512])

        s_w = sem("weights_loaded")
        s_set = sem("setup_step")
        s_band = sem("band_ready")
        s_setp = sem("pool_setup_step")
        s_x = sem("x_loaded")
        s_filt = sem("filters_in_psum")
        s_edges = sem("edges_abs")
        s_hT = sem("h0_in_psum")
        s_h0 = sem("h0_ready")
        s_stat1 = sem("ln1_stats")
        s_stat2 = sem("ln2_stats")
        s_stat3 = sem("ln3_stats")
        s_var1 = sem("ln1_variance")
        s_var2 = sem("ln2_variance")
        s_var3 = sem("ln3_variance")
        s_qkmax = sem("qk_sums_guarded")
        s_rstd1 = sem("ln1_rstd")
        s_rstd2 = sem("ln2_rstd")
        s_rstd3 = sem("ln3_rstd")
        s_xn1 = sem("xn1_ready")
        s_x8 = sem("x8_ready")
        s_xn3 = sem("xn3_ready")
        s_bn1 = sem("ln1_partial_stats")
        s_bn2 = sem("ln2_partial_stats")
        s_bn3 = sem("ln3_partial_stats")
        s_clip = sem("exponentials_clipped")
        s_den = sem("denominators")
        s_tap = sem("short_conv_taps")
        s_xT1p = sem("xT1_in_psum")
        s_xT1 = sem("xT1_ready")
        s_xT3p = sem("xT3_in_psum")
        s_xT3 = sem("xT3_ready")
        s_qkp = sem("qk_in_psum")
        s_vp = sem("v_in_psum")
        s_qk = sem("qk_ready")
        s_v = sem("v_ready")
        s_qksq = sem("qk_squared")
        s_qkss = sem("qk_sums")
        s_qkr = sem("qk_rnorm")
        s_qkn = sem("qk_normed")
        s_qkTp = sem("qkT_in_psum")
        s_qkT = sem("qkT_ready")
        s_fp = sem("proj_in_psum")
        s_fe = sem("feature_parts")
        s_f = sem("features_ready")
        s_sc = sem("scores_in_psum")
        s_att = sem("att_masked")
        s_pv = sem("pv_done")
        s_ctx = sem("weighted_values_copied")
        s_ctxp = sem("weighted_values_turned")
        s_on = sem("out_normed")
        s_onTp = sem("onT_in_psum")
        s_onT = sem("onT_ready")
        s_op = sem("proj_out_in_psum")
        s_h0b = sem("h0_plus_bias")
        s_h1 = sem("h1_ready")
        s_h1b = sem("h1_plus_bias")
        s_x8b = sem("x8_as_bf16")
        s_x8Tp = sem("x8T_in_psum")
        s_x8T = sem("x8T_ready")
        s_yp = sem("ffn_in_psum")
        s_y16 = sem("ffn_as_f16")
        s_h2 = sem("h2_ready")
        s_h2st = sem("h2_stored")
        s_l1p = sem("l1_in_psum")
        s_raw = sem("l1_raw")
        s_yc = sem("short_conv")
        s_th = sem("tanh_done")
        s_act = sem("l1_silu")
        s_bp = sem("beta_in_psum")
        s_thb = sem("beta_tanh")
        s_beta = sem("beta_ready")
        s_st = sem("l1_stored")
        s_bst = sem("beta_stored")
        block = ctx.enter_context(nc.Block())

        loads = [(ident, ident_d), (causal, causal_d), (parity, parity_d), (place, place_d), (sch, scharr), (tap, taps),
                 (wqkv, w_qkv.rearrange("(c p) n -> p c n", p=P)), (bqkv, b_qkv),
                 (wout, w_out.rearrange("(c p) n -> p c n", p=P)), (bout, b_out),
                 (om, omega.rearrange("(c p) n -> p c n", p=P)),
                 (fw, ffn_w.rearrange("(c p) n -> p c n", p=P)), (fb, ffn_b),
                 (w1, w1_qkv.rearrange("(c p) n -> p c n", p=P)), (w1b, w1_b.rearrange("(c p) n -> p c n", p=P)),
                 (cw, conv_w.rearrange("(c p) k -> p c k", p=P)), (node, nodes), (wgt, weights)]
        NW = 16 * len(loads)
        NX = 16 * 9

        def rounds(engine, body, stages_of=lambda b: (b + 1 < NB, 0 <= b < NB, 0 < b <= NB, 1 < b)):
            for b in (-1, 0, 1):
                body(b, *stages_of(b))
            with engine.Fori(2, NB - 2) as b:
                body(b, True, True, True, True)
            for b in (NB - 2, NB - 1, NB, NB + 1):
                body(b, *stages_of(b))

        @block.sync
        def _(sp):
            for sem_ in (s_h2st, s_thb, s_raw, s_bst, s_st):
                sp.sem_inc(sem_, 1)
            for tile, src in loads:
                sp.dma_start(tile[tuple(slice(None) for _ in tile.shape)], src).then_inc(s_w, 16)
            sp.wait_ge(s_set, 1)

            def load(n):
                for c in range(3):
                    img = x[bass.ds(n, 1), c, :, :].rearrange("o r w -> (o r) w")
                    sp.dma_start(xin[c * XR + 1:(c + 1) * XR, 0, 1:C + 1], img[0:XR - 1, :]).then_inc(s_x, 16)
                    mid = bass.AP(tensor=img.tensor, offset=img.offset + (TR - 1) * C,
                                  ap=[[C, XR], [TR * C, XT - 2], [1, C]])
                    sp.dma_start(xin[c * XR:(c + 1) * XR, 1:XT - 1, 1:C + 1], mid).then_inc(s_x, 16)
                    r0 = (XT - 1) * TR - 1
                    sp.dma_start(xin[c * XR:c * XR + T - r0, XT - 1, 1:C + 1], img[r0:T, :]).then_inc(s_x, 16)

            load(0)

            def body(b, a, v, c, d):
                n, p, e = b + 1, b - 1, b - 2
                if v or a:
                    if a and not (isinstance(b, int) and n + 1 >= NB):
                        sp.wait_ge(s_filt, at(n, PAIRS, PAIRS))
                        load(n + 1)
                if d:
                    sp.wait_ge(s_act, at(e, 1))
                    for i, name in enumerate("qkv"):
                        sp.dma_start(image(scratch[name], e), act[:, 2 * i:2 * i + 2, :]).then_inc(s_st, 16)
                if c:
                    sp.wait_ge(s_h2, at(p, 1))
                    sp.dma_start(image(scratch["h"], p), h2[:, :, :]).then_inc(s_h2st, 16)
                    sp.wait_ge(s_beta, at(p, 1))
                    sp.dma_start(scratch["beta"][bass.ds(p, 1), :, :].rearrange("o h t -> (o h) t"),
                                 beta[:, :]).then_inc(s_bst, 16)

            rounds(sp, body)
            sp.wait_ge(s_h2st, 16 * NB + 1)
            sp.wait_ge(s_bst, 16 * NB + 1)
            sp.wait_ge(s_st, 48 * NB + 1)

        @block.gpsimd
        def _(pool):
            n = [0]

            def step(ins):
                n[0] += 1
                ins.then_inc(s_setp, 1)
                pool.wait_ge(s_setp, n[0])

            step(nc.gpsimd.memset(idle_pool[:, :], 0.0))
            step(nc.gpsimd.memset(half[:, :], 0.5))
            step(nc.gpsimd.memset(quarter[:, :], 0.25))
            step(nc.gpsimd.memset(minus_half[:, :], -0.5))
            pool.wait_ge(s_w, NW)
            step(nc.gpsimd.tensor_scalar(n2p[:, :], node[:, :], 0.0, 2.0, ALU.max, ALU.mult))
            step(nc.gpsimd.tensor_tensor(root2s[:, :], n2p[:, :], half[:, :], ALU.pow))
            step(nc.gpsimd.tensor_scalar(nneg[:, :], node[:, :], -1.0, None, ALU.mult))
            step(nc.gpsimd.tensor_scalar(wpos[:, :], wgt[:, :], 0.0, None, ALU.max))
            step(nc.gpsimd.tensor_tensor(wroot[:, :], wpos[:, :], quarter[:, :], ALU.pow))
            step(nc.gpsimd.tensor_scalar(sqscale[:, :], wroot[:, :], float(M ** -0.5), None, ALU.mult))

            def body(b, a, v, c, d):
                n, p, e = b + 1, b - 1, b - 2

                def rsqrt_ln(i, s_stat, s_var, s_rstd):
                    apart(pool, idle_pool, s_stat, at(i, 1))
                    nc.gpsimd.tensor_scalar(vare[:, :], mv[:, :, 1], LN_EPS, None, ALU.add).then_inc(s_var, 1)
                    pool.wait_ge(s_var, at(i, 1))
                    nc.gpsimd.tensor_tensor(rstd[:, :], vare[:, :], minus_half[:, 0:NT], ALU.pow).then_inc(s_rstd, 1)

                if a:
                    rsqrt_ln(n, s_stat1, s_var1, s_rstd1)
                    nc.gpsimd.tensor_tensor(h0b[:, bass.ds(n * NT, NT), :], h0[:, :, :],
                                            bout[:, :].unsqueeze(1).to_broadcast([P, NT, C]),
                                            ALU.add).then_inc(s_h0b, 1)
                if c:
                    rsqrt_ln(p, s_stat2, s_var2, s_rstd2)
                    nc.gpsimd.tensor_tensor(h1b[:, :, :], h1[:, :, :], fb[:, :].unsqueeze(1).to_broadcast([P, NT, C]),
                                            ALU.add).then_inc(s_h1b, 1)
                if c:
                    rsqrt_ln(p, s_stat3, s_var3, s_rstd3)
                if a:
                    apart(pool, idle_pool, s_qkss, at(n, 1))
                    nc.gpsimd.tensor_scalar(qkss2[:, :], qkss[:, :], 1e-24, None, ALU.max).then_inc(s_qkmax, 1)
                    pool.wait_ge(s_qkmax, at(n, 1))
                    nc.gpsimd.tensor_tensor(qkr[:, :], qkss2[:, :], minus_half[:, :], ALU.pow).then_inc(s_qkr, 1)

            rounds(pool, body)

        @block.vector
        def _(dve):
            n = [0]

            def step(ins):
                n[0] += 1
                ins.then_inc(s_set, 1)
                dve.wait_ge(s_set, n[0])

            step(nc.vector.memset(xin[:, :, :], 0.0))
            step(nc.vector.memset(raw[:, :, 0:3], 0.0))
            step(nc.vector.memset(vv[:, :, :, D:VW], 1.0))
            dve.wait_ge(s_w, NW)
            step(nc.vector.tensor_copy(identb[:, :], ident[:, :]))
            step(nc.vector.tensor_scalar(cwh[:, :, :], cw[:, :, :], 0.5, None, ALU.mult))
            for a in range(2):
                step(nc.vector.tensor_scalar(omblk[:, :, a, :], om[:, :, :], parity[:, a:a + 1], None, ALU.mult))
            for dx in range(3):
                for f in range(2):
                    step(nc.vector.tensor_scalar(band[:, dx, f, :], tap[:, 0, :], sch[0:KX, f, 0, dx:dx + 1], None,
                                                 ALU.mult))
                    for dy in (1, 2):
                        step(nc.vector.scalar_tensor_tensor(band[:, dx, f, :], tap[:, dy, :],
                                                            sch[0:KX, f, dy, dx:dx + 1], band[:, dx, f, :],
                                                            ALU.mult, ALU.add))
            step(nc.vector.tensor_scalar(fw8[:, :, :], fw[:, :, :], 240.0, -240.0, ALU.min, ALU.max, saturate=False))
            step(nc.vector.tensor_copy(fwa[:, :, :], fw8[:, :, :]))
            step(nc.vector.tensor_scalar(fwb[:, :, :], fw[:, :, :], 448.0, -448.0, ALU.min, ALU.max))
            step(nc.vector.tensor_scalar(fw8[:, :, :], fwb[:, :, :], 0.5, None, ALU.mult, saturate=False))
            step(nc.vector.tensor_copy(fwb[:, :, :], fw8[:, :, :]))
            step(nc.vector.scalar_tensor_tensor(fwb[:, :, :], fwb[:, :, :], 2.0, fwa[:, :, :], ALU.mult, ALU.subtract))
            step(nc.vector.tensor_tensor(fwm[:, :, :], fw[:, :, :], fw[:, :, :], ALU.mult))
            step(nc.vector.tensor_scalar(fwm[:, :, :], fwm[:, :, :], 128.0 * 128.0, None, ALU.is_ge))
            step(nc.vector.tensor_tensor(fwb[:, :, :], fwb[:, :, :], fwm[:, :, :], ALU.mult))
            nc.vector.tensor_tensor(fwq[:, :, :], fwa[:, :, :], fwb[:, :, :], ALU.add).then_inc(s_band, 1)

            def body(b, a, v, c, d):
                n, p, e = b + 1, b - 1, b - 2

                def ln_stats(h, i, s_h, s_bn, s_stat):
                    dve.wait_ge(s_h, at(i, 1))
                    for t in range(NT):
                        last = nc.vector.bn_stats(stats[:, t, :], h[:, t, :])
                    last.then_inc(s_bn, 1)
                    apart(dve, idle_dve, s_bn, at(i, 1))
                    for t in range(NT):
                        last = nc.vector.bn_aggr(mv[:, t, :], stats[:, t, :])
                    last.then_inc(s_stat, 1)

                def ln_apply(h, out, i, s_rstd, s_out, **kinds):
                    apart(dve, idle_dve, s_rstd, at(i, 1))
                    for t in range(NT):
                        last = nc.vector.tensor_scalar(out[:, t, :], h[:, t, :], mv[:, t, 0:1], rstd[:, t:t + 1],
                                                       ALU.subtract, ALU.mult, **kinds)
                    last.then_inc(s_out, 1)

                def values():
                    dve.wait_ge(s_vp, at(b, 1))
                    for t in range(NT):
                        last = nc.vector.tensor_tensor(vv[:, t, :, 0:D],
                                                       ptr[:, t * C:(t + 1) * C].rearrange("p (h d) -> p h d", h=H),
                                                       bqkv[:, 2 * C:3 * C].rearrange("p (h d) -> p h d", h=H), ALU.add)
                    last.then_inc(s_v, 1)

                def feature(i):
                    dve.wait_ge(s_fe, at(b, i + 1, NF))
                    nc.vector.tensor_scalar(fexp[:, i % 2, :, :], fexp[:, i % 2, :, :], LO, HI, ALU.max,
                                            ALU.min).then_inc(s_clip, 1)
                    dve.wait_ge(s_clip, at(b, i + 1, NF))
                    nc.vector.tensor_tensor(feats[:, i // 4, i % 4:i % 4 + 5:4, :], fsq[:, i % 2, :, :],
                                            fexp[:, i % 2, :, :], ALU.mult).then_inc(s_f, 1)

                def mask(h):
                    dve.wait_ge(s_sc, at(b, h + 1, H))
                    if h >= 2:
                        dve.wait_ge(s_pv, at(b, h - 1, H))
                    nc.vector.tensor_tensor(att[:, h % 2, :], psc[h % 2][:, 0:T + P], causal[:, :],
                                            ALU.mult).then_inc(s_att, 1)

                def divide(g, i):
                    turned = (pe_[0], ppv)[g][:, :, :].rearrange("p t (h e) -> p t h e", e=VW)
                    dve.wait_ge(s_ctxp, at(i, g + 1, 2))
                    nc.vector.tensor_scalar(den[:, :, :], turned[:, :, :, D], 1e-6, None, ALU.max).then_inc(s_den, 1)
                    dve.wait_ge(s_den, at(i, 2 * g + 1, 4))
                    nc.vector.reciprocal(rden[:, :, :], den[:, :, :]).then_inc(s_den, 1)
                    dve.wait_ge(s_den, at(i, 2 * g + 2, 4))
                    for t in range(NT):
                        last = nc.vector.tensor_tensor(on[:, t, 8 * g:8 * g + 8, :], turned[:, t, :, 0:D],
                                                       rden[:, t, :].unsqueeze(2).to_broadcast([P, 8, D]), ALU.mult)
                    last.then_inc(s_on, 1)

                def h0_stats():
                    dve.wait_ge(s_hT, at(n, 1))
                    nc.vector.tensor_copy(h0[:, :, :].rearrange("p a c -> p (a c)"), ptr[:, :]).then_inc(s_h0, 1)
                    ln_stats(h0, n, s_h0, s_bn1, s_stat1)

                def qk_bias():
                    dve.wait_ge(s_qkp, at(n, 1))
                    nc.vector.tensor_tensor(qk[:, :, :], pf[:, :, :],
                                            bqkv[:, 0:2 * C].unsqueeze(1).to_broadcast([P, NT, 2 * C]),
                                            ALU.add).then_inc(s_qk, 1)

                def qk_sums():
                    dve.wait_ge(s_qksq, at(n, 1))
                    nc.vector.tensor_reduce(qkss[:, :], qksq[:, :, :].rearrange("p a (h d) -> p (a h) d", d=D), AX.X,
                                            ALU.add).then_inc(s_qkss, 1)

                def qk_norm():
                    dve.wait_ge(s_qkr, at(n, 1))
                    nc.vector.tensor_tensor(qkn[:, :, :].rearrange("p a (h d) -> p (a h) d", d=D),
                                            qk[:, :, :].rearrange("p a (h d) -> p (a h) d", d=D),
                                            qkr[:, :].unsqueeze(2).to_broadcast([P, NT * 2 * H, D]),
                                            ALU.mult).then_inc(s_qkn, 1)

                def h1_stats():
                    dve.wait_ge(s_op, at(p, 1))
                    dve.wait_ge(s_h0b, at(p, 1))
                    nc.vector.tensor_tensor(h1[:, :, :], ptr[:, :].rearrange("p (a c) -> p a c", a=NT),
                                            h0b[:, bass.ds(p * NT, NT), :], ALU.add).then_inc(s_h1, 1)
                    ln_stats(h1, p, s_h1, s_bn2, s_stat2)

                def h2_stats():
                    dve.wait_ge(s_y16, at(p, 1))
                    dve.wait_ge(s_h1b, at(p, 1))
                    dve.wait_ge(s_h2st, at(p, 0, unit=16, **CREDIT))
                    nc.vector.tensor_tensor(h2[:, :, :], y16[:, :, :], h1b[:, :, :], ALU.add).then_inc(s_h2, 1)
                    ln_stats(h2, p, s_h2, s_bn3, s_stat3)

                def short_conv(k):
                    if k == 3:
                        dve.wait_ge(s_raw, at(e, 3, 3, **CREDIT))
                        for o in range(6):
                            last = nc.vector.tensor_scalar(yc[:, o, :], raw[:, o, 3:T + 3], cwh[:, o, 3:4], None,
                                                           ALU.mult)
                        last.then_inc(s_tap, 1)
                        return
                    dve.wait_ge(s_tap, at(e, k + 1, 3))
                    for o in range(6):
                        last = nc.vector.scalar_tensor_tensor(yc[:, o, :], raw[:, o, k:k + T], cwh[:, o, k:k + 1],
                                                              yc[:, o, :], ALU.mult, ALU.add)
                    last.then_inc(s_yc if k == 2 else s_tap, 1)

                def beta_out():
                    dve.wait_ge(s_thb, at(p, 1, **CREDIT))
                    dve.wait_ge(s_bst, at(p, 0, unit=16, **CREDIT))
                    nc.vector.tensor_scalar(beta[:, :], thb[:, :], 0.5, 0.5, ALU.mult, ALU.add).then_inc(s_beta, 1)

                def silu():
                    dve.wait_ge(s_th, at(e, 1))
                    dve.wait_ge(s_st, at(e, 0, unit=48, **CREDIT))
                    nc.vector.scalar_tensor_tensor(act[:, :, :], th[:, :, :], 1.0, yc[:, :, :], ALU.add,
                                                   ALU.mult).then_inc(s_act, 1)

                if v:
                    values()
                    feature(0)
                    feature(1)
                if c:
                    divide(1, p)
                if d:
                    for k in (3, 0, 1, 2):
                        short_conv(k)
                if v:
                    feature(2)
                if d:
                    silu()
                if v:
                    feature(3)
                if a:
                    h0_stats()
                if v:
                    feature(4)
                if a:
                    ln_apply(h0, xn1, n, s_rstd1, s_xn1)
                if c:
                    h1_stats()
                if v:
                    feature(5)
                if c:
                    ln_apply(h1, x8, p, s_rstd2, s_x8, saturate=False)
                    apart(dve, idle_dve, s_x8, at(p, 1))
                    nc.vector.tensor_copy(x8b[:, :, :], x8[:, :, :]).then_inc(s_x8b, 1)
                if a:
                    qk_bias()
                if v:
                    feature(6)
                    mask(0)
                    feature(7)
                    mask(1)
                if c:
                    h2_stats()
                if v:
                    mask(2)
                    mask(3)
                if c:
                    ln_apply(h2, xn3, p, s_rstd3, s_xn3)
                if v:
                    mask(4)
                if a:
                    qk_sums()
                if v:
                    for h in range(5, 9):
                        mask(h)
                if a:
                    qk_norm()
                if v:
                    mask(9)
                    mask(10)
                    divide(0, b)
                    mask(11)
                    mask(12)
                if c:
                    beta_out()
                if v:
                    mask(13)
                    mask(14)
                    mask(15)

            rounds(dve, body)

        @block.scalar
        def _(sc):
            A = nc.scalar.activation
            sc.wait_ge(s_setp, 10)

            def body(b, a, v, c, d):
                n, p, e = b + 1, b - 1, b - 2

                def feature(i):
                    sc.wait_ge(s_fp, at(b, i + 1, NF))
                    if i >= 2:
                        sc.wait_ge(s_f, at(b, i - 1, NF))
                    A(fsq[:, i % 2, :, :], pe_[i % 2][:, :, :], ACT.Square, scale=sqscale[:, 0:1])
                    A(fexp[:, i % 2, :, :], pe_[i % 2][:, :, :], ACT.Exp, bias=nneg[:, 0:1],
                      scale=root2s[:, 0:1]).then_inc(s_fe, 1)

                if v:
                    feature(0)
                    feature(1)
                if a:
                    for k in range(PAIRS):
                        tiles = min(2, XT - 2 * k)
                        sc.wait_ge(s_filt, at(n, k + 1, PAIRS))
                        A(edges[:, 2 * k:2 * k + tiles, :], pf[0:2 * TR, k % 2, 0:tiles * C].rearrange(
                            "p (a w) -> p a w", a=tiles), ACT.Abs, scale=0.5).then_inc(s_edges, 1)
                if v:
                    feature(2)
                if c:
                    sc.wait_ge(s_onTp, at(p, 1))
                    A(onT[:, :, :].rearrange("p c t -> p (c t)"), ptr[:, :], ACT.Copy).then_inc(s_onT, 1)
                if d:
                    sc.wait_ge(s_yc, at(e, 1))
                    A(th[:, :, :], yc[:, :, :], ACT.Tanh).then_inc(s_th, 1)
                if v:
                    for i in (3, 4, 5):
                        feature(i)
                if a:
                    sc.wait_ge(s_xT1p, at(n, 1))
                    A(xT1[:, :, :].rearrange("p c t -> p (c t)"), ptr[:, :], ACT.Copy).then_inc(s_xT1, 1)
                if v:
                    feature(6)
                if c:
                    sc.wait_ge(s_x8Tp, at(p, 1))
                    A(x8T[:, :, :].rearrange("p c t -> p (c t)"), ptr[:, 0:T].bitcast(bf16),
                      ACT.Copy).then_inc(s_x8T, 1)
                if v:
                    feature(7)
                if c:
                    sc.wait_ge(s_yp, at(p, 1))
                    A(y16[:, :, :].rearrange("p c t -> p (c t)"), ptr[:, :], ACT.Copy).then_inc(s_y16, 1)
                if a:
                    sc.wait_ge(s_qk, at(n, 1))
                    A(qksq[:, :, :], qk[:, :, :], ACT.Square).then_inc(s_qksq, 1)
                if c:
                    sc.wait_ge(s_xT3p, at(p, 1))
                    A(xT3[:, :, :].rearrange("p c t -> p (c t)"), ptr[:, :], ACT.Copy).then_inc(s_xT3, 1)
                    for r in range(3):
                        sc.wait_ge(s_l1p, at(p, r + 1, 3))
                        if r == 0 and d:
                            sc.wait_ge(s_yc, at(e, 1))
                        A(raw[:, 2 * r:2 * r + 2, 3:T + 3], pf[:, r % 2, :].rearrange("p (o t) -> p o t", o=2),
                          ACT.Copy).then_inc(s_raw, 1)
                    sc.wait_ge(s_bp, at(p, 1))
                    A(thb[:, :], ptr[0:H, 0:T], ACT.Tanh, scale=0.5).then_inc(s_thb, 1)
                def copy_ctx(g):
                    sc.wait_ge(s_pv, at(b, 8 * (g + 1), H))
                    A(ctxT[:, :, :], ppv[:, :, :], ACT.Copy).then_inc(s_ctx, 1)

                if v:
                    copy_ctx(0)
                if a:
                    sc.wait_ge(s_qkTp, at(n, 1))
                    for i in range(2):
                        last = A(qkT[:, 2 * i:2 * i + 2, :], pe_[i][:, :, :], ACT.Copy)
                    last.then_inc(s_qkT, 1)
                if v:
                    copy_ctx(1)

            rounds(sc, body)

        @block.tensor
        def _(pe):
            mm, tr = nc.tensor.matmul, nc.tensor.transpose
            pe.wait_ge(s_band, 1)

            def body(b, a, v, c, d):
                n, p, e = b + 1, b - 1, b - 2

                def turn(src, dst, ident_):
                    for i in range(2):
                        for j in range(2):
                            last = tr(dst[:, i * T + j * P:i * T + (j + 1) * P], src[:, j, i * P:(i + 1) * P], ident_)
                    return last

                def project(dst, lhs, w, cols):
                    for t in range(NT):
                        for k in range(CT):
                            last = mm(dst[:, t * cols.size:(t + 1) * cols.size], lhs[:, k, t * P:(t + 1) * P],
                                      w[:, k, cols.start:cols.start + cols.size], start=(k == 0), stop=(k == CT - 1))
                    return last

                def conv():
                    pe.wait_ge(s_x, at(n, 1, unit=NX))
                    if not isinstance(b, int) or n >= 1:
                        pe.wait_ge(s_qk, at(n - 1, 1))
                    if not isinstance(b, int) or n >= 2:
                        pe.wait_ge(s_raw, at(n - 2, 0, 3, **CREDIT))
                    for k in range(PAIRS):
                        tiles = min(2, XT - 2 * k)
                        if k >= 2:
                            pe.wait_ge(s_edges, at(n, k - 1, PAIRS))
                        for dx in range(3):
                            last = mm(pf[0:2 * TR, k % 2, 0:tiles * C].rearrange("p (a w) -> p a w", a=tiles),
                                      band[:, dx, :, :].rearrange("p f r -> p (f r)"),
                                      xin[0:KX, 2 * k:2 * k + tiles, dx:dx + C], start=(dx == 0), stop=(dx == 2))
                        last.then_inc(s_filt, 1)

                def edge_sums():
                    for i in range(NT):
                        over = [j for j in range(XT) if j * TR < (i + 1) * P and min((j + 1) * TR, T) > i * P]
                        for j in over:
                            start = P - (j * TR - i * P)
                            last = mm(ptr[:, i * C:(i + 1) * C], place[:, start:start + P], edges[:, j, :],
                                      start=(j == over[0]), stop=(j == over[-1]))
                    return last

                def feature(i):
                    if i == 0:
                        pe.wait_ge(s_qkT, at(b, 1))
                    if i >= 2:
                        pe.wait_ge(s_fe, at(b, i - 1, NF))
                    rows = slice(32 * (i % 4), 32 * (i % 4) + 32)
                    for k in range(CT):
                        last = mm(pe_[i % 2][:, k, :], omblk[rows, k, :, :], qkT[rows, 2 * (i // 4) + k, :],
                                  start=True, stop=True)
                    last.then_inc(s_fp, 1)

                def score(h):
                    if h % 2 == 0 and h // 2 < 4:
                        pe.wait_ge(s_f, at(b, 5 + h // 2, NF))
                    if h >= 2:
                        pe.wait_ge(s_att, at(b, h - 1, H))
                    rows = slice(F * (h % 2), F * (h % 2) + F)
                    q, k = feats[rows, 0, h // 2, :], feats[rows, 1, h // 2, :]
                    mm(psc[h % 2][:, 0:T], k[:, 0:P], q, start=True, stop=True)
                    mm(psc[h % 2][:, T:T + P], k[:, P:T], q[:, P:T], start=True, stop=True).then_inc(s_sc, 1)

                def value(h):
                    pe.wait_ge(s_att, at(b, h + 1, H))
                    if h == 8:
                        pe.wait_ge(s_ctx, at(b, 1, 2))
                    w, dst = att[:, h % 2, :], ppv[VW * (h % 4):VW * (h % 4) + VW, h // 4 % 2, :]
                    mm(dst[:, 0:P], vv[:, 0, h, :], w[:, 0:P], start=True, stop=True)
                    mm(dst[:, P:T], vv[:, 0, h, :], w[:, P:T], start=True, stop=False)
                    mm(dst[:, P:T], vv[:, 1, h, :], w[:, T:T + P], start=False, stop=True).then_inc(s_pv, 1)

                def turn_ctx(g, i):
                    pe.wait_ge(s_ctx, at(i, g + 1, 2))
                    dst = (pe_[0], ppv)[g]
                    for t in range(NT):
                        for k in range(2):
                            last = tr(dst[:, t, k * P:(k + 1) * P], ctxT[:, k, t * P:(t + 1) * P], ident[:, :])
                    last.then_inc(s_ctxp, 1)

                if not isinstance(b, int) or b >= 1:
                    ptr_left = (s_thb, at(p, 0, **CREDIT))
                else:
                    ptr_left = None
                if v:
                    if b_is(b, 0):
                        ptr_left = (s_xT1, at(b, 1))
                    pe.wait_ge(*ptr_left)
                    project(ptr, xT1, wqkv, Cols(2 * C, C)).then_inc(s_vp, 1)
                    ptr_left = (s_v, at(b, 1))
                    feature(0)
                if c:
                    turn_ctx(1, p)
                if v:
                    feature(1)
                if a:
                    conv()
                if v:
                    feature(2)
                if c:
                    if b_is(b, NB):
                        pe.wait_ge(s_on, at(p, 2, 2))
                        pe.wait_ge(*ptr_left)
                    else:
                        pe.wait_ge(*ptr_left)
                        pe.wait_ge(s_on, at(p, 2, 2))
                    for i in range(CT):
                        for j in range(NT):
                            last = tr(ptr[:, i * T + j * P:i * T + (j + 1) * P],
                                      on[:, j, :, :].rearrange("p h d -> p (h d)")[:, i * P:(i + 1) * P], ident[:, :])
                    last.then_inc(s_onTp, 1)
                    ptr_left = (s_onT, at(p, 1))
                if v:
                    feature(3)
                if a:
                    pe.wait_ge(s_edges, at(n, PAIRS, PAIRS))
                    if ptr_left:
                        pe.wait_ge(*ptr_left)
                    edge_sums().then_inc(s_hT, 1)
                    ptr_left = (s_h0, at(n, 1))
                if v:
                    feature(4)
                if c:
                    pe.wait_ge(s_onT, at(p, 1))
                    pe.wait_ge(*ptr_left)
                    project(ptr, onT, wout, Cols(0, C)).then_inc(s_op, 1)
                    ptr_left = (s_h1, at(p, 1))
                if v:
                    feature(5)
                if a:
                    pe.wait_ge(s_xn1, at(n, 1))
                    pe.wait_ge(*ptr_left)
                    turn(xn1, ptr[:, :], ident[:, :]).then_inc(s_xT1p, 1)
                    ptr_left = (s_xT1, at(n, 1))
                if v:
                    feature(6)
                if a:
                    pe.wait_ge(s_xT1, at(n, 1))
                    project(pf[:, :, :].rearrange("p a k -> p (a k)"), xT1, wqkv, Cols(0, 2 * C)).then_inc(s_qkp, 1)
                if c:
                    pe.wait_ge(s_x8b, at(p, 1))
                    pe.wait_ge(*ptr_left)
                    turn(x8b, ptr[:, 0:T].bitcast(bf16), identb[:, :]).then_inc(s_x8Tp, 1)
                if v:
                    feature(7)
                if c:
                    pe.wait_ge(s_x8T, at(p, 1))
                    project(ptr, x8T, fwq, Cols(0, C)).then_inc(s_yp, 1)
                if v:
                    score(0)
                    score(1)
                    value(0)
                    for h in range(2, 5):
                        score(h)
                        value(h - 1)
                if c:
                    pe.wait_ge(s_y16, at(p, 1))
                    pe.wait_ge(s_xn3, at(p, 1))
                    turn(xn3, ptr[:, :], ident[:, :]).then_inc(s_xT3p, 1)
                for r in range(3):
                    if v:
                        score(5 + r)
                        value(4 + r)
                    if c:
                        if r == 0:
                            pe.wait_ge(s_xT3, at(p, 1))
                            if a:
                                pe.wait_ge(s_qk, at(n, 1))
                        if r == 2:
                            pe.wait_ge(s_raw, at(p, 1, 3, **CREDIT))
                        for o in range(2):
                            for k in range(CT):
                                last = mm(pf[:, r % 2, o * T:(o + 1) * T],
                                          w1[:, k, (2 * r + o) * P:(2 * r + o + 1) * P], xT3[:, k, :],
                                          start=(k == 0), stop=(k == CT - 1))
                        last.then_inc(s_l1p, 1)
                if c:
                    for k in range(CT):
                        last = mm(ptr[0:H, 0:T], w1b[:, k, :], xT3[:, k, :], start=(k == 0), stop=(k == CT - 1))
                    last.then_inc(s_bp, 1)
                if v:
                    for h in range(8, 13):
                        score(h)
                        value(h - 1)
                        if h == 9:
                            pe.wait_ge(s_fe, at(b, NF, NF))
                            turn_ctx(0, b)
                if a:
                    pe.wait_ge(s_qkn, at(n, 1))
                    if v:
                        pe.wait_ge(s_on, at(b, 1, 2))
                    for j in range(4):
                        for t in range(NT):
                            last = tr(pe_[j // 2][:, j % 2, t * P:(t + 1) * P], qkn[:, t, j * P:(j + 1) * P],
                                      ident[:, :])
                    last.then_inc(s_qkTp, 1)
                if v:
                    for h in range(13, H):
                        score(h)
                        value(h - 1)
                    value(H - 1)

            rounds(pe, body)


def delta_rule(nc, NB, ident_d, scratch):
    f32 = mybir.dt.float32
    ALU, ACT, AX = mybir.AluOpType, mybir.ActivationFunctionType, mybir.AxisListType
    G, BLOCKS = NB // LANES, T // TB
    HALVES = [slice(0, G // 2), slice(G // 2, G)]
    FOUR = 4
    ROUND = 2 * FOUR
    ROUNDS = TB // ROUND // 4
    PIECES = 2 * ROUNDS
    PIECE = TB // PIECES
    GD = G * D
    lanes = lambda n: scratch[n].rearrange("(g b) (h d) t -> g (b h) d t", b=LANES, h=H)
    with ExitStack() as ctx:
        sb = lambda n, s, t=f32: ctx.enter_context(nc.sbuf_tensor(n, s, t))
        sem = lambda n: ctx.enter_context(nc.semaphore(n))
        idle_pool, idle_dve = sb("d_idle", [1, IDLE]), sb("d_idle_dve", [1, IDLE])
        ident = sb("d_ident", [P, P])
        kr, qr, vr = ([sb(f"d_{n}{i}", [P, G, D, TB]) for i in range(2)] for n in ("k", "q", "v"))
        beta = [sb(f"d_beta{i}", [P, G, TB]) for i in range(2)]
        ob = [sb(f"d_o{i}", [P, G, D, TB]) for i in range(2)]
        squares = sb("d_squares", [P, 2, G, D, PIECE])
        sums = sb("d_sums", [P, 2, G, TB])
        root_o, root_k = sb("d_root_o", [P, G, TB]), sb("d_root_k", [P, G, TB])
        v_scale = sb("d_v_scale", [P, G, TB])
        k_scale = [sb(f"d_k_scale{i}", [P, G, TB]) for i in range(2)]
        q_eps = [sb(f"d_q_eps{i}", [P, G, TB]) for i in range(2)]
        S = sb("d_S", [P, 2, G, D, D])
        pk = sb("d_pk", [P, G, D, D])
        outer = sb("d_outer", [P, G, D, D])
        kS, u = sb("d_kS", [P, G, D]), sb("d_u", [P, G, D])
        pq = sb("d_pq", [P, 2, FOUR, G, D, D])
        ps_o = [ctx.enter_context(nc.psum_tensor(f"d_ps_o{i}", [P, 512], f32)) for i in range(2)]
        ps_sum = ctx.enter_context(nc.psum_tensor("d_ps_sum", [P, 512], f32))

        s_ident = sem("d_ident_loaded")
        s_ldkq = [sem(f"d_k_and_q_loaded{i}") for i in range(2)]
        s_ld = [sem(f"d_v_and_beta_loaded{i}") for i in range(2)]
        s_st = [sem(f"d_o_stored{i}") for i in range(2)]
        s_init = sem("d_init")
        s_arg_o = sem("d_argument_of_o_roots")
        s_arg_k = sem("d_argument_of_k_roots")
        s_root = sem("d_root")
        s_inv = sem("d_inverse_root")
        s_vscale = sem("d_v_scale_ready")
        s_S = [sem(f"d_state_ready{i}") for i in range(2)]
        s_pk = [sem(f"d_Sk_products{i}") for i in range(2)]
        s_kS = [sem(f"d_Sk_ready{i}") for i in range(2)]
        s_u = [sem(f"d_u_ready{i}") for i in range(2)]
        s_outer = [sem(f"d_outer_ready{i}") for i in range(2)]
        s_pq = sem("d_Sq_products")
        s_osum = sem("d_o_summed")
        s_o = sem("d_o_out_of_psum")
        s_sq = sem("d_squares_ready")
        s_sqsum = sem("d_squares_summed")
        s_sums = sem("d_sums_out_of_psum")
        s_vs = sem("d_v_scaled")
        s_onorm = sem("d_o_scaled")
        block = ctx.enter_context(nc.Block())
        NLD = 2 * G * 16
        AHEAD = 2

        def over_d(a):
            return a.unsqueeze(2).to_broadcast([P, G, D, PIECE])

        QUARTERS = []
        for n in range(-1, BLOCKS + 1):
            runs = n if 0 <= n < BLOCKS else None
            last, nxt = (n - 1 if n > 0 else None), (n + 1 if n + 1 < BLOCKS else None)
            for i, side in enumerate((dict(sum_o=last), dict(root_o=last, sum_kq=nxt), dict(scale_o=last, root_k=nxt),
                                      dict(scale_v=nxt))):
                if runs is not None or any(v is not None for v in side.values()):
                    QUARTERS.append((runs, i * ROUND * ROUNDS, side))

        def before(quarter, *works):
            return PIECES * sum(q[2].get(k) is not None for q in QUARTERS[:quarter] for k in works)

        @block.sync
        def _(sp):
            for sem_ in (s_pq, s_osum, s_o):
                sp.sem_inc(sem_, AHEAD)
            sp.sem_inc(s_sqsum, 1)
            sp.sem_inc(s_sums, 1)
            sp.dma_start(ident[:, :], ident_d[:, :]).then_inc(s_ident, 16)

            def load(n):
                cols = slice(n * TB, (n + 1) * TB)
                for g in range(G):
                    for tile, name in ((kr, "k"), (qr, "q")):
                        sp.dma_start(tile[n % 2][:, g, :, :], lanes(name)[g, :, :, cols]).then_inc(s_ldkq[n % 2], 16)
                for g in range(G):
                    sp.dma_start(vr[n % 2][:, g, :, :], lanes("v")[g, :, :, cols]).then_inc(s_ld[n % 2], 16)
                    sp.dma_start(beta[n % 2][:, g, :], scratch["beta"].rearrange("(g b) h t -> g (b h) t", b=LANES)
                                 [g, :, cols]).then_inc(s_ld[n % 2], 16)

            def store(n):
                sp.wait_ge(s_onorm, PIECES * (n + 1))
                for g in range(G):
                    sp.dma_start(lanes("o")[g, :, :, n * TB:(n + 1) * TB],
                                 ob[n % 2][:, g, :, :]).then_inc(s_st[n % 2], 16)

            load(0)
            load(1)
            for n in range(1, BLOCKS):
                if n + 1 < BLOCKS:
                    for c in range(2):
                        sp.wait_ge(s_S[c], n * TB + 1)
                    sp.wait_ge(s_pq, n * TB + AHEAD)
                    load(n + 1)
                store(n - 1)
            store(BLOCKS - 1)
            for i in range(2):
                sp.wait_ge(s_st[i], 16 * G * BLOCKS // 2)

        @block.vector
        def _(dve):
            TT = nc.vector.tensor_tensor
            for c, half in enumerate(HALVES):
                nc.vector.memset(S[:, 0, half, :, :], 0.0).then_inc(s_S[c], 1)
            for quarter, (n, first, side) in enumerate(QUARTERS):
                scale_o, scale_v, root_next = side.get("scale_o"), side.get("scale_v"), side.get("root_k")
                if n is not None and first == 0:
                    apart(dve, idle_dve, s_ldkq[n % 2], (n // 2 + 1) * NLD)
                    apart(dve, idle_dve, s_vs, 2 * PIECES * (n + 1))
                if n is None and scale_o is None and scale_v is None and root_next is None:
                    continue
                with dve.Fori(0, ROUNDS) as i:
                    for j in range(ROUND):
                        t = first + ROUND * i + j
                        if j % FOUR == 0 and (scale_o is not None or scale_v is not None):
                            piece, cols = 2 * i + j // FOUR, bass.ds(PIECE * (2 * i + j // FOUR), PIECE)
                            a = root_o if scale_v is None else root_k
                            dve.wait_ge(s_root, before(quarter, "scale_o", "scale_v") + piece + 1)
                            nc.vector.reciprocal(a[:, :, cols], a[:, :, cols]).then_inc(s_inv, 1)
                        if j % FOUR == 0 and root_next is not None:
                            piece, cols = 2 * i + j // FOUR, bass.ds(PIECE * (2 * i + j // FOUR), PIECE)
                            dve.wait_ge(s_sums, before(quarter, "sum_o", "sum_kq") - PIECES + piece + 2)
                            nc.vector.tensor_scalar(sums[:, :, :, cols], sums[:, :, :, cols], RMS_EPS * RMS_EPS, None,
                                                    ALU.max).then_inc(s_arg_k, 1)
                        if n is None:
                            continue
                        tok, b, odd = n * TB + t, n % 2, j % 2
                        at_t = bass.ds(t, 1)
                        col = lambda a, half: a[:, half, :, at_t].rearrange("p g d o -> p g (d o)")
                        full = [P, G // 2, D, D]
                        for c, half in enumerate(HALVES):
                            dve.wait_ge(s_S[c], tok + 1)
                            TT(pk[:, half, :, :], S[:, odd, half, :, :],
                               col(kr[b], half).unsqueeze(2).to_broadcast(full), ALU.mult).then_inc(s_pk[c], 1)
                        for c, half in enumerate(HALVES):
                            dve.wait_ge(s_pk[c], tok + 1)
                            nc.vector.tensor_reduce(kS[:, half, :], pk[:, half, :, :], AX.X, ALU.add).then_inc(s_kS[c], 1)
                        for c, half in enumerate(HALVES):
                            dve.wait_ge(s_kS[c], tok + 1)
                            for g in range(half.start, half.stop):
                                last = nc.vector.scalar_tensor_tensor(
                                    u[:, g, :], kS[:, g, :], k_scale[b][:, g, at_t],
                                    vr[b][:, g, :, at_t].rearrange("p d o -> p (d o)"), ALU.mult, ALU.subtract)
                            last.then_inc(s_u[c], 1)
                        for c, half in enumerate(HALVES):
                            dve.wait_ge(s_u[c], tok + 1)
                            TT(outer[:, half, :, :], u[:, half, :].unsqueeze(3).to_broadcast(full),
                               col(kr[b], half).unsqueeze(2).to_broadcast(full), ALU.mult).then_inc(s_outer[c], 1)
                        for c, half in enumerate(HALVES):
                            dve.wait_ge(s_outer[c], tok + 1)
                            dve.wait_ge(s_pq, tok - 1 + AHEAD)
                            TT(S[:, 1 - odd, half, :, :], S[:, odd, half, :, :], outer[:, half, :, :],
                               ALU.subtract).then_inc(s_S[c], 1)

        @block.gpsimd
        def _(pool):
            TT = nc.gpsimd.tensor_tensor
            nc.gpsimd.memset(idle_pool[:, :], 0.0).then_inc(s_init, 1)
            pool.wait_ge(s_init, 1)
            for quarter, (n, first, side) in enumerate(QUARTERS):
                with pool.Fori(0, ROUNDS) as i:
                    for v in range(2):
                        for j in range(FOUR):
                            if n is None:
                                break
                            t = first + ROUND * i + FOUR * v + j
                            tok, four = n * TB + t, (n * TB + first) // FOUR + 2 * i + v
                            for c in range(2):
                                pool.wait_ge(s_S[c], tok + 2)
                            if j == 0:
                                pool.wait_ge(s_osum, four - 1 + AHEAD)
                            TT(pq[:, v, j, :, :, :], S[:, 1 - j % 2, :, :, :],
                               qr[n % 2][:, :, :, bass.ds(t, 1)].rearrange("p g d o -> p g (d o)").unsqueeze(2)
                               .to_broadcast([P, G, D, D]), ALU.mult).then_inc(s_pq, 1)
                        piece, cols = 2 * i + v, bass.ds(PIECE * (2 * i + v), PIECE)
                        sums_out = before(quarter, "sum_o", "sum_kq")
                        if (m := side.get("root_o")) is not None:
                            pool.wait_ge(s_sums, sums_out - PIECES + piece + 2)
                            TT(root_o[:, :, cols], root_o[:, :, cols], q_eps[m % 2][:, :, cols],
                               ALU.add).then_inc(s_arg_o, 1)
                        if (m := side.get("scale_o")) is not None:
                            pool.wait_ge(s_inv, before(quarter, "scale_o", "scale_v") + piece + 1)
                            a = ob[m % 2]
                            TT(a[:, :, :, cols], a[:, :, :, cols], over_d(root_o[:, :, cols]),
                               ALU.mult).then_inc(s_onorm, 1)
                        if (m := side.get("scale_v")) is not None:
                            pool.wait_ge(s_inv, before(quarter, "scale_o", "scale_v") + piece + 1)
                            pool.wait_ge(s_ld[m % 2], (m // 2 + 1) * NLD)
                            TT(v_scale[:, :, cols], root_k[:, :, cols], beta[m % 2][:, :, cols],
                               ALU.mult).then_inc(s_vscale, 1)
                            pool.wait_ge(s_vscale, before(quarter, "scale_v") + piece + 1)
                            TT(k_scale[m % 2][:, :, cols], root_k[:, :, cols], v_scale[:, :, cols],
                               ALU.mult).then_inc(s_vs, 1)
                            a = vr[m % 2]
                            TT(a[:, :, :, cols], a[:, :, :, cols], over_d(v_scale[:, :, cols]),
                               ALU.mult).then_inc(s_vs, 1)

        @block.scalar
        def _(sc):
            def out(dst, src):
                return nc.scalar.activation(dst, src, ACT.Copy)

            for quarter, (n, first, side) in enumerate(QUARTERS):
                sum_o, sum_kq = side.get("sum_o"), side.get("sum_kq")
                with sc.Fori(0, ROUNDS) as i:
                    for v in range(2):
                        cols, piece = bass.ds(PIECE * (2 * i + v), PIECE), before(quarter, "sum_o", "sum_kq") + 2 * i + v
                        if sum_o is not None:
                            sc.wait_ge(s_sqsum, piece + 1)
                            sc.wait_ge(s_o, (sum_o + 1) * TB // FOUR + AHEAD)
                            nc.scalar.activation(squares[:, 0, :, :, :], ob[sum_o % 2][:, :, :, cols],
                                                 ACT.Square).then_inc(s_sq, 2)
                        if sum_kq is not None:
                            sc.wait_ge(s_sqsum, piece + 1)
                            sc.wait_ge(s_ldkq[sum_kq % 2], (sum_kq // 2 + 1) * NLD)
                            for a, src in enumerate((kr, qr)):
                                nc.scalar.activation(squares[:, a, :, :, :], src[sum_kq % 2][:, :, :, cols],
                                                     ACT.Square).then_inc(s_sq, 1)
                        if n is not None:
                            four = (n * TB + first) // FOUR + 2 * i + v
                            sc.wait_ge(s_osum, four + 1 + AHEAD)
                            if n >= 2:
                                sc.wait_ge(s_st[n % 2], n // 2 * 16 * G)
                            out(ob[n % 2][:, :, :, bass.ds(first + FOUR * (2 * i + v), FOUR)].rearrange("p g d t -> p (g d) t"),
                                ps_o[v][:, 0:FOUR * GD].rearrange("p (t e) -> p e t", t=FOUR)).then_inc(s_o, 1)
                        if sum_o is not None:
                            sc.wait_ge(s_sqsum, piece + 2)
                            nc.scalar.activation(root_o[:, :, cols], ps_sum[:, 0:G * PIECE].rearrange(
                                "p (g t) -> p g t", g=G), ACT.Copy, scale=1.0 / D).then_inc(s_sums, 1)
                        if sum_kq is not None:
                            sc.wait_ge(s_sqsum, piece + 2)
                            out(sums[:, :, :, cols].rearrange("p a g t -> p (a g) t"),
                                ps_sum[:, 0:2 * G * PIECE].rearrange("p (a t) -> p a t", a=2 * G)).then_inc(s_sums, 1)

                        if side.get("root_o") is not None:
                            sc.wait_ge(s_arg_o, before(quarter, "root_o") + 2 * i + v + 1)
                            nc.scalar.activation(root_o[:, :, cols], root_o[:, :, cols], ACT.Sqrt).then_inc(s_root, 1)
                        if (m := side.get("root_k")) is not None:
                            sc.wait_ge(s_arg_k, before(quarter, "root_k") + 2 * i + v + 1)
                            nc.scalar.activation(q_eps[m % 2][:, :, cols], sums[:, 1, :, cols], ACT.Copy,
                                                 scale=RMS_EPS * D)
                            nc.scalar.activation(root_k[:, :, cols], sums[:, 0, :, cols], ACT.Sqrt).then_inc(s_root, 1)

        @block.tensor
        def _(pe):
            def add_up(dst, src):
                for d in range(D):
                    ins = pe.matmul(dst, lhsT=ident[:, :], rhs=src(d), start=d == 0, stop=d == D - 1)
                return ins

            for quarter, (n, first, side) in enumerate(QUARTERS):
                sum_o, sum_kq = side.get("sum_o"), side.get("sum_kq")
                if n is None and sum_o is None and sum_kq is None:
                    continue
                with pe.Fori(0, ROUNDS) as i:
                    for v in range(2):
                        if quarter == 0:
                            pe.wait_ge(s_ident, 16)
                        if n is not None:
                            four = (n * TB + first) // FOUR + 2 * i + v
                            pe.wait_ge(s_pq, FOUR * (four + 1) + AHEAD)
                            pe.wait_ge(s_o, four - 1 + AHEAD)
                            add_up(ps_o[v][:, 0:FOUR * GD], lambda d: pq[:, v, :, :, :, d].rearrange("p t g e -> p (t g e)")
                                   ).then_inc(s_osum, 1)
                        if sum_o is not None or sum_kq is not None:
                            piece = before(quarter, "sum_o", "sum_kq") + 2 * i + v
                            pe.wait_ge(s_sq, 2 * (piece + 1))
                            pe.wait_ge(s_sums, piece + 1)
                        if sum_o is not None:
                            add_up(ps_sum[:, 0:G * PIECE].rearrange("p (g t) -> p g t", g=G),
                                   lambda d: squares[:, 0, :, d, :]).then_inc(s_sqsum, 1)
                        if sum_kq is not None:
                            add_up(ps_sum[:, 0:2 * G * PIECE].rearrange("p (a g t) -> p a g t", a=2, g=G),
                                   lambda d: squares[:, :, :, d, :]).then_inc(s_sqsum, 1)


def back(nc, NB, ident_d, first_d, w1_o, norm_w, router, w_in, b_in, w_dn, b_dn, scratch, out):
    f32 = mybir.dt.float32
    ALU, ACT, AX = mybir.AluOpType, mybir.ActivationFunctionType, mybir.AxisListType
    with ExitStack() as ctx:
        sb = lambda n, s, t=f32: ctx.enter_context(nc.sbuf_tensor(n, s, t))
        ps = lambda n, s, t=f32: ctx.enter_context(nc.psum_tensor(n, s, t))
        sem = lambda n: ctx.enter_context(nc.semaphore(n))
        idle_pool, idle_dve = sb("m_idle_pool", [1, IDLE]), sb("m_idle_dve", [1, IDLE])
        ident = sb("m_ident", [P, P])
        first = sb("m_first", [P, E, E])
        wo = sb("m_wo", [P, CT, C])
        nw = sb("m_nw", [P, 1])
        wr = sb("m_wr", [P, CT, E])
        wi = sb("m_wi", [P, E, CT, C])
        bi = sb("m_bi", [P, E, CT])
        wd = sb("m_wd", [P, E, CT, C])
        bd = sb("m_bd", [E, C])
        mh = sb("m_mh", [P, NT])
        euler = sb("m_euler", [P, NT, E])

        oT = sb("m_oT", [P, CT, T])
        oTw = sb("m_oTw", [P, CT, T])
        h2 = sb("m_h2", [P, NT, C])
        h3 = [sb(f"m_h3_{i}", [P, NT, C]) for i in range(2)]
        stats = sb("m_stats", [P, NT, 6])
        mv = sb("m_mv", [P, NT, 2])
        vare = sb("m_vare", [P, NT])
        rstd = sb("m_rstd", [P, NT])
        xn = sb("m_xn", [P, NT, C])
        xT = [sb(f"m_xT{i}", [P, CT, T]) for i in range(2)]
        lmax = sb("m_lmax", [P, NT])
        lsub = sb("m_lsub", [P, NT, E])
        pexp = sb("m_pexp", [P, NT, E])
        psum_ = sb("m_psum", [P, NT])
        prec = sb("m_prec", [P, NT])
        prob = sb("m_prob", [P, NT, E])
        gt = sb("m_gt", [P, NT, E, E])
        eq = sb("m_eq", [P, NT, E, E])
        rank = sb("m_rank", [P, NT, E])
        gate = [sb(f"m_gate{i}", [P, NT, E]) for i in range(2)]
        gateT = [sb(f"m_gateT{i}", [E, T]) for i in range(2)]
        hid = sb("m_hid", [P, 2, CT, T])
        acc = sb("m_acc", [P, NT, C])

        pA = ps("m_pA", [P, 512])
        pG = ps("m_pG", [P, 512])
        pB = ps("m_pB", [P, 512])
        pH = [ps(f"m_pH{i}", [P, CT, T]) for i in range(2)]
        pY = [ps(f"m_pY{i}", [P, NT, C]) for i in range(2)]

        s_w = sem("m_weights")
        s_in = sem("m_loaded")
        s_init = sem("m_init")
        s_ow = sem("m_o_weighted")
        s_wo = sem("m_wo_in_psum")
        s_h3 = sem("m_h3_ready")
        s_stat = sem("m_ln_stats")
        s_rstd = sem("m_ln_rstd")
        s_ln = sem("m_ln_out")
        s_pool = sem("m_pool_step")
        s_xTp = sem("m_xT_in_psum")
        s_xT = sem("m_xT_ready")
        s_lg = sem("m_logits_in_psum")
        s_lsub = sem("m_logits_less_max")
        s_pexp = sem("m_exponentials")
        s_dve = sem("m_vector_step")
        s_gate = sem("m_gates")
        s_gTp = sem("m_gateT_in_psum")
        s_gT = sem("m_gateT_ready")
        s_bp = sem("m_bias_in_psum")
        s_hp = sem("m_hidden_in_psum")
        s_hid = sem("m_hidden_ready")
        s_yp = sem("m_y_in_psum")
        s_acc = sem("m_y_added")
        s_out = sem("m_out_ready")
        s_st = sem("m_out_stored")
        block = ctx.enter_context(nc.Block())
        loads = [(ident, ident_d), (first, first_d), (wo, w1_o.rearrange("(c p) n -> p c n", p=P)), (nw, norm_w),
                 (wr, router.rearrange("(c p) n -> p c n", p=P)),
                 (wi, w_in.rearrange("e (c p) n -> p (e c) n", p=P).rearrange("p (e c) n -> p e c n", c=CT)),
                 (bi, b_in.rearrange("e (c p) -> p e c", p=P)),
                 (wd, w_dn.rearrange("e (c p) n -> p (e c) n", p=P).rearrange("p (e c) n -> p e c n", c=CT)), (bd, b_dn)]
        NW = 16 * len(loads)

        AHEAD = 2

        def rounds(engine, body):
            body(-1, 1, False, True)
            with engine.Fori(0, NB // 2 - 1) as i:
                for parity in range(2):
                    body(2 * i + parity, parity, True, True)
            body(NB - 2, 0, True, True)
            body(NB - 1, 1, True, False)

        @block.sync
        def _(sp):
            for sem_ in (s_h3, s_out, s_st):
                sp.sem_inc(sem_, 1)
            for sem_ in (s_hid, s_yp, s_acc):
                sp.sem_inc(sem_, AHEAD)
            for tile, src in loads:
                with nc.allow_non_contiguous_dma(reason="biases, once"):
                    sp.dma_start(tile[tuple(slice(None) for _ in tile.shape)], src).then_inc(s_w, 16)

            def load(n):
                sp.dma_start(oT[:, :, :], image(scratch["o"], n)).then_inc(s_in, 16)
                sp.dma_start(h2[:, :, :], image(scratch["h"], n)).then_inc(s_in, 16)

            load(0)

            def body(b, parity, experts, prepare):
                if not isinstance(b, int) or b + 2 < NB:
                    sp.wait_ge(s_h3, at(b + 2, 0, **CREDIT))
                    load(b + 2)
                if experts:
                    sp.wait_ge(s_out, at(b, 1, **CREDIT))
                    sp.dma_start(image(out, b), acc[:, :, :]).then_inc(s_st, 16)

            rounds(sp, body)
            sp.wait_ge(s_st, 16 * NB + 1)

        @block.gpsimd
        def _(pool):
            nc.gpsimd.memset(mh[:, :], -0.5).then_inc(s_init, 1)
            nc.gpsimd.memset(euler[:, :, :], float(np.e)).then_inc(s_init, 1)
            nc.gpsimd.memset(idle_pool[:, :], 0.0).then_inc(s_init, 1)
            pool.wait_ge(s_init, 3)

            def body(b, parity, experts, prepare):
                n = b + 1
                if prepare:
                    apart(pool, idle_pool, s_stat, at(n, 1))
                    nc.gpsimd.tensor_scalar(vare[:, :], mv[:, :, 1], LN_EPS, None, ALU.add).then_inc(s_pool, 1)
                    pool.wait_ge(s_pool, at(n, 1))
                    nc.gpsimd.tensor_tensor(rstd[:, :], vare[:, :], mh[:, :], ALU.pow).then_inc(s_rstd, 1)
                    pool.wait_ge(s_lsub, at(n, 1))
                    nc.gpsimd.tensor_tensor(pexp[:, :, :], euler[:, :, :], lsub[:, :, :], ALU.pow).then_inc(s_pexp, 1)

            rounds(pool, body)

        @block.vector
        def _(dve):
            TT, RED = nc.vector.tensor_tensor, nc.vector.tensor_reduce
            dve.wait_ge(s_w, NW)

            def body(b, parity, experts, prepare):
                n, next_ = b + 1, 1 - parity
                m = [0]
                PER = 7

                def link(ins, alone=False):
                    m[0] += 1
                    ins.then_inc(s_dve, 1)
                    if alone:
                        apart(dve, idle_dve, s_dve, at(n, m[0], PER))
                    else:
                        dve.wait_ge(s_dve, at(n, m[0], PER))

                def projected():
                    dve.wait_ge(s_wo, at(n, 1))
                    TT(h3[next_][:, :, :].rearrange("p a c -> p (a c)"), pA[:, :],
                       h2[:, :, :].rearrange("p a c -> p (a c)"), ALU.add).then_inc(s_h3, 1)
                    dve.wait_ge(s_h3, at(n, 1, **CREDIT))
                    for t in range(NT):
                        last = nc.vector.bn_stats(stats[:, t, :], h3[next_][:, t, :])
                    link(last, alone=True)
                    for t in range(NT):
                        last = nc.vector.bn_aggr(mv[:, t, :], stats[:, t, :])
                    last.then_inc(s_stat, 1)

                def normed():
                    dve.wait_ge(s_rstd, at(n, 1))
                    for t in range(NT):
                        last = nc.vector.tensor_scalar(xn[:, t, :], h3[next_][:, t, :], mv[:, t, 0:1], rstd[:, t:t + 1],
                                                       ALU.subtract, ALU.mult)
                    last.then_inc(s_ln, 1)

                wide = [P, NT, E]

                def less_max():
                    dve.wait_ge(s_lg, at(n, 1))
                    lg = pG[:, 0:NT * E].rearrange("p (a e) -> p a e", a=NT)
                    link(RED(lmax[:, :], lg, AX.X, ALU.max))
                    TT(lsub[:, :, :], lg, lmax[:, :].unsqueeze(2).to_broadcast(wide), ALU.subtract).then_inc(s_lsub, 1)

                def gates():
                    dve.wait_ge(s_pexp, at(n, 1))
                    link(RED(psum_[:, :], pexp[:, :, :], AX.X, ALU.add))
                    link(nc.vector.reciprocal(prec[:, :], psum_[:, :]))
                    link(TT(prob[:, :, :], pexp[:, :, :], prec[:, :].unsqueeze(2).to_broadcast(wide), ALU.mult))
                    for t in range(NT):
                        mine = prob[:, t, :].unsqueeze(2).to_broadcast([P, E, E])
                        theirs = prob[:, t, :].unsqueeze(1).to_broadcast([P, E, E])
                        TT(gt[:, t, :, :], theirs, mine, ALU.is_gt)
                        last = TT(eq[:, t, :, :], theirs, mine, ALU.is_equal)
                    link(last)
                    for t in range(NT):
                        last = TT(eq[:, t, :, :], eq[:, t, :, :], first[:, :, :], ALU.mult)
                    link(last)
                    flat = lambda a: a[:, :, :, :].rearrange("p a e f -> p (a e f)")
                    TT(flat(gt), flat(gt), flat(eq), ALU.add).then_inc(s_gate, 1)
                    dve.wait_ge(s_gate, at(n, 1, 3))
                    RED(rank[:, :, :].rearrange("p a e -> p (a e)"), gt[:, :, :, :].rearrange("p a e f -> p (a e) f"),
                        AX.X, ALU.add).then_inc(s_gate, 1)
                    dve.wait_ge(s_gate, at(n, 2, 3))
                    nc.vector.scalar_tensor_tensor(gate[next_][:, :, :], rank[:, :, :], 2.0, prob[:, :, :], ALU.is_lt,
                                                   ALU.mult).then_inc(s_gate, 1)

                def add(e):
                    if e == 0:
                        dve.wait_ge(s_gate, at(b, 3, 3))
                        dve.wait_ge(s_st, at(b, 0, unit=16, **CREDIT))
                    dve.wait_ge(s_yp, at(b, e + 1, E, credit=AHEAD))
                    if e:
                        dve.wait_ge(s_acc, at(b, e, E, credit=AHEAD))
                    for t in range(NT):
                        last = nc.vector.scalar_tensor_tensor(acc[:, t, :], pY[e % 2][:, t, :],
                                                              gate[parity][:, t, e:e + 1],
                                                              (acc if e else h3[parity])[:, t, :], ALU.mult, ALU.add)
                    last.then_inc(s_acc, 1)

                between = {0: projected, 1: normed, 3: less_max, 4: gates}
                for e in range(E):
                    if experts:
                        add(e)
                    if prepare and e in between:
                        between[e]()
                if experts:
                    dve.wait_ge(s_acc, at(b, E, E, credit=AHEAD))
                    dve.wait_ge(s_bp, at(b, 1))
                    TT(acc[:, :, :].rearrange("p a c -> p (a c)"), acc[:, :, :].rearrange("p a c -> p (a c)"), pB[:, :],
                       ALU.add).then_inc(s_out, 1)
                assert m[0] == (PER if prepare else 0)

            rounds(dve, body)

        @block.scalar
        def _(sc):
            A = nc.scalar.activation
            sc.wait_ge(s_w, NW)

            def body(b, parity, experts, prepare):
                n, next_ = b + 1, 1 - parity

                def weigh():
                    sc.wait_ge(s_in, at(n, 1) * 32)
                    A(oTw[:, :, :], oT[:, :, :], ACT.Copy, scale=nw[:, 0:1]).then_inc(s_ow, 1)

                def turned():
                    sc.wait_ge(s_xTp, at(n, 1))
                    A(xT[next_][:, :, :].rearrange("p c t -> p (c t)"), pA[:, :], ACT.Copy).then_inc(s_xT, 1)

                def gates_turned():
                    sc.wait_ge(s_gTp, at(n, 1))
                    A(gateT[next_][:, :], pG[0:E, 0:T], ACT.Copy).then_inc(s_gT, 1)

                def hidden(e):
                    sc.wait_ge(s_hp, at(b, e + 1, E))
                    sc.wait_ge(s_yp, at(b, e - 1, E, credit=AHEAD))
                    for c in range(CT):
                        last = A(hid[:, e % 2, c, :], pH[e % 2][:, c, :], ACT.Gelu_apprx_tanh, bias=bi[:, e, c:c + 1])
                    last.then_inc(s_hid, 1)

                if prepare:
                    weigh()
                for e in range(E):
                    if experts:
                        hidden(e)
                    if prepare and e == 3:
                        turned()
                if prepare:
                    gates_turned()

            rounds(sc, body)

        @block.tensor
        def _(pe):
            mm, tr = nc.tensor.matmul, nc.tensor.transpose
            pe.wait_ge(s_w, NW)

            def body(b, parity, experts, prepare):
                n, next_ = b + 1, 1 - parity

                def project():
                    pe.wait_ge(s_ow, at(n, 1))
                    if not b_is(b, -1):
                        pe.wait_ge(s_xT, at(n, 0))
                    for t in range(NT):
                        for c in range(CT):
                            last = mm(pA[:, t * C:(t + 1) * C], oTw[:, c, t * P:(t + 1) * P], wo[:, c, :],
                                      start=(c == 0), stop=(c == CT - 1))
                    last.then_inc(s_wo, 1)

                def turn():
                    pe.wait_ge(s_ln, at(n, 1))
                    for i in range(CT):
                        for j in range(NT):
                            last = tr(pA[:, i * T + j * P:i * T + (j + 1) * P], xn[:, j, i * P:(i + 1) * P], ident[:, :])
                    last.then_inc(s_xTp, 1)

                def logits():
                    pe.wait_ge(s_xT, at(n, 1))
                    if not b_is(b, -1):
                        pe.wait_ge(s_gT, at(n, 0))
                    for t in range(NT):
                        for c in range(CT):
                            last = mm(pG[:, t * E:(t + 1) * E], xT[next_][:, c, t * P:(t + 1) * P], wr[:, c, :],
                                      start=(c == 0), stop=(c == CT - 1))
                    last.then_inc(s_lg, 1)

                def turn_gates():
                    pe.wait_ge(s_gate, at(n, 3, 3))
                    for t in range(NT):
                        last = tr(pG[0:E, t * P:(t + 1) * P], gate[next_][:, t, :], ident[:, :])
                    last.then_inc(s_gTp, 1)

                def bias():
                    pe.wait_ge(s_gT, at(b, 1))
                    pe.wait_ge(s_out, at(b, 0, **CREDIT))
                    for t in range(NT):
                        last = mm(pB[:, t * C:(t + 1) * C], gateT[parity][:, t * P:(t + 1) * P], bd[:, :],
                                  start=True, stop=True)
                    last.then_inc(s_bp, 1)

                def up(e):
                    pe.wait_ge(s_hid, at(b, e - 1, E, credit=AHEAD))
                    if e == 0:
                        pe.wait_ge(s_xT, at(b, 1))
                    for f in range(CT):
                        for c in range(CT):
                            last = mm(pH[e % 2][:, f, :], wi[:, e, c, f * P:(f + 1) * P], xT[parity][:, c, :],
                                      start=(c == 0), stop=(c == CT - 1))
                    last.then_inc(s_hp, 1)

                def down(e):
                    pe.wait_ge(s_hid, at(b, e + 1, E, credit=AHEAD))
                    pe.wait_ge(s_acc, at(b, e - 1, E, credit=AHEAD))
                    for t in range(NT):
                        for c in range(CT):
                            last = mm(pY[e % 2][:, t, :], hid[:, e % 2, c, t * P:(t + 1) * P], wd[:, e, c, :],
                                      start=(c == 0), stop=(c == CT - 1))
                    last.then_inc(s_yp, 1)

                if experts:
                    up(0)
                if prepare:
                    project()
                between = {2: turn, 3: logits, 6: turn_gates}
                for e in range(E):
                    if experts:
                        if e + 1 < E:
                            up(e + 1)
                        down(e)
                        if e == 4:
                            bias()
                    if prepare and e in between:
                        between[e]()

            rounds(pe, body)


def kernel(**inputs):
    import numpy as _np
    import concourse.bacc as _bacc
    from concourse import mybir as _mybir
    from concourse.bass_utils import run_bass_kernel_spmd as _run

    a = {k: _np.asarray(v) for k, v in inputs.items()}
    rows = lambda v: _np.broadcast_to(v.reshape(1, -1), (P, v.size))
    tap = _np.zeros((3, XR, 3, TR), _np.float32)
    for c in range(3):
        for dy in range(3):
            for r in range(TR):
                tap[c, r + dy, dy, r] = GRAY[c]
    s, t = _np.arange(P)[:, None], _np.arange(P)[None, :]
    tri = (t >= s).astype(_np.float32)
    causal = _np.concatenate([tri, _np.ones((P, P), _np.float32), tri], 1)
    parity = _np.stack([(_np.arange(P) // D) % 2 == i for i in range(2)], 1).astype(_np.float32)
    place = _np.zeros((2, TR, 2 * P + TR), _np.float32)
    place[:, _np.arange(TR), P + _np.arange(TR)] = 1.0
    place = place.reshape(2 * TR, 2 * P + TR)
    first = _np.broadcast_to((_np.arange(E)[None, :] < _np.arange(E)[:, None]).astype(_np.float32), (P, E, E))
    laid = {
        "x": a["x"],
        "scharr": rows(a["L0_tok_scharr"]).reshape(P, 2, 3, 3),
        "taps": tap.reshape(KX, 3, TR),
        "ident": _np.eye(P, dtype=_np.float32),
        "causal": causal,
        "first": first,
        "parity": parity,
        "place": place,
        "w_qkv": a["L0_attn_w_qkv"].T,
        "b_qkv": rows(a["L0_attn_b_qkv"]),
        "w_out": a["L0_attn_w_out"].T,
        "b_out": rows(a["L0_attn_b_out"]),
        "omega": a["L0_attn_omega"].transpose(1, 2, 0, 3).reshape(C, F),
        "nodes": _np.tile(_np.repeat(a["L0_attn_quad_nodes"], M), 2).reshape(P, 1),
        "weights": _np.tile(_np.repeat(a["L0_attn_quad_weights"], M), 2).reshape(P, 1),
        "ffn_w": a["L0_ffn_weight"].T,
        "ffn_b": rows(a["L0_ffn_bias"]),
        "w1_qkv": _np.concatenate([a["L1_attn_Wq"], a["L1_attn_Wk"], a["L1_attn_Wv"]], 0).T,
        "w1_b": a["L1_attn_Wb"].T,
        "w1_o": a["L1_attn_Wo"].T,
        "conv_w": _np.concatenate([a["L1_attn_conv_q"], a["L1_attn_conv_k"], a["L1_attn_conv_v"]], 0),
        "norm_w": _np.tile(a["L1_attn_o_norm_w"], P // D).reshape(P, 1),
        "router": a["L1_ffn_router_w"],
        "w_in": a["L1_ffn_w_in"],
        "b_in": a["L1_ffn_b_in"],
        "w_dn": a["L1_ffn_w_out"],
        "b_dn": a["L1_ffn_b_out"],
    }
    nc = _bacc.Bacc("TRN2", target_bir_lowering=False, num_devices=1)
    arrays, args = {}, {}
    for name, v in laid.items():
        v = _np.ascontiguousarray(v)
        arrays[f"in_{name}"] = v
        args[name] = nc.dram_tensor(f"in_{name}", v.shape, _mybir.dt.from_np(v.dtype), kind="ExternalInput").ap()
    shape = (a["x"].shape[0], T, C)
    args["out"] = nc.dram_tensor("out_0", shape, _mybir.dt.float32, kind="ExternalOutput").ap()
    tower(nc, **args)
    return _run(nc, [arrays], core_ids=[0]).results[0]["out_0"]
```
